# Optimizing a Trainium2 kernel written in Bass

```python
import numpy as np
import jax
import jax.numpy as jnp

def _softmax(x, axis=-1):
    return jax.nn.softmax(x, axis=axis)

def _gelu(x):
    return jax.nn.gelu(x, approximate=True)

def _silu(x):
    return jax.nn.silu(x)

def _sigmoid(x):
    return jax.nn.sigmoid(x)

def _layernorm(x, axis=-1, eps=1e-05):
    m = jnp.mean(x, axis=axis, keepdims=True)
    v = jnp.var(x, axis=axis, keepdims=True)
    return (x - m) / jnp.sqrt(v + eps)

def _scatter_add(tgt, idx, src, axis=0):
    return tgt.at[idx].add(src)

def _segment_sum(src, seg, n):
    return jax.ops.segment_sum(src, seg, n)
kernel_name = 'mk_gnn_resnorm_d4_gnn_r64_fb22fd'

def setup_inputs(seed: int=0):
    np.random.seed(seed)
    _w = jnp.asarray

    def _rec_inputs():
        import jax
        import jax.numpy as jnp
        _gk = jax.random.key(seed)
        x = -0.0005121 + 1.001 * jax.random.normal(jax.random.fold_in(_gk, 1), (100000, 64), jnp.float32)
        src = jax.random.randint(jax.random.fold_in(_gk, 2), (25000,), 0, 100000, jnp.int32)
        dst = jax.random.randint(jax.random.fold_in(_gk, 3), (25000,), 0, 100000, jnp.int32)
        _o = jnp.argsort(dst, stable=True)
        src = src[_o]
        dst = dst[_o]
        edge_weight = jax.random.uniform(jax.random.fold_in(_gk, 13), (25000,), jnp.float32, 0.0, 0.999999)
        return (x, src, dst, edge_weight)
    x, src, dst, edge_weight = _rec_inputs()

    def _L0_gnn_setup():
        import jax, jax.numpy as jnp
        import numpy as np
        N_NODES = 50000
        N_EDGES = 12500
        IN_CH = 64
        OUT_CH = 64
        NHEAD = 8

        def _edge_softmax(e, dst, num_nodes):
            mx = jax.ops.segment_max(e, dst, num_segments=num_nodes)
            mx = jax.lax.stop_gradient(mx)
            ex = jnp.exp(e - mx[dst])
            s = jax.ops.segment_sum(ex, dst, num_segments=num_nodes)
            return ex / s[dst]
        key = jax.random.key(seed)
        ks = jax.random.split(key, 10)
        ndata = jax.random.normal(ks[0], (N_NODES, IN_CH), dtype=jnp.float32)
        src = jax.random.randint(ks[1], (N_EDGES,), 0, N_NODES)
        dst = jax.random.randint(ks[2], (N_EDGES,), 0, N_NODES)
        sc = 1.0 / np.sqrt(IN_CH)
        W1 = jax.random.normal(ks[3], (IN_CH, OUT_CH), dtype=jnp.float32) * sc
        b1 = jnp.zeros((OUT_CH,), dtype=jnp.float32)
        W2 = jax.random.normal(ks[4], (IN_CH, OUT_CH), dtype=jnp.float32) * sc
        b2 = jnp.zeros((OUT_CH,), dtype=jnp.float32)
        Wres = jax.random.normal(ks[5], (IN_CH, OUT_CH), dtype=jnp.float32) * sc
        bres = jnp.zeros((OUT_CH,), dtype=jnp.float32)
        m = jnp.ones((3, NHEAD, OUT_CH // NHEAD), dtype=jnp.float32)
        return {'ndata': ndata, 'src': src, 'dst': dst, 'W1': W1, 'b1': b1, 'W2': W2, 'b2': b2, 'Wres': Wres, 'bres': bres, 'm': m}
    _L0_gnn_all = _L0_gnn_setup()
    _L0_gnn_in = {k: v for k, v in _L0_gnn_all.items() if k in ('W1', 'b1', 'W2', 'b2', 'Wres', 'bres', 'm')}
    del _L0_gnn_all

    def _L1_gnn_setup():
        import jax, jax.numpy as jnp
        import numpy as np
        N_NODES = 100000
        N_EDGES = 25000
        F_IN = 64
        F_OUT = 64
        K = 6
        key = jax.random.key(seed)
        k1, k2, k3, k4 = jax.random.split(key, 4)
        x = jax.random.normal(k1, (N_NODES, F_IN), dtype=jnp.float32)
        edge_index = jax.random.randint(k2, (2, N_EDGES), 0, N_NODES, dtype=jnp.int64)
        edge_weight = jax.random.uniform(k3, (N_EDGES,), dtype=jnp.float32)
        W = jax.random.normal(k4, (K, F_IN, F_OUT), dtype=jnp.float32) * (1.0 / np.sqrt(F_IN))
        b = jnp.zeros((F_OUT,), dtype=jnp.float32)
        return {'x': x, 'edge_index': edge_index, 'edge_weight': edge_weight, 'W': W, 'b': b}
    _L1_gnn_all = _L1_gnn_setup()
    _L1_gnn_in = {k: v for k, v in _L1_gnn_all.items() if k in ('W', 'b')}
    del _L1_gnn_all

    def _L2_gnn_setup():
        import jax, jax.numpy as jnp
        import numpy as np
        N_NODES = 100000
        N_EDGES = 18750
        D_FEAT = 64
        key = jax.random.key(seed)
        k1, k2, k3 = jax.random.split(key, 3)
        h = jax.random.normal(k1, (N_NODES, D_FEAT), dtype=jnp.float32)
        edge_src = jax.random.randint(k2, (N_EDGES,), 0, N_NODES, dtype=jnp.int32)
        edge_dst = jax.random.randint(k3, (N_EDGES,), 0, N_NODES, dtype=jnp.int32)
        return {'h': h, 'edge_src': edge_src, 'edge_dst': edge_dst}
    _L2_gnn_all = _L2_gnn_setup()
    _L2_gnn_in = {k: v for k, v in _L2_gnn_all.items() if k in ()}
    del _L2_gnn_all

    def _L3_gnn_setup():
        import jax, jax.numpy as jnp
        import numpy as np
        N_NODES = 50000
        N_EDGES = 12500
        D_IN = 64
        D_HID = 128
        D_OUT = 64
        key = jax.random.key(seed)
        k0, k1, k2, k3 = jax.random.split(key, 4)
        x = jax.random.normal(k0, (N_NODES, D_IN), dtype=jnp.float32)
        edge_index = jax.random.randint(k1, (2, N_EDGES), 0, N_NODES, dtype=jnp.int32)
        W1 = jax.random.normal(k2, (2 * D_IN, D_HID), dtype=jnp.float32) * 0.05
        b1 = jnp.zeros((D_HID,), dtype=jnp.float32)
        W2 = jax.random.normal(k3, (D_HID, D_OUT), dtype=jnp.float32) * 0.05
        b2 = jnp.zeros((D_OUT,), dtype=jnp.float32)
        return {'x': x, 'edge_index': edge_index, 'W1': W1, 'b1': b1, 'W2': W2, 'b2': b2}
    _L3_gnn_all = _L3_gnn_setup()
    _L3_gnn_in = {k: v for k, v in _L3_gnn_all.items() if k in ('W1', 'b1', 'W2', 'b2')}
    del _L3_gnn_all
    return {'x': x, 'src': src, 'dst': dst, 'edge_weight': edge_weight, 'L0_gnn_W1': _L0_gnn_in['W1'], 'L0_gnn_b1': _L0_gnn_in['b1'], 'L0_gnn_W2': _L0_gnn_in['W2'], 'L0_gnn_b2': _L0_gnn_in['b2'], 'L0_gnn_Wres': _L0_gnn_in['Wres'], 'L0_gnn_bres': _L0_gnn_in['bres'], 'L0_gnn_m': _L0_gnn_in['m'], 'L1_gnn_W': _L1_gnn_in['W'], 'L1_gnn_b': _L1_gnn_in['b'], 'L3_gnn_W1': _L3_gnn_in['W1'], 'L3_gnn_b1': _L3_gnn_in['b1'], 'L3_gnn_W2': _L3_gnn_in['W2'], 'L3_gnn_b2': _L3_gnn_in['b2']}

def reference(x, src, dst, edge_weight, L0_gnn_W1, L0_gnn_b1, L0_gnn_W2, L0_gnn_b2, L0_gnn_Wres, L0_gnn_bres, L0_gnn_m, L1_gnn_W, L1_gnn_b, L3_gnn_W1, L3_gnn_b1, L3_gnn_W2, L3_gnn_b2):
    import jax
    import jax.numpy as jnp

    def _L0_gnn_ref(ndata, src, dst, W1, b1, W2, b2, Wres, bres, m):
        import jax, jax.numpy as jnp
        import numpy as np
        N_NODES = 50000
        N_EDGES = 12500
        IN_CH = 64
        OUT_CH = 64
        NHEAD = 8

        def _edge_softmax(e, dst, num_nodes):
            mx = jax.ops.segment_max(e, dst, num_segments=num_nodes)
            mx = jax.lax.stop_gradient(mx)
            ex = jnp.exp(e - mx[dst])
            s = jax.ops.segment_sum(ex, dst, num_segments=num_nodes)
            return ex / s[dst]
        N = ndata.shape[0]
        H = NHEAD
        loop = jnp.arange(N, dtype=src.dtype)
        s = jnp.concatenate([src, loop])
        d = jnp.concatenate([dst, loop])
        mn = jnp.min(ndata, axis=-1, keepdims=True)
        mx = jnp.max(ndata, axis=-1, keepdims=True)
        x = (ndata - mn) / (mx - mn + 1e-05)
        l = (x @ W1 + b1).reshape(N, H, -1)
        r = (x @ W2 + b2).reshape(N, H, -1)
        le = jax.nn.sigmoid(l[s] + l[d])
        re = jax.nn.sigmoid(r[s] + r[d])
        le = _edge_softmax(le, d, N)
        re = _edge_softmax(re, d, N)
        ft_r = jax.ops.segment_sum(r[s] * le, d, num_segments=N)
        ft_l = jax.ops.segment_sum(ft_r[s] * re, d, num_segments=N)
        h = (m[0] * ft_l).reshape(N, -1) + (x @ Wres + bres)
        return h

    def _L1_gnn_ref(x, edge_index, edge_weight, W, b):
        import jax, jax.numpy as jnp
        import numpy as np
        N_NODES = 100000
        N_EDGES = 25000
        F_IN = 64
        F_OUT = 64
        K = 6
        n = x.shape[0]
        row, col = (edge_index[0], edge_index[1])
        deg = jax.ops.segment_sum(edge_weight, row, num_segments=n)
        dis = jnp.where(deg > 0, jax.lax.rsqrt(jnp.maximum(deg, 1e-30)), 0.0)
        norm = -dis[row] * edge_weight * dis[col]

        def prop(t):
            return jax.ops.segment_sum(norm[:, None] * t[col], row, num_segments=n)
        Kc = W.shape[0]
        Tx0 = x
        out = Tx0 @ W[0]
        Tx1 = prop(Tx0)
        out = out + Tx1 @ W[1]
        for k in range(2, Kc):
            Tx2 = 2.0 * prop(Tx1) - Tx0
            out = out + Tx2 @ W[k]
            Tx0, Tx1 = (Tx1, Tx2)
        return jax.nn.relu(out + b)

    def _L2_gnn_ref(h, edge_src, edge_dst):
        import jax, jax.numpy as jnp
        import numpy as np
        N_NODES = 100000
        N_EDGES = 18750
        D_FEAT = 64
        'LightGCN propagation: h_out[v] = sum_{(u,v) in E} h[u] / sqrt(deg_out(u)*deg_in(v)).'
        n = h.shape[0]
        ones = jnp.ones(edge_src.shape[0], dtype=h.dtype)
        deg_out = jnp.maximum(jax.ops.segment_sum(ones, edge_src, num_segments=n), 1.0)
        deg_in = jnp.maximum(jax.ops.segment_sum(ones, edge_dst, num_segments=n), 1.0)
        inv_sqrt_out = jax.lax.rsqrt(deg_out)
        inv_sqrt_in = jax.lax.rsqrt(deg_in)
        w = inv_sqrt_out[edge_src] * inv_sqrt_in[edge_dst]
        m = h[edge_src] * w[:, None]
        h_out = jax.ops.segment_sum(m, edge_dst, num_segments=n)
        return h_out

    def _L3_gnn_ref(x, edge_index, W1, b1, W2, b2):
        import jax, jax.numpy as jnp
        import numpy as np
        N_NODES = 50000
        N_EDGES = 12500
        D_IN = 64
        D_HID = 128
        D_OUT = 64
        row, col = (edge_index[0], edge_index[1])
        x_row = x[row]
        x_col = x[col]
        h = jnp.concatenate([x_row, x_col - x_row], axis=1)
        h = jax.nn.relu(h @ W1 + b1)
        h = h @ W2 + b2
        out = jax.ops.segment_max(h, row, num_segments=x.shape[0])
        out = jnp.where(jnp.isfinite(out), out, jnp.zeros_like(out))
        return out
    edge_index = jnp.stack([src, dst])
    x = _layernorm(x + _L0_gnn_ref(x, src, dst, L0_gnn_W1, L0_gnn_b1, L0_gnn_W2, L0_gnn_b2, L0_gnn_Wres, L0_gnn_bres, L0_gnn_m), axis=-1)
    x = _layernorm(x + _L1_gnn_ref(x, edge_index, edge_weight, L1_gnn_W, L1_gnn_b), axis=-1)
    x = _layernorm(x + _L2_gnn_ref(x, src, dst), axis=-1)
    x = _layernorm(x + _L3_gnn_ref(x, edge_index, L3_gnn_W1, L3_gnn_b1, L3_gnn_W2, L3_gnn_b2), axis=-1)
    return x

_drawn_inputs = setup_inputs


def setup_inputs(seed=0):
    import zlib

    import numpy as np

    out = dict(_drawn_inputs(seed))
    spreads = {'L0_gnn_b1': (0.0, 0.8),
     'L0_gnn_b2': (0.0, 0.1),
     'L0_gnn_bres': (0.0, 0.1),
     'L0_gnn_m': (1.0, 0.2),
     'L1_gnn_b': (0.0, 0.1),
     'L3_gnn_b1': (0.0, 0.393),
     'L3_gnn_b2': (0.0, 0.1)}
    factors = {'L0_gnn_W1': 8.0}
    for name, (base, spread) in spreads.items():
        noise = np.random.default_rng([zlib.crc32(name.encode()), seed]).standard_normal(out[name].shape)
        drawn = base * np.exp(spread * noise) if base else spread * noise
        out[name] = jnp.asarray(drawn.astype(out[name].dtype))
    for name, factor in factors.items():
        out[name] = (out[name] * factor).astype(out[name].dtype)
    return out
```

```python
import concourse.bass as bass
from concourse import mybir
from contextlib import ExitStack

FP32 = mybir.dt.float32
I32 = mybir.dt.int32
U32 = mybir.dt.uint32
F16 = mybir.dt.float16
BF16 = mybir.dt.bfloat16
ALU = mybir.AluOpType
ACT = mybir.ActivationFunctionType
AX = mybir.AxisListType

P = 128
D = 64
N = 100000
E = 25000
NT = -(-E // P)
SLOTS = NT * P
CT = 7
NCH = NT // CT
NONE = N
LO = 784
BLK = 4
NBLK = NT // BLK
META = 8


class Link:

    def __init__(self, eng, sem):
        self.eng, self.sem, self.base, self.k = eng, sem, 0, 0

    def __call__(self, ins):
        self.k += 1
        ins.then_inc(self.sem, 1)
        self.eng.wait_ge(self.sem, self.base + self.k)
        return ins


def turns(eng, count, body, links=()):
    starts = [ln.base + ln.k for ln in links]
    body(0)
    per = [ln.base + ln.k - s for ln, s in zip(links, starts)]
    if count > 1:
        with eng.Fori(1, count) as i:
            for ln, s, n in zip(links, starts, per):
                ln.base, ln.k = i * n + s, 0
            body(i)
    for ln, s, n in zip(links, starts, per):
        ln.base, ln.k = s + n * count, 0


def wait(eng, sem, value):
    if isinstance(value, int) and value <= 0:
        return
    eng.wait_ge(sem, value)


def pass_gate(nc, pool, gate, gates, value):
    pool.wait_ge(gates, value)
    nc.gpsimd.tensor_tensor(gate[:, 0:1], gate[:, 1:2], gate[:, 1:2], ALU.add).then_inc(gates, 1)


class Scope(ExitStack):
    def __init__(self, nc, tag=""):
        super().__init__()
        self.nc, self.tag, self.sems = nc, tag, []
        self.callback(self.clear)

    def sb(self, name, shape, dt=FP32):
        return self.enter_context(self.nc.sbuf_tensor(self.tag + name, shape, dt))

    def ps(self, name, shape, dt=FP32):
        return self.enter_context(self.nc.psum_tensor(self.tag + name, shape, dt))

    def sem(self, name):
        self.sems.append(self.nc.alloc_semaphore(self.tag + name))
        return self.sems[-1]

    def clear(self):
        if self.sems:
            self.nc.clear_and_free_semaphores(self.sems)
            self.nc.all_engine_barrier()

    def block(self):
        return self.enter_context(self.nc.Block())


def constants(nc, c):
    with Scope(nc, "const_") as s:
        io = s.sb("iota_i", [P, LO], I32)
        pi = s.sb("part_i", [P, 1], I32)
        made = s.sem("made")
        piped = s.sem("linked")
        block = s.block()

        @block.gpsimd
        def _(pool):
            link = Link(pool, piped)
            link(pool.iota(io[:, :], pattern=[[1, LO]], base=0, channel_multiplier=0))
            link(pool.iota(pi[:, :], pattern=[[0, 1]], base=0, channel_multiplier=1))
            for t in (c.ident, c.ones, c.tri, c.rank_mask):
                link(pool.memset(t[:, :], 1.0))
            link(pool.affine_select(out=c.ident[:, :], in_=c.ident[:, :], compare_op=ALU.is_equal, fill=0.0,
                                    base=0, pattern=[[-1, P]], channel_multiplier=1))
            link(pool.affine_select(out=c.tri[:, :], in_=c.tri[:, :], compare_op=ALU.is_gt, fill=0.0,
                                    base=0, pattern=[[1, P]], channel_multiplier=-1))
            own = c.rank_mask[:, (BLK - 1) * P:BLK * P]
            link(pool.affine_select(out=own, in_=own, compare_op=ALU.is_gt, fill=0.0,
                                    base=0, pattern=[[-1, P]], channel_multiplier=1))
            pool.nop().then_inc(made, 1)

        @block.vector
        def _(dve):
            dve.wait_ge(made, 1)
            link = Link(dve, s.sem("dve_linked"))
            link(nc.vector.tensor_copy(c.iota16[:, :], io[:, :]))
            link(nc.vector.tensor_copy(c.iota_part[:, :], pi[:, :]))
            link(nc.vector.tensor_copy(c.ident16[:, :], c.ident[:, :]))
            link(nc.vector.memset(c.ones16[:, :], 1.0))
            link(nc.vector.memset(c.w128_16[:, :], 128.0))


def load_edges(nc, c, src, dst, ew):
    full = E // NT
    rest = E - full * NT
    with Scope(nc, "edges_") as s:
        arrived = s.sem("arrived")
        cleared = s.sem("cleared")
        linked = s.sem("linked")
        hi_i = s.sb("hi_i", [P, NT], I32)
        lo_i = s.sb("lo_i", [P, NT], I32)
        block = s.block()

        @block.sync
        def _(sp):
            sp.wait_ge(cleared, 3)
            for a, t in ((src, c.src), (dst, c.dst), (ew, c.ew)):
                sp.dma_start(t[0:full, :], a[0:full * NT].rearrange("(p t) -> p t", t=NT)).then_inc(arrived, 16)
                sp.dma_start(t[full:full + 1, 0:rest], a[full * NT:E].rearrange("(a t) -> a t", a=1)).then_inc(arrived, 16)

        @block.vector
        def _(dve):
            link = Link(dve, linked)
            nc.vector.memset(c.src[:, :], NONE).then_inc(cleared, 1)
            nc.vector.memset(c.dst[:, :], NONE).then_inc(cleared, 1)
            nc.vector.memset(c.ew[:, :], 0.0).then_inc(cleared, 1)
            dve.wait_ge(cleared, 3)
            dve.wait_ge(arrived, 96)
            for v, key, u, g in ((c.src, c.key_s, c.node_s, c.safe_s), (c.dst, c.key_d, c.node_d, c.safe_d)):
                link(nc.vector.tensor_single_scalar(hi_i[:, :], v[:, :], 127, ALU.bitwise_and))
                link(nc.vector.tensor_single_scalar(lo_i[:, :], v[:, :], 7, ALU.logical_shift_right))
                link(nc.vector.tensor_copy(key[:, :, 0], hi_i[:, :]))
                link(nc.vector.tensor_copy(key[:, :, 1], lo_i[:, :]))
                link(nc.vector.tensor_copy(key[:, :, 2], v[:, :]))
                link(nc.vector.scalar_tensor_tensor(out=u[:, :], in0=key[:, :, 0], scalar=float(LO), in1=key[:, :, 1],
                                                    op0=ALU.mult, op1=ALU.add))
                link(nc.vector.tensor_scalar(g[:, :], key[:, :, 2], float(N - 1), None, ALU.min))


def rank_edges(nc, c, key, rank, count, tag):
    H = 512
    with Scope(nc, tag) as s:
        kc = s.sb("keys", [P, BLK, 3])
        oh_hi = s.sb("onehot_hi", [P, BLK, P], BF16)
        oh_lo = s.sb("onehot_lo", [P, BLK, LO], BF16)
        oh_hiT = s.sb("onehot_hiT", [P, BLK * P], BF16)
        diag_hi = s.sb("diag_hi", [P, BLK, P], F16)
        diag_lo = s.sb("diag_lo", [P, BLK, P], F16)
        tab_h = s.sb("count_high", [P, LO], BF16)
        tab_l = s.sb("count_low", [P, LO], BF16)
        near = s.sb("near", [P, BLK])
        far = s.sb("far", [P, BLK])
        junk = s.sb("junk", [P, LO])
        run = s.ps("running", [P, 1024])
        got = [s.ps(f"got{k}", [P, 1024]) for k in range(2)]
        row_hi = s.ps("row_hi", [P, 512])
        row_v = s.ps("row_v", [P, 512])
        keys_in = s.sem("keys_in")
        diags = s.sem("diags")
        rows = s.sem("rows")
        rows_used = s.sem("rows_used")
        hots = s.sem("hots")
        queried = s.sem("queried")
        extracted = s.sem("extracted")
        counted = s.sem("counted")
        high = s.sem("high")
        low = s.sem("low")
        dve_l = s.sem("dve_linked")
        cleared = s.sem("cleared")
        block = s.block()

        @block.scalar
        def _(act):
            def body(i):
                act.wait_ge(keys_in, i + 1)
                wait(act, rows, i)
                for k in range(BLK):
                    nc.scalar.activation(diag_hi[:, k, :], c.ident16[:, :], ACT.Copy, scale=kc[:, k, 0:1])
                    last = nc.scalar.activation(diag_lo[:, k, :], c.ident16[:, :], ACT.Copy, scale=kc[:, k, 1:2])
                last.then_inc(diags, 1)
                act.wait_ge(counted, i + 1)
                nc.scalar.activation(tab_h[:, :], run[:, 0:LO], ACT.Copy).then_inc(high, 1)
            turns(act, NBLK, body)

        @block.tensor
        def _(pe):
            pe.wait_ge(cleared, 1)
            nc.tensor.matmul(run[:, 0:H], tab_h[:, 0:P], tab_h[:, 0:H], start=True, stop=False, skip_group_check=True)
            nc.tensor.matmul(run[:, H:LO], tab_h[:, 0:P], tab_h[:, H:LO], start=True, stop=False, skip_group_check=True)

            def body(i):
                pe.wait_ge(diags, i + 1)
                wait(pe, rows_used, i)
                nc.tensor.matmul(row_hi[:, :], c.ones16[:, :], diag_hi[:, :, :].rearrange("p a b -> p (a b)"), start=True, stop=True)
                nc.tensor.matmul(row_v[:, :], c.ones16[:, :], diag_hi[:, :, :].rearrange("p a b -> p (a b)"), start=True, stop=False)
                nc.tensor.matmul(row_v[:, :], c.w128_16[:, :], diag_lo[:, :, :].rearrange("p a b -> p (a b)"), start=False, stop=True).then_inc(rows, 1)
                pe.wait_ge(hots, i + 1)
                wait(pe, low, i)
                for k in range(BLK):
                    n = i * BLK + k
                    wait(pe, extracted, n - 1)
                    hot = oh_hiT[:, k * P:(k + 1) * P]
                    for a, b in ((0, H), (H, LO)):
                        nc.tensor.matmul(got[k % 2][:, a:b], hot, tab_h[:, a:b], start=True, stop=False)
                        last = nc.tensor.matmul(got[k % 2][:, a:b], hot, tab_l[:, a:b], start=False, stop=True)
                    last.then_inc(queried, 1)
                for k in range(BLK):
                    for a, b in ((0, H), (H, LO)):
                        last = nc.tensor.matmul(run[:, a:b], oh_hi[:, k, :], oh_lo[:, k, a:b], start=False, stop=False,
                                                skip_group_check=True)
                last.then_inc(counted, 1)
            turns(pe, NBLK, body)

        @block.vector
        def _(dve):
            link = Link(dve, dve_l)
            link(nc.vector.memset(tab_l[:, :], 0.0))
            nc.vector.memset(tab_h[:, :], 0.0).then_inc(cleared, 1)

            def body(i):
                wait(dve, diags, i)
                link(nc.vector.tensor_scalar(kc[:, :, :].rearrange("p a b -> p (a b)"),
                                             key[:, :, :].rearrange("p a b -> p (a b)")[:, bass.ds(i * (3 * BLK), 3 * BLK)],
                                             1.0, None, ALU.mult))
                nc.vector.tensor_scalar(near[:, :], kc[:, :, 0], 0.0, None, ALU.mult).then_inc(keys_in, 1)
                dve.wait_ge(keys_in, i + 1)
                wait(dve, counted, i)
                link(nc.vector.tensor_tensor(oh_hi[:, :, :], c.iota16[:, 0:P].unsqueeze(1).to_broadcast([P, BLK, P]),
                                             kc[:, :, 0:1].to_broadcast([P, BLK, P]), ALU.is_equal))
                for k in range(BLK):
                    link(nc.vector.tensor_scalar(oh_lo[:, k, :], c.iota16[:, :], kc[:, k, 1:2], None, ALU.is_equal))
                dve.wait_ge(rows, i + 1)
                link(nc.vector.tensor_scalar(oh_hiT[:, :], row_hi[:, :], c.iota_part[:, :], None, ALU.is_equal))
                for k in range(BLK):
                    n = (k + 1) * P
                    last = link(nc.vector.scalar_tensor_tensor(out=junk[:, 0:n], in0=row_v[:, 0:n], scalar=kc[:, k, 2:3],
                                                        in1=c.rank_mask[:, BLK * P - n:BLK * P], op0=ALU.is_equal,
                                                        op1=ALU.mult, accum_out=near[:, k:k + 1]))
                nc.vector.tensor_scalar(junk[:, 0:1], near[:, 0:1], 0.0, None, ALU.mult).then_inc(rows_used, 1)
                dve.wait_ge(rows_used, i + 1)
                nc.vector.tensor_scalar(junk[:, 0:1], near[:, 0:1], 0.0, None, ALU.mult).then_inc(hots, 1)
                dve.wait_ge(hots, i + 1)
                for k in range(BLK):
                    n = i * BLK + k
                    dve.wait_ge(queried, n + 1)
                    nc.vector.tensor_tensor_reduce(out=junk[:, :], in0=got[k % 2][:, 0:LO], in1=oh_lo[:, k, :], scale=1.0,
                                                   scalar=0.0, op0=ALU.mult, op1=ALU.add,
                                                   accum_out=far[:, k:k + 1]).then_inc(extracted, 1)
                    dve.wait_ge(extracted, n + 1)
                link(nc.vector.tensor_tensor(rank[:, bass.ds(i * BLK, BLK)], near[:, :], far[:, :], ALU.add))
                dve.wait_ge(high, i + 1)
                nc.vector.tensor_tensor(tab_l[:, :], run[:, 0:LO], tab_h[:, :], ALU.subtract).then_inc(low, 1)
                dve.wait_ge(low, i + 1)
            turns(dve, NBLK, body, [link])
            link(nc.vector.tensor_copy(count[:, :], run[:, 0:LO]))


def node_table(nc, c, table):
    with Scope(nc, "nodes_") as s:
        ones = s.sb("ones", [P, LO])
        incl = s.sb("inclusive", [P, LO])
        has = s.sb("has", [P, LO])
        out = s.sb("entries", [P, LO, 4])
        base = [s.ps(f"base{k}", [P, 1]) for k in range(2)]
        summed = s.sem("summed")
        based = s.sem("based")
        dve_l = s.sem("dve_linked")
        stored = s.sem("stored")
        filled = s.sem("filled")
        block = s.block()

        @block.tensor
        def _(pe):
            for k in range(2):
                pe.wait_ge(summed, k + 1)
                nc.tensor.matmul(base[k][:, :], c.tri[:, :], incl[:, LO - 1:LO], start=True, stop=True).then_inc(based, 1)

        @block.vector
        def _(dve):
            link = Link(dve, dve_l)
            link(nc.vector.memset(ones[:, :], 1.0))
            for k, cnt in enumerate((c.count_s, c.count_d)):
                nc.vector.tensor_tensor_scan(out=incl[:, :], data0=ones[:, :], data1=cnt[:, :], initial=0.0,
                                             op0=ALU.mult, op1=ALU.add).then_inc(summed, 1)
                dve.wait_ge(summed, k + 1)
                dve.wait_ge(based, k + 1)
                link(nc.vector.tensor_scalar(incl[:, :], incl[:, :], base[k][:, :], None, ALU.add))
                link(nc.vector.tensor_tensor(out[:, :, 2 * k], incl[:, :], cnt[:, :], ALU.subtract))
                link(nc.vector.tensor_scalar(has[:, :], cnt[:, :], 0.0, None, ALU.is_gt))
                link(nc.vector.tensor_tensor(out[:, :, 2 * k + 1], incl[:, :], has[:, :], ALU.mult))
            nc.vector.tensor_copy(has[:, 0:1], incl[:, 0:1]).then_inc(filled, 1)

        @block.sync
        def _(sp):
            sp.wait_ge(filled, 1)
            sp.dma_start(table.rearrange("(p a) k -> p a k", p=P), out[:, :, :]).then_inc(stored, 16)
            sp.wait_ge(stored, 16)


def gather_small(nc, c, jobs, words, tag):
    with Scope(nc, tag) as s:
        stage = [s.sb(f"stage{b}", [P, CT], I32) for b in range(2)]
        rows = [s.sb(f"rows{b}", [P, CT, words]) for b in range(2)]
        gate = s.sb("gate", [P, 2], I32)
        staged = [s.sem(f"staged{b}") for b in range(2)]
        gathered = [s.sem(f"gathered{b}") for b in range(2)]
        taken = [s.sem(f"taken{b}") for b in range(2)]
        gates = s.sem("gates")
        turns_n = NCH // 2
        block = s.block()
        for_j = list(enumerate(jobs))

        @block.sync
        def _(sp):
            for j, (table, index, out) in for_j:
                def body(i):
                    for b in range(2):
                        n = i + j * turns_n
                        wait(sp, gathered[b], n * (16 * CT))
                        sp.dma_start(stage[b][:, :], index[:, bass.ds((i * 2 + b) * CT, CT)]).then_inc(staged[b], 16)
                turns(sp, turns_n, body)

        @block.gpsimd
        def _(pool):
            nc.gpsimd.memset(gate[:, :], 0).then_inc(gates, 1)
            for j, (table, index, out) in for_j:
                def body(i):
                    for b in range(2):
                        n = i + j * turns_n
                        pool.wait_ge(staged[b], (n + 1) * 16)
                        wait(pool, taken[b], n)
                        pass_gate(nc, pool, gate, gates, n * 2 + b + 1)
                        for k in range(CT):
                            nc.gpsimd.indirect_dma_start(
                                out=rows[b][:, k, :], out_offset=None, in_=table[:, :],
                                in_offset=bass.IndirectOffsetOnAxis(ap=stage[b][:, k:k + 1].bitcast(U32), axis=0),
                            ).then_inc(gathered[b], 16)
                turns(pool, turns_n, body)

        @block.vector
        def _(dve):
            for j, (table, index, out) in for_j:
                def body(i):
                    for b in range(2):
                        n = i + j * turns_n
                        dve.wait_ge(gathered[b], (n + 1) * (16 * CT))
                        w = CT * words
                        flat = out.rearrange("p t k -> p (t k)")
                        nc.vector.tensor_scalar(flat[:, bass.ds((i * 2 + b) * w, w)],
                                                rows[b][:, :, :].rearrange("p t k -> p (t k)"), 1.0, None,
                                                ALU.mult).then_inc(taken[b], 1)
                turns(dve, turns_n, body)


CW = CT * P
ZERO = SLOTS
PAIRS = NCH // 2
EPS = 1e-5


def bc(ap, n):
    return ap.unsqueeze(2).to_broadcast([ap.shape[0], ap.shape[1], n])


def slot_rows(nc, link, row, slot, tmp_i, tmp_p, tmp_t):
    link(nc.vector.tensor_copy(tmp_i[:, :], slot))
    link(nc.vector.tensor_single_scalar(tmp_p[:, :], tmp_i[:, :], 127, ALU.bitwise_and))
    link(nc.vector.tensor_single_scalar(tmp_t[:, :], tmp_i[:, :], 7, ALU.logical_shift_right))
    link(nc.vector.scalar_tensor_tensor(out=row, in0=tmp_p[:, :], scalar=float(NT), in1=tmp_t[:, :],
                                        op0=ALU.mult, op1=ALU.add))


def edge_records(nc, c):
    with Scope(nc, "rec_") as s:
        ti, tp, tt = (s.sb(n, [P, NT], I32) for n in ("ti", "tp", "tt"))
        pa, pb, ea_s, eb_s, ea_d, eb_d, ta, tb, own = (s.sb(n, [P, NT]) for n in
                                                      ("pa", "pb", "ea_s", "eb_s", "ea_d", "eb_d", "ta", "tb", "own"))
        linked = s.sem("linked")
        block = s.block()

        @block.vector
        def _(dve):
            link = Link(dve, linked)
            v = nc.vector

            def tt_(o, a, b, op):
                link(v.tensor_tensor(o, a, b, op))

            def ts_(o, a, x, op):
                link(v.tensor_scalar(o, a, x, None, op))

            for out, seg, col, rank in ((pa, c.seg_s, 0, c.rank_s), (pb, c.seg_d, 2, c.rank_d)):
                tt_(ta[:, :], seg[:, :, col], rank[:, :], ALU.add)
                slot_rows(nc, link, out[:, :], ta[:, :], ti, tp, tt)
            for out, seg, col in ((ea_s, c.seg_s, 1), (eb_s, c.seg_s, 3), (ea_d, c.seg_d, 1), (eb_d, c.seg_d, 3)):
                link(v.tensor_scalar(ta[:, :], seg[:, :, col], -1.0, 0.0, ALU.add, ALU.max))
                slot_rows(nc, link, out[:, :], ta[:, :], ti, tp, tt)
            link(v.tensor_copy(c.row_a[:, :], pa[:, :]))
            link(v.tensor_copy(c.row_b[:, :], pb[:, :]))

            def choose(out, has, x, y, y_add):
                ts_(ta[:, :], has, 0.0, ALU.is_gt)
                if y is None:
                    link(v.tensor_scalar(tb[:, :], x, -float(y_add), None, ALU.add))
                    tt_(tb[:, :], tb[:, :], ta[:, :], ALU.mult)
                    ts_(out, tb[:, :], float(y_add), ALU.add)
                else:
                    link(v.scalar_tensor_tensor(out=tb[:, :], in0=x, scalar=-float(y_add), in1=y,
                                                op0=ALU.add, op1=ALU.subtract))
                    tt_(tb[:, :], tb[:, :], ta[:, :], ALU.mult)
                    link(v.scalar_tensor_tensor(out=out, in0=tb[:, :], scalar=float(y_add), in1=y,
                                                op0=ALU.add, op1=ALU.add))

            b, a = c.rec_b, c.rec_a
            bf, af = b[:, :, :].bitcast(FP32), a[:, :, :].bitcast(FP32)
            link(v.tensor_copy(bf[:, :, 0], c.dst[:, :]))
            choose(b[:, :, 1], c.seg_s[:, :, 3], eb_s[:, :], None, ZERO)
            link(v.tensor_copy(b[:, :, 2], ea_s[:, :]))
            ts_(pa[:, :], pa[:, :], 2.0 * SLOTS, ALU.add)
            ts_(own[:, :], ea_d[:, :], float(SLOTS), ALU.add)
            choose(b[:, :, 3], c.seg_d[:, :, 1], own[:, :], pa[:, :], 0.0)
            ts_(bf[:, :, 4], c.seg_d[:, :, 1], 0.0, ALU.is_gt)
            tt_(bf[:, :, 5], c.seg_d[:, :, 3], c.seg_d[:, :, 2], ALU.subtract)
            link(v.memset(b[:, :, 6:8], 0))
            link(v.tensor_copy(af[:, :, 0], c.src[:, :]))
            link(v.tensor_copy(af[:, :, 1], c.ew[:, :]))
            link(v.tensor_copy(a[:, :, 2], eb_d[:, :]))
            choose(a[:, :, 3], c.seg_s[:, :, 3], eb_s[:, :], pb[:, :], SLOTS)
            choose(a[:, :, 4], c.seg_d[:, :, 1], ea_d[:, :], None, ZERO)
            link(v.tensor_copy(a[:, :, 5], eb_d[:, :]))
            choose(a[:, :, 6], c.seg_s[:, :, 3], eb_s[:, :], ea_s[:, :], SLOTS)
            tt_(af[:, :, 7], c.seg_s[:, :, 1], c.seg_s[:, :, 0], ALU.subtract)


def sort_edges(nc, c, x, by_dst, by_src):
    NB = 4
    W = 2 * D + META
    with Scope(nc, "sort_") as s:
        st_s, st_d, st_a, st_b = ([s.sb(f"{n}{b}", [P, CT], I32) for b in range(NB)] for n in ("st_s", "st_d", "st_a", "st_b"))
        pay = [s.sb(f"pay{b}", [P, CT, W]) for b in range(NB)]
        rec = [s.sb(f"rec{b}", [P, CT, META]) for b in range(NB)]
        gate = s.sb("gate", [P, 4], I32)
        gates_g, gates_s = s.sem("gates_gather"), s.sem("gates_scatter")
        staged_g, staged_s, gathered, scattered, copied = ([s.sem(f"{n}{b}") for b in range(NB)] for n in
                                                 ("staged_gather", "staged_scatter", "gathered", "scattered", "copied"))
        turns_n = NCH // NB
        block = s.block()

        @block.sync
        def _(sp):
            def body(i):
                for b in range(NB):
                    at = bass.ds((i * NB + b) * CT, CT)
                    wait(sp, gathered[b], i * (32 * CT))
                    sp.dma_start(st_s[b][:, :], c.safe_s[:, at]).then_inc(staged_g[b], 16)
                    sp.dma_start(st_d[b][:, :], c.safe_d[:, at]).then_inc(staged_g[b], 16)
            turns(sp, turns_n, body)

        @block.scalar
        def _(act):
            def body(i):
                for b in range(NB):
                    at = bass.ds((i * NB + b) * CT, CT)
                    wait(act, scattered[b], i * (32 * CT))
                    act.dma_start(st_b[b][:, :], c.row_b[:, at]).then_inc(staged_s[b], 16)
                    act.dma_start(st_a[b][:, :], c.row_a[:, at]).then_inc(staged_s[b], 16)
            turns(act, turns_n, body)

        @block.vector
        def _(dve):
            def body(i):
                for b in range(NB):
                    at = bass.ds((i * NB + b) * CT * META, CT * META)
                    wait(dve, scattered[b], i * (32 * CT))
                    nc.vector.tensor_copy(pay[b][:, :, 2 * D:W].bitcast(I32),
                                          c.rec_b[:, :, :].rearrange("p t k -> p (t k)")[:, at]
                                          .rearrange("p (t k) -> p t k", k=META)).then_inc(copied[b], 1)
                    nc.vector.tensor_copy(rec[b][:, :, :].rearrange("p t k -> p (t k)").bitcast(I32),
                                          c.rec_a[:, :, :].rearrange("p t k -> p (t k)")[:, at]).then_inc(copied[b], 1)
            turns(dve, turns_n, body)

        @block.gpsimd
        def _(pool):
            nc.gpsimd.memset(gate[:, :], 0).then_inc(gates_g, 1)
            pool.wait_ge(gates_g, 1)
            pool.nop().then_inc(gates_s, 1)

            def scatter(b, turn, n):
                pool.wait_ge(copied[b], turn * 2 + 2)
                pool.wait_ge(gathered[b], turn * (32 * CT) + 32 * CT)
                pool.wait_ge(staged_s[b], turn * 32 + 32)
                pool.wait_ge(gates_s, n + 1)
                nc.gpsimd.tensor_tensor(gate[:, 2:3], gate[:, 1:2], gate[:, 1:2], ALU.add).then_inc(gates_s, 1)
                for k in range(CT):
                    for table, stage, src in ((by_dst, st_b, pay), (by_src, st_a, rec)):
                        nc.gpsimd.indirect_dma_start(
                            out=table[:, :], out_offset=bass.IndirectOffsetOnAxis(ap=stage[b][:, k:k + 1].bitcast(U32), axis=0),
                            in_=src[b][:, k, :], in_offset=None).then_inc(scattered[b], 16)

            def body(i):
                for b in range(NB):
                    n = i * NB + b
                    pool.wait_ge(staged_g[b], i * 32 + 32)
                    wait(pool, scattered[b], i * (32 * CT))
                    pool.wait_ge(gates_g, n + 1)
                    nc.gpsimd.tensor_tensor(gate[:, 0:1], gate[:, 1:2], gate[:, 1:2], ALU.add).then_inc(gates_g, 1)
                    for k in range(CT):
                        for stage, at in ((st_s, 0), (st_d, D)):
                            nc.gpsimd.indirect_dma_start(
                                out=pay[b][:, k, at:at + D], out_offset=None, in_=x[:, :],
                                in_offset=bass.IndirectOffsetOnAxis(ap=stage[b][:, k:k + 1].bitcast(U32), axis=0),
                            ).then_inc(gathered[b], 16)
                    if b:
                        scatter(b - 1, i, n - 1)
                    elif not isinstance(i, int):
                        scatter(NB - 1, i - 1, n - 1)
            turns(pool, turns_n, body)
            scatter(NB - 1, turns_n - 1, NCH - 1)
            for b in range(NB):
                pool.wait_ge(scattered[b], turns_n * 32 * CT)


def order_marks(nc, c, sorted_rows, rec, vrow, same_row, far_row, last, tag, val_row=None):
    T0, T1 = P, NT - P
    with Scope(nc, tag) as s:
        v = s.sb("v", [P, NT])
        w = s.sb("w", [P, NT])
        vT = [s.sb("vT0", [T0, P]), s.sb("vT1", [T1, P])]
        wT = [s.sb("wT0", [T0, P]), s.sb("wT1", [T1, P])]
        pv = [s.sb("pv0", [T0, P]), s.sb("pv1", [T1, P])]
        nx = [s.sb("nx0", [T0, P]), s.sb("nx1", [T1, P])]
        fl = [s.sb("fl0", [T0, P]), s.sb("fl1", [T1, P])]
        ng = [s.sb("ng0", [T0, P]), s.sb("ng1", [T1, P])]
        edge = s.sb("edge", [1, 2])
        tp = [s.ps("tp0", [T0, P]), s.ps("tp1", [T1, P])]
        wp = [s.ps("wp0", [T0, P]), s.ps("wp1", [T1, P])]
        bp = s.ps("bp", [P, NT])
        loaded, ready, turned, evac, stored, reread, marked, back, linked, kept = (
            s.sem(n) for n in ("loaded", "ready", "turned", "evac", "stored", "reread", "marked", "back", "linked", "kept"))
        cut = ((0, T0), (T0, NT))
        block = s.block()

        @block.sync
        def _(sp):
            sp.dma_start(rec[:, :, :], sorted_rows.rearrange("(p t) k -> p t k", p=P)[:, :, -META:].bitcast(I32)).then_inc(loaded, 16)
            sp.wait_ge(evac, 1)
            sp.dma_start(vrow[0:1].rearrange("(a n) -> a n", a=1), edge[0:1, 0:1]).then_inc(stored, 16)
            sp.dma_start(vrow[SLOTS + 1:SLOTS + 2].rearrange("(a n) -> a n", a=1), edge[0:1, 1:2]).then_inc(stored, 16)
            for k, (a, b) in enumerate(cut):
                sp.dma_start(vrow[1 + a * P:1 + b * P].rearrange("(t p) -> t p", p=P), vT[k][:, :]).then_inc(stored, 16)
                sp.dma_start(val_row[a * P:b * P].rearrange("(t p) -> t p", p=P), wT[k][:, :]).then_inc(stored, 16)
            sp.wait_ge(stored, 96)
            for k, (a, b) in enumerate(cut):
                sp.dma_start(pv[k][:, :], vrow[a * P:b * P].rearrange("(t p) -> t p", p=P)).then_inc(reread, 16)
                sp.dma_start(nx[k][:, :], vrow[2 + a * P:2 + b * P].rearrange("(t p) -> t p", p=P)).then_inc(reread, 16)
            sp.wait_ge(marked, 1)
            for k, (a, b) in enumerate(cut):
                sp.dma_start(same_row[a * P:b * P].rearrange("(t p) -> t p", p=P), fl[k][:, :]).then_inc(kept, 16)
                sp.dma_start(far_row[a * P:b * P].rearrange("(t p) -> t p", p=P), ng[k][:, :]).then_inc(kept, 16)
            sp.wait_ge(kept, 64)

        @block.vector
        def _(dve):
            link = Link(dve, linked)
            link(nc.vector.memset(edge[:, :], -1.0))
            dve.wait_ge(loaded, 16)
            link(nc.vector.tensor_copy(v[:, :], rec[:, :, 0].bitcast(FP32)))
            nc.vector.tensor_copy(w[:, :], rec[:, :, 1].bitcast(FP32)).then_inc(ready, 1)
            dve.wait_ge(turned, 1)
            for k in range(2):
                link(nc.vector.tensor_copy(vT[k][:, :], tp[k][:, :]))
                last_i = link(nc.vector.tensor_copy(wT[k][:, :], wp[k][:, :]))
            nc.vector.memset(edge[:, :], -1.0).then_inc(evac, 1)
            dve.wait_ge(evac, 1)
            dve.wait_ge(reread, 64)
            for k in range(2):
                link(nc.vector.tensor_tensor(fl[k][:, :], vT[k][:, :], pv[k][:, :], ALU.is_equal))
                link(nc.vector.tensor_scalar(ng[k][:, :], fl[k][:, :], -1.0, 1e30, ALU.add, ALU.mult))
                link(nc.vector.tensor_tensor(nx[k][:, :], vT[k][:, :], nx[k][:, :], ALU.not_equal))
            nc.vector.tensor_copy(pv[0][:, 0:1], nx[0][:, 0:1]).then_inc(marked, 1)
            dve.wait_ge(back, 1)
            link(nc.vector.tensor_copy(last[:, :], bp[:, :]))

        @block.tensor
        def _(pe):
            pe.wait_ge(ready, 1)
            for k, (a, b) in enumerate(cut):
                nc.tensor.transpose(tp[k][:, :], v[:, a:b], c.ident[:, :])
                mm = nc.tensor.transpose(wp[k][:, :], w[:, a:b], c.ident[:, :])
            mm.then_inc(turned, 1)
            pe.wait_ge(marked, 1)
            for k, (a, b) in enumerate(cut):
                mm = nc.tensor.transpose(bp[:, a:b], nx[k][:, :], c.ident[0:b - a, 0:b - a])
            mm.then_inc(back, 1)


def source_scale(nc, c, same_row, w_row, deg_row, dis_table):
    T0, T1 = P, NT - P
    HALF = SLOTS // 2
    with Scope(nc, "dis_") as s:
        fl = s.sb("fl", [1, HALF])
        wr = s.sb("wr", [1, HALF])
        carry = s.sb("carry", [1, 1])
        dT = [s.sb("dT0", [T0, P]), s.sb("dT1", [T1, P])]
        deg = s.sb("deg", [P, NT])
        pos = s.sb("pos", [P, NT])
        wide = s.sb("wide", [P, NT, 4])
        zero = s.sb("zero", [1, 4])
        bp = s.ps("bp", [P, NT])
        loaded, scanned, stored, reread, back, floored, rooted, filled, kept, linked = (
            s.sem(n) for n in ("loaded", "scanned", "stored", "reread", "back", "floored", "rooted", "filled", "kept", "linked"))
        cut = ((0, T0), (T0, NT))
        block = s.block()

        def row(a, h):
            return a[h * HALF:(h + 1) * HALF].rearrange("(a n) -> a n", a=1)

        @block.sync
        def _(sp):
            for h in range(2):
                wait(sp, stored, 16 * h)
                sp.dma_start(fl[:, :], row(same_row, h)).then_inc(loaded, 16)
                sp.dma_start(wr[:, :], row(w_row, h)).then_inc(loaded, 16)
                sp.wait_ge(scanned, h + 1)
                sp.dma_start(row(deg_row, h), wr[:, :]).then_inc(stored, 16)
            sp.wait_ge(stored, 32)
            for k, (a, b) in enumerate(cut):
                sp.dma_start(dT[k][:, :], deg_row[a * P:b * P].rearrange("(t p) -> t p", p=P)).then_inc(reread, 16)
            sp.wait_ge(filled, 1)
            sp.dma_start(dis_table[0:SLOTS, :].rearrange("(p t) k -> p t k", p=P), wide[:, :, :]).then_inc(kept, 16)
            sp.dma_start(dis_table[ZERO:ZERO + 1, :], zero[:, :]).then_inc(kept, 16)
            sp.wait_ge(kept, 32)

        @block.tensor
        def _(pe):
            pe.wait_ge(reread, 32)
            for k, (a, b) in enumerate(cut):
                mm = nc.tensor.transpose(bp[:, a:b], dT[k][:, :], c.ident[0:b - a, 0:b - a])
            mm.then_inc(back, 1)

        @block.scalar
        def _(act):
            act.wait_ge(floored, 1)
            nc.scalar.activation(deg[:, :], deg[:, :], ACT.Sqrt).then_inc(rooted, 1)

        @block.vector
        def _(dve):
            link = Link(dve, linked)
            link(nc.vector.memset(carry[:, :], 0.0))
            for h in range(2):
                dve.wait_ge(loaded, 32 * (h + 1))
                link(nc.vector.tensor_tensor_scan(out=wr[:, :], data0=fl[:, :], data1=wr[:, :], initial=carry[:, :],
                                                  op0=ALU.mult, op1=ALU.add))
                nc.vector.tensor_copy(carry[:, :], wr[:, HALF - 1:HALF]).then_inc(scanned, 1)
                dve.wait_ge(scanned, h + 1)
            link(nc.vector.memset(zero[:, :], 0.0))
            dve.wait_ge(back, 1)
            link(nc.vector.tensor_scalar(pos[:, :], bp[:, :], 0.0, None, ALU.is_gt))
            nc.vector.tensor_scalar(deg[:, :], bp[:, :], 1e-30, None, ALU.max).then_inc(floored, 1)
            dve.wait_ge(rooted, 1)
            link(nc.vector.reciprocal(deg[:, :], deg[:, :]))
            link(nc.vector.tensor_tensor(deg[:, :], deg[:, :], pos[:, :], ALU.mult))
            link(nc.vector.tensor_scalar(c.neg_dis[:, :], deg[:, :], -1.0, None, ALU.mult))
            nc.vector.tensor_copy(wide[:, :, :], bc(deg[:, :], 4)).then_inc(filled, 1)


class Norm:

    def __init__(self, nc, s, c, n, rows=P, tag=""):
        self.nc, self.c, self.n = nc, c, n
        self.sum = s.sb(tag + "ln_sum", [rows, n])
        self.sq = s.sb(tag + "ln_sq", [rows, n, D])
        self.std = s.sb(tag + "ln_std", [rows, n])
        self.var_ready, self.rooted = s.sem(tag + "var_ready"), s.sem(tag + "rooted")

    def dve(self, dve, link, turn, y, out):
        v = self.nc.vector
        link(v.tensor_reduce(self.sum[:, :], y, AX.X, ALU.add))
        link(v.tensor_scalar(self.sum[:, :], self.sum[:, :], 1.0 / D, None, ALU.mult))
        link(v.tensor_tensor(y, y, bc(self.sum[:, :], D), ALU.subtract))
        link(v.tensor_tensor(self.sq[:, :, :], y, y, ALU.mult))
        v.tensor_reduce(self.std[:, :], self.sq[:, :, :], AX.X, ALU.add).then_inc(self.var_ready, 1)
        dve.wait_ge(self.rooted, turn + 1)
        link(v.reciprocal(self.std[:, :], self.std[:, :]))
        link(v.tensor_tensor(out, y, bc(self.std[:, :], D), ALU.mult))

    def root(self, act, turn):
        act.wait_ge(self.var_ready, turn + 1)
        self.nc.scalar.activation(self.std[:, :], self.std[:, :], ACT.Sqrt, bias=self.c.eps[0:self.std.shape[0], :],
                                  scale=1.0 / D).then_inc(self.rooted, 1)


def chunk_of(table, first_row, i, b, words, width=None):
    t = table[first_row:first_row + SLOTS, :].rearrange("(p t) k -> p (t k)", p=P)
    return t[:, bass.ds((i * 2 + b) * (CT * words), CT * words)]


def flag_chunk(row, i, b):
    return row[bass.ds((i * 2 + b) * CW, CW)].rearrange("(a n) -> a n", a=1).to_broadcast([P, CW])


def flat(t):
    return t.rearrange("p t k -> p (t k)")


def pieces():
    return ((0, 512), (512, CW))


def turn_64(nc, out, rows, ident, waits):
    if waits:
        return nc.tensor.matmul(out, rows, ident[:, :], start=True, stop=True)
    return nc.tensor.transpose(out, rows, ident[:, :])


class Gather:

    def __init__(self, nc, s, jobs, width):
        self.nc, self.jobs = nc, jobs
        self.buf = [s.sb(f"gathered_rows{b}", [P, CT, width]) for b in range(2)]
        self.stage = [[s.sb(f"stage{j}_{b}", [P, CT], I32) for b in range(2)] for j in range(len(jobs))]
        self.gate = s.sb("gate", [P, 2], I32)
        self.gates = s.sem("gates")
        self.staged = [s.sem(f"staged{b}") for b in range(2)]
        self.done = [s.sem(f"gathered{b}") for b in range(2)]
        self.per = 16 * CT * len(jobs)

    def sp(self, sp, i, b):
        wait(sp, self.done[b], i * self.per)
        for j, job in enumerate(self.jobs):
            sp.dma_start(self.stage[j][b][:, :], job[1][:, bass.ds((i * 2 + b) * CT, CT)]).then_inc(self.staged[b], 16)

    def start(self, pool):
        self.nc.gpsimd.memset(self.gate[:, :], 0).then_inc(self.gates, 1)

    def pool(self, pool, i, b):
        pool.wait_ge(self.staged[b], (i + 1) * (16 * len(self.jobs)))
        pass_gate(self.nc, pool, self.gate, self.gates, i * 2 + b + 1)
        for j, (table, _, at, words) in enumerate(self.jobs):
            for k in range(CT):
                self.nc.gpsimd.indirect_dma_start(
                    out=self.buf[b][:, k, at:at + words], out_offset=None, in_=table[:, :],
                    in_offset=bass.IndirectOffsetOnAxis(ap=self.stage[j][b][:, k:k + 1].bitcast(U32), axis=0),
                ).then_inc(self.done[b], 16)

    def wait(self, eng, i, b):
        eng.wait_ge(self.done[b], (i + 1) * self.per)


def load_weights(nc, c, a):
    with Scope(nc, "w_") as s:
        w = s.sb("l1w", [D, 6, D])
        half = s.sb("half", [P, 2, D])
        brow = s.sb("brow", [1, 8, D])
        mrow = s.sb("mrow", [P, D])
        t = s.sb("t", [P, D])
        loaded, linked = s.sem("loaded"), s.sem("linked")
        block = s.block()
        W1, W2, WR = a["L0_gnn_W1"], a["L0_gnn_W2"], a["L0_gnn_Wres"]
        loads = []

        def row(v):
            return v.rearrange("(a n) -> a n", a=1)

        src_part = [W1, W2, None, None, W2, None, None, WR]
        dst_part = [W1, W2, W1, W2, None, W2, WR, None]
        for k in range(8):
            if src_part[k] is not None:
                loads.append((c.w0[0:D, k, :], src_part[k][:, :]))
            if dst_part[k] is not None:
                loads.append((c.w0[D:P, k, :], dst_part[k][:, :]))
        b1, b2, br = row(a["L0_gnn_b1"]), row(a["L0_gnn_b2"]), row(a["L0_gnn_bres"])
        for k, v in enumerate((b1, b2, b1, b2, b2, b2, br, br)):
            loads.append((c.b0[0:1, k, :], v))
        m0 = row(a["L0_gnn_m"][0, :, :].rearrange("h k -> (h k)"))
        loads.append((c.m0[:, :], m0.to_broadcast([P, D])))
        for h in range(2):
            loads.append((c.wiso[h * D:(h + 1) * D, h * D:(h + 1) * D], W2[:, :]))
            loads.append((half[h * D:(h + 1) * D, 0, :], WR[:, :]))
            loads.append((c.b1x[0:1, h, :], row(a["L1_gnn_b"])))
            loads.append((brow[0:1, h, :], b2))
            loads.append((brow[0:1, 2 + h, :], br))
        loads.append((w[:, :, :], a["L1_gnn_W"].rearrange("k i o -> i k o")))
        loads.append((c.w31[:, :], a["L3_gnn_W1"][:, :]))
        loads.append((c.w32[:, :], a["L3_gnn_W2"][:, :]))
        loads.append((c.b31[:, :], a["L3_gnn_b1"].rearrange("(n a) -> n a", a=1)))
        loads.append((c.b32[:, :], row(a["L3_gnn_b2"]).to_broadcast([P, D])))

        zeroed, copied = s.sem("zeroed"), s.sem("copied")

        @block.sync
        def _(sp):
            sp.wait_ge(zeroed, 3)
            for o, v in loads:
                sp.dma_start(o, v).then_inc(loaded, 16)
            sp.wait_ge(copied, 1)
            for o, v in ((c.w1d[D:P, D:2 * D], c.w1d[0:D, 0:D]),):
                sp.dma_start(o, v).then_inc(loaded, 16)
            sp.wait_ge(loaded, 16 * (len(loads) + 1))

        @block.vector
        def _(dve):
            link = Link(dve, linked)
            v = nc.vector
            v.memset(c.w0[:, :, :], 0.0).then_inc(zeroed, 1)
            v.memset(c.wiso[:, :], 0.0).then_inc(zeroed, 1)
            v.memset(c.w1d[:, :], 0.0).then_inc(zeroed, 1)
            link(v.memset(c.eps[:, :], EPS))
            dve.wait_ge(zeroed, 3)
            dve.wait_ge(loaded, 16 * len(loads))
            link(v.tensor_scalar(c.w0[D:P, 2:4, :], c.w0[D:P, 2:4, :], 2.0, None, ALU.mult))
            link(v.tensor_scalar(c.b0[:, 0:4, :], c.b0[:, 0:4, :], 2.0, None, ALU.mult))
            for h in range(2):
                q = c.wiso[h * D:(h + 1) * D, h * D:(h + 1) * D]
                link(v.tensor_tensor(q, q, c.m0[h * D:(h + 1) * D, :], ALU.mult))
                link(v.tensor_tensor(q, q, half[h * D:(h + 1) * D, 0, :], ALU.add))
                link(v.tensor_tensor(c.biso[:, h, :], brow[:, h, :], c.m0[0:1, :], ALU.mult))
                link(v.tensor_tensor(c.biso[:, h, :], c.biso[:, h, :], brow[:, 2 + h, :], ALU.add))
            link(v.tensor_tensor(c.w1d[0:D, 0:D], w[:, 0, :], w[:, 2, :], ALU.subtract))
            v.tensor_tensor(c.w1d[0:D, 0:D], c.w1d[0:D, 0:D], w[:, 4, :], ALU.add).then_inc(copied, 1)
            link(v.tensor_tensor(c.wp[:, 0, D:], w[:, 1, :], w[:, 3, :], ALU.subtract))
            link(v.tensor_tensor(c.wp[:, 0, D:], c.wp[:, 0, D:], w[:, 5, :], ALU.add))
            for k, hi in ((1, 4), (2, 5)):
                link(v.tensor_tensor(c.wp[:, k, D:], w[:, k + 1, :], w[:, hi, :], ALU.subtract))
                link(v.tensor_scalar(c.wp[:, k, D:], c.wp[:, k, D:], 2.0, None, ALU.mult))
            for k in (3, 4):
                link(v.tensor_scalar(c.wp[:, k, D:], w[:, k + 1, :], 2.0, None, ALU.mult))
            for k in range(5):
                link(v.tensor_copy(c.wp[:, k, 0:D], c.ident[0:D, 0:D]))


def attention_sums(nc, c, by_dst, same, stash, d_table, x1_table):
    W = 2 * D + META
    with Scope(nc, "att_") as s:
        xb = [s.sb(f"ends{b}", [P, CT, 2 * D]) for b in range(2)]
        fl = [s.sb(f"same{b}", [P, CW]) for b in range(2)]
        xn = s.sb("normed", [P, CT, 2 * D])
        low, high_, rng = (s.sb(n, [P, 2 * CT]) for n in ("low", "high", "range"))
        xnT = s.sb("normedT", [P, CW])
        sg = s.sb("sigmoid", [P, CT, 4 * D])
        eb = s.sb("exps", [P, CT, 5 * D])
        rr = s.sb("rest", [P, CT, 4 * D])
        sca, scb = s.sb("scan_a", [P, CW]), s.sb("scan_b", [D, CW])
        ca, cb = s.sb("carry_a", [P, 1]), s.sb("carry_b", [D, 1])
        t1, t2 = s.sb("t1", [P, CT, D]), s.sb("t2", [P, CT, D])
        sl, sr = s.sb("sum_l", [P, CT, D]), s.sb("sum_r", [P, CT, D])
        dv = [s.sb(f"delta{b}", [P, CT, D]) for b in range(2)]
        st = [s.sb(f"stash{b}", [P, CT, 4 * D]) for b in range(2)]
        xs1 = [s.sb(f"x1_src{b}", [P, CT, D]) for b in range(2)]
        ones = s.sb("ones_row", [1, P])
        zero = s.sb("zero_row", [1, D])
        norm = Norm(nc, s, c, CT)
        pA = s.ps("pA", [P, 1024])
        pB = s.ps("pB", [P, 1024])
        q = [s.ps(f"q{k}", [P, 512]) for k in range(2)]
        loaded = [s.sem(f"loaded{b}") for b in range(2)]
        stored = [s.sem(f"stored{b}") for b in range(2)]
        (normed, turned, evac, product, read_s, read_c, expd, fed, turned2, scanned, back, finished, linked, zeroed) = (
            s.sem(n) for n in ("normed", "turned", "evac", "product", "read_sig", "read_copy", "expd", "fed", "turned2",
                               "scanned", "back", "finished", "linked", "zeroed"))
        block = s.block()
        src3 = by_dst.rearrange("(p t) k -> p t k", p=P)

        @block.sync
        def _(sp):
            sp.wait_ge(zeroed, 1)
            sp.dma_start(d_table[ZERO:ZERO + 1, :], zero[:, :]).then_inc(zeroed, 16)

            def loads(i):
                for b in range(2):
                    wait(sp, finished, i * 2 + b - 1)
                    sp.dma_start(xb[b][:, :, :], src3[:, bass.ds((i * 2 + b) * CT, CT), 0:2 * D]).then_inc(loaded[b], 16)
                    sp.dma_start(fl[b][:, :], flag_chunk(same, i, b)).then_inc(loaded[b], 16)

            turns(sp, PAIRS, loads)
            sp.wait_ge(zeroed, 17)
            for b in range(2):
                sp.wait_ge(stored[b], 48 * PAIRS)

        @block.gpsimd
        def _(pool):
            def body(i):
                for b in range(2):
                    pool.wait_ge(finished, i * 2 + b + 1)
                    pool.dma_start(chunk_of(d_table, 0, i, b, D), flat(dv[b][:, :, :])).then_inc(stored[b], 16)
                    pool.dma_start(chunk_of(stash, 0, i, b, 4 * D), flat(st[b][:, :, :])).then_inc(stored[b], 16)
                    pool.dma_start(chunk_of(x1_table, SLOTS, i, b, D), flat(xs1[b][:, :, :])).then_inc(stored[b], 16)
            turns(pool, PAIRS, body)

        @block.tensor
        def _(pe):
            def body(i):
                for b in range(2):
                    n = i * 2 + b
                    pe.wait_ge(normed, n + 1)
                    wait(pe, finished, n)
                    for k in range(CT):
                        mm = nc.tensor.transpose(pA[:, k * P:(k + 1) * P], xn[:, k, :], c.ident[:, :])
                    mm.then_inc(turned, 1)
                    pe.wait_ge(evac, n + 1)
                    for k in range(CT):
                        t = n * CT + k
                        wait(pe, read_s, t - 1)
                        wait(pe, read_c, t - 1)
                        par = (b * CT + k) % 2
                        nc.tensor.matmul(q[par][:, :], xnT[:, k * P:(k + 1) * P], c.w0[:, :, :].rearrange("p a b -> p (a b)"),
                                         start=True, stop=False)
                        nc.tensor.matmul(q[par][:, :], ones[:, :], c.b0[:, :, :].rearrange("p a b -> p (a b)"),
                                         start=False, stop=True).then_inc(product, 1)
                    pe.wait_ge(fed, n + 1)
                    for k in range(CT):
                        nc.tensor.transpose(pA[:, k * P:(k + 1) * P], eb[:, k, 0:2 * D], c.ident[:, :])
                        mm = nc.tensor.transpose(pB[0:D, k * P:(k + 1) * P], eb[:, k, 2 * D:3 * D], c.ident[:, :])
                    mm.then_inc(turned2, 1)
                    pe.wait_ge(scanned, n + 1)
                    for k in range(CT):
                        nc.tensor.transpose(pA[:, k * P:(k + 1) * P], sca[:, k * P:(k + 1) * P], c.ident[:, :])
                        mm = nc.tensor.transpose(pB[:, k * D:(k + 1) * D], scb[:, k * P:(k + 1) * P], c.ident[0:D, 0:D])
                    mm.then_inc(back, 1)
            pe.wait_ge(zeroed, 1)
            turns(pe, PAIRS, body)

        @block.scalar
        def _(act):
            def body(i):
                for b in range(2):
                    n = i * 2 + b
                    act.wait_ge(turned, n + 1)
                    nc.scalar.activation(xnT[:, :], pA[:, 0:CW], ACT.Copy).then_inc(evac, 1)
                    wait(act, finished, n)
                    for k in range(CT):
                        par = (b * CT + k) % 2
                        act.wait_ge(product, n * CT + k + 1)
                        nc.scalar.activation(sg[:, k, :], q[par][:, 0:4 * D], ACT.Sigmoid).then_inc(read_s, 1)
                    act.wait_ge(read_s, n * CT + CT)
                    nc.scalar.activation(eb[:, :, D:5 * D], sg[:, :, :], ACT.Exp).then_inc(expd, 1)
                    norm.root(act, n)
            turns(act, PAIRS, body)

        @block.vector
        def _(dve):
            link = Link(dve, linked)
            v = nc.vector
            link(v.memset(ca[:, :], 0.0))
            link(v.memset(cb[:, :], 0.0))
            link(v.memset(ones[:, :], 1.0))
            v.memset(zero[:, :], 0.0).then_inc(zeroed, 1)

            def body(i):
                for b in range(2):
                    n = i * 2 + b
                    dve.wait_ge(loaded[b], i * 32 + 32)
                    x2 = xb[b][:, :, :].rearrange("p t (e k) -> p (t e) k", e=2)
                    n2 = xn[:, :, :].rearrange("p t (e k) -> p (t e) k", e=2)
                    link(v.tensor_reduce(low[:, :], x2, AX.X, ALU.min))
                    link(v.tensor_reduce(high_[:, :], x2, AX.X, ALU.max))
                    link(v.scalar_tensor_tensor(out=rng[:, :], in0=high_[:, :], scalar=EPS, in1=low[:, :],
                                                op0=ALU.add, op1=ALU.subtract))
                    link(v.reciprocal(rng[:, :], rng[:, :]))
                    wait(dve, turned, n)
                    link(v.tensor_tensor(n2, x2, bc(low[:, :], D), ALU.subtract))
                    v.tensor_tensor(n2, n2, bc(rng[:, :], D), ALU.mult).then_inc(normed, 1)
                    for k in range(CT):
                        par = (b * CT + k) % 2
                        dve.wait_ge(read_s, n * CT + k + 1)
                        v.tensor_copy(rr[:, k, :], q[par][:, 4 * D:8 * D]).then_inc(read_c, 1)
                    dve.wait_ge(read_c, n * CT + CT)
                    rs, rd, resd, ress = (rr[:, :, k * D:(k + 1) * D] for k in range(4))
                    er, sel, ser = eb[:, :, 2 * D:3 * D], eb[:, :, 3 * D:4 * D], eb[:, :, 4 * D:5 * D]
                    dve.wait_ge(expd, n + 1)
                    v.tensor_tensor(eb[:, :, 0:D], eb[:, :, D:2 * D], rs, ALU.mult).then_inc(fed, 1)
                    dve.wait_ge(turned2, n + 1)
                    link(v.tensor_tensor_scan(out=sca[:, :], data0=fl[b][:, :], data1=pA[:, 0:CW], initial=ca[:, :],
                                              op0=ALU.mult, op1=ALU.add))
                    link(v.tensor_tensor_scan(out=scb[:, :], data0=fl[b][0:D, :], data1=pB[0:D, 0:CW], initial=cb[:, :],
                                              op0=ALU.mult, op1=ALU.add))
                    link(v.tensor_copy(ca[:, :], sca[:, CW - 1:CW]))
                    v.tensor_copy(cb[:, :], scb[:, CW - 1:CW]).then_inc(scanned, 1)
                    dve.wait_ge(scanned, n + 1)
                    wait(dve, stored[b], i * 48)
                    dve.wait_ge(back, n + 1)
                    back_a = pA[:, 0:CW].rearrange("p (t k) -> p t k", k=P)
                    back_b = pB[:, 0:CT * D].rearrange("p (t k) -> p t k", k=D)
                    link(v.tensor_tensor(t1[:, :, :], sel, rd, ALU.mult))
                    link(v.tensor_tensor(t1[:, :, :], back_a[:, :, 0:D], t1[:, :, :], ALU.add))
                    link(v.tensor_tensor(sl[:, :, :], back_a[:, :, D:P], sel, ALU.add))
                    link(v.tensor_tensor(sr[:, :, :], back_b, ser, ALU.add))
                    link(v.reciprocal(sl[:, :, :], sl[:, :, :]))
                    link(v.reciprocal(sr[:, :, :], sr[:, :, :]))
                    link(v.tensor_tensor(t1[:, :, :], t1[:, :, :], sl[:, :, :], ALU.mult))
                    link(v.tensor_tensor(dv[b][:, :, :], t1[:, :, :], rd, ALU.subtract))
                    so = st[b]
                    link(v.tensor_copy(so[:, :, 0:D], er))
                    link(v.tensor_copy(so[:, :, D:2 * D], rs))
                    w3 = so[:, :, 2 * D:3 * D]
                    link(v.tensor_tensor(w3, sr[:, :, :], c.m0[:, :].unsqueeze(1).to_broadcast([P, CT, D]), ALU.mult))
                    link(v.tensor_tensor(t1[:, :, :], t1[:, :, :], ser, ALU.mult))
                    link(v.tensor_tensor(t1[:, :, :], t1[:, :, :], w3, ALU.mult))
                    link(v.tensor_tensor(t1[:, :, :], t1[:, :, :], resd, ALU.add))
                    link(v.tensor_tensor(so[:, :, 3 * D:4 * D], t1[:, :, :], xb[b][:, :, D:2 * D], ALU.add))
                    link(v.tensor_tensor(t2[:, :, :], rs, c.m0[:, :].unsqueeze(1).to_broadcast([P, CT, D]), ALU.mult))
                    link(v.tensor_tensor(t2[:, :, :], t2[:, :, :], ress, ALU.add))
                    link(v.tensor_tensor(t2[:, :, :], t2[:, :, :], xb[b][:, :, 0:D], ALU.add))
                    norm.dve(dve, link, n, t2[:, :, :], xs1[b][:, :, :])
                    v.tensor_copy(t1[:, 0, 0:1], t2[:, 0, 0:1]).then_inc(finished, 1)
                    dve.wait_ge(finished, n + 1)
            turns(dve, PAIRS, body, [link])
            for b in range(2):
                pass


def attention_out(nc, c, same, stash, d_table, x1_table):
    with Scope(nc, "ato_") as s:
        g = Gather(nc, s, [(d_table, c.idx["b1"], 0, D)], D)
        st = [s.sb(f"stash{b}", [P, CT, 4 * D]) for b in range(2)]
        fl = [s.sb(f"same{b}", [P, CW]) for b in range(2)]
        t = s.sb("t", [P, CT, D])
        sc = s.sb("scan", [D, CW])
        ca = s.sb("carry", [D, 1])
        y = s.sb("y", [P, CT, D])
        o = [s.sb(f"out{b}", [P, CT, D]) for b in range(2)]
        norm = Norm(nc, s, c, CT)
        pT = s.ps("pT", [D, 1024])
        pR = s.ps("pR", [P, 512])
        loaded = [s.sem(f"loaded{b}") for b in range(2)]
        stored = [s.sem(f"stored{b}") for b in range(2)]
        fed, turned, scanned, back, finished, linked = (s.sem(n) for n in ("fed", "turned", "scanned", "back", "finished", "linked"))
        block = s.block()

        @block.sync
        def _(sp):
            def body(i):
                for b in range(2):
                    g.sp(sp, i, b)
                    wait(sp, finished, i * 2 + b - 1)
                    sp.dma_start(flat(st[b][:, :, :]), chunk_of(stash, 0, i, b, 4 * D)).then_inc(loaded[b], 16)
                    sp.dma_start(fl[b][:, :], flag_chunk(same, i, b)).then_inc(loaded[b], 16)
            turns(sp, PAIRS, body)

        @block.gpsimd
        def _(pool):
            g.start(pool)

            def body(i):
                for b in range(2):
                    wait(pool, finished, i * 2 + b - 1)
                    g.pool(pool, i, b)
            turns(pool, PAIRS, body)

        @block.tensor
        def _(pe):
            def body(i):
                for b in range(2):
                    n = i * 2 + b
                    pe.wait_ge(fed, n + 1)
                    for k in range(CT):
                        mm = turn_64(nc, pT[:, k * P:(k + 1) * P], t[:, k, :], c.ident, k == 0)
                    mm.then_inc(turned, 1)
                    pe.wait_ge(scanned, n + 1)
                    for k in range(CT):
                        mm = nc.tensor.matmul(pR[:, k * D:(k + 1) * D], sc[:, k * P:(k + 1) * P], c.ident[0:D, 0:D], start=True, stop=True)
                    mm.then_inc(back, 1)
            turns(pe, PAIRS, body)

        @block.scalar
        def _(act):
            def body(i):
                for b in range(2):
                    norm.root(act, i * 2 + b)
                    act.wait_ge(finished, i * 2 + b + 1)
                    act.dma_start(chunk_of(x1_table, 0, i, b, D), flat(o[b][:, :, :])).then_inc(stored[b], 16)
            turns(act, PAIRS, body)
            for b in range(2):
                act.wait_ge(stored[b], 16 * PAIRS)

        @block.vector
        def _(dve):
            link = Link(dve, linked)
            v = nc.vector
            link(v.memset(ca[:, :], 0.0))

            def body(i):
                for b in range(2):
                    n = i * 2 + b
                    g.wait(dve, i, b)
                    dve.wait_ge(loaded[b], i * 32 + 32)
                    so = st[b]
                    link(v.tensor_tensor(t[:, :, :], g.buf[b][:, :, :], so[:, :, D:2 * D], ALU.add))
                    v.tensor_tensor(t[:, :, :], t[:, :, :], so[:, :, 0:D], ALU.mult).then_inc(fed, 1)
                    dve.wait_ge(turned, n + 1)
                    link(v.tensor_tensor_scan(out=sc[:, :], data0=fl[b][0:D, :], data1=pT[:, 0:CW], initial=ca[:, :],
                                              op0=ALU.mult, op1=ALU.add))
                    v.tensor_copy(ca[:, :], sc[:, CW - 1:CW]).then_inc(scanned, 1)
                    dve.wait_ge(scanned, n + 1)
                    wait(dve, stored[b], i * 16)
                    dve.wait_ge(back, n + 1)
                    rows = pR[:, 0:CT * D].rearrange("p (t k) -> p t k", k=D)
                    link(v.tensor_tensor(y[:, :, :], rows, so[:, :, 2 * D:3 * D], ALU.mult))
                    link(v.tensor_tensor(y[:, :, :], y[:, :, :], so[:, :, 3 * D:4 * D], ALU.add))
                    norm.dve(dve, link, n, y[:, :, :], o[b][:, :, :])
                    v.tensor_copy(t[:, 0, 0:1], y[:, 0, 0:1]).then_inc(finished, 1)
                    dve.wait_ge(finished, n + 1)
            turns(dve, PAIRS, body, [link])


def chebyshev_start(nc, c, x1_table, t0_src, x2_table):
    with Scope(nc, "ch0_") as s:
        g = Gather(nc, s, [(x1_table, c.idx["a3"], 0, D), (x1_table, c.idx["a2"], D, D)], 2 * D)
        xT = s.sb("rowsT", [P, CW])
        y = s.sb("y", [P, CT, D])
        o = [s.sb(f"out{b}", [P, CT, D]) for b in range(2)]
        ones = s.sb("ones_row", [1, P])
        norm = Norm(nc, s, c, CT)
        pT = s.ps("pT", [P, 1024])
        pR = s.ps("pR", [P, 1024])
        stored = [s.sem(f"stored{b}") for b in range(2)]
        kept = [s.sem(f"kept{b}") for b in range(2)]
        turned, evac, product, finished, linked, ready = (s.sem(n) for n in ("turned", "evac", "product", "finished", "linked", "ready"))
        block = s.block()
        t0v = t0_src.rearrange("(p t) k -> p t k", p=P)

        @block.sync
        def _(sp):
            def body(i):
                for b in range(2):
                    g.sp(sp, i, b)
            turns(sp, PAIRS, body)

        @block.gpsimd
        def _(pool):
            g.start(pool)

            def body(i):
                for b in range(2):
                    wait(pool, finished, i * 2 + b - 1)
                    wait(pool, kept[b], i * 16)
                    g.pool(pool, i, b)
            turns(pool, PAIRS, body)

        @block.tensor
        def _(pe):
            def body(i):
                for b in range(2):
                    n = i * 2 + b
                    g.wait(pe, i, b)
                    wait(pe, evac, n)
                    for k in range(CT):
                        mm = nc.tensor.transpose(pT[:, k * P:(k + 1) * P], g.buf[b][:, k, :], c.ident[:, :])
                    mm.then_inc(turned, 1)
                    pe.wait_ge(evac, n + 1)
                    wait(pe, finished, n)
                    for k in range(CT):
                        nc.tensor.matmul(pR[:, k * P:(k + 1) * P], xT[:, k * P:(k + 1) * P], c.w1d[:, :], start=True, stop=False)
                        mm = nc.tensor.matmul(pR[:, k * P:(k + 1) * P], ones[:, :], flat(c.b1x[:, :, :]), start=False, stop=True)
                    mm.then_inc(product, 1)
            pe.wait_ge(ready, 1)
            turns(pe, PAIRS, body)

        @block.scalar
        def _(act):
            def body(i):
                for b in range(2):
                    n = i * 2 + b
                    act.wait_ge(turned, n + 1)
                    wait(act, product, n)
                    nc.scalar.activation(xT[:, :], pT[:, 0:CW], ACT.Copy).then_inc(evac, 1)
                    g.wait(act, i, b)
                    act.dma_start(t0v[:, bass.ds((i * 2 + b) * CT, CT), :], g.buf[b][:, :, 0:D]).then_inc(kept[b], 16)
                    norm.root(act, n)
                    act.wait_ge(finished, n + 1)
                    act.dma_start(chunk_of(x2_table, 2 * SLOTS, i, b, D), flat(o[b][:, :, :])).then_inc(stored[b], 16)
            turns(act, PAIRS, body)
            for b in range(2):
                act.wait_ge(kept[b], 16 * PAIRS)
                act.wait_ge(stored[b], 16 * PAIRS)

        @block.vector
        def _(dve):
            link = Link(dve, linked)
            v = nc.vector
            v.memset(ones[:, :], 1.0).then_inc(ready, 1)

            def body(i):
                for b in range(2):
                    n = i * 2 + b
                    dve.wait_ge(product, n + 1)
                    g.wait(dve, i, b)
                    wait(dve, stored[b], i * 16)
                    rows = pR[:, 0:CW].rearrange("p (t k) -> p t k", k=P)
                    at = bass.ds((i * 2 + b) * CT * D, CT * D)
                    link(v.tensor_scalar(flat(c.acc[:, :, :])[:, at].rearrange("p (t k) -> p t k", k=D), rows[:, :, 0:D], 1.0, None, ALU.mult))
                    link(v.tensor_scalar(flat(c.t_even[:, :, :])[:, at].rearrange("p (t k) -> p t k", k=D), g.buf[b][:, :, D:2 * D], 1.0, None, ALU.mult))
                    link(v.scalar_tensor_tensor(out=y[:, :, :], in0=rows[:, :, D:P], scalar=0.0, in1=g.buf[b][:, :, D:2 * D],
                                                op0=ALU.max, op1=ALU.add))
                    norm.dve(dve, link, n, y[:, :, :], o[b][:, :, :])
                    v.tensor_copy(y[:, 0, 0:1], o[b][:, 0, 0:1]).then_inc(finished, 1)
                    dve.wait_ge(finished, n + 1)
            turns(dve, PAIRS, body, [link])


def chebyshev_hop(nc, c, k_hop, same, p_in, p_out):
    with Scope(nc, f"hop{k_hop}_") as s:
        g = Gather(nc, s, [(p_in, c.idx["a4"], 0, D)], D) if k_hop else None
        fl = [s.sb(f"same{b}", [P, CW]) for b in range(2)]
        cur = s.sb("current", [P, CT, D])
        tch = s.sb("t_chunk", [P, CT, D])
        msg = s.sb("messages", [P, CT, D])
        nrm = s.sb("norms", [P, CT])
        nd = s.sb("neg_dis", [P, CT])
        sc = s.sb("scan", [D, CW])
        ca = s.sb("carry", [D, 1])
        o = [s.sb(f"out{b}", [P, CT, D]) for b in range(2)]
        pT = s.ps("pT", [D, 1024])
        pR = s.ps("pR", [P, 1024])
        loaded = [s.sem(f"loaded{b}") for b in range(2)]
        stored = [s.sem(f"stored{b}") for b in range(2)]
        fed, turned, scanned, back, finished, linked = (s.sem(n) for n in ("fed", "turned", "scanned", "back", "finished", "linked"))
        t_here = c.t_odd if k_hop % 2 else c.t_even
        block = s.block()

        @block.sync
        def _(sp):
            def body(i):
                for b in range(2):
                    if g:
                        g.sp(sp, i, b)
                    wait(sp, finished, i * 2 + b - 1)
                    sp.dma_start(fl[b][:, :], flag_chunk(same, i, b)).then_inc(loaded[b], 16)
            turns(sp, PAIRS, body)

        if g:
            @block.gpsimd
            def _(pool):
                g.start(pool)

                def body(i):
                    for b in range(2):
                        wait(pool, finished, i * 2 + b - 1)
                        g.pool(pool, i, b)
                turns(pool, PAIRS, body)

        @block.tensor
        def _(pe):
            def body(i):
                for b in range(2):
                    n = i * 2 + b
                    pe.wait_ge(fed, n + 1)
                    for k in range(CT):
                        mm = turn_64(nc, pT[:, k * P:(k + 1) * P], msg[:, k, :], c.ident, k == 0)
                    mm.then_inc(turned, 1)
                    pe.wait_ge(scanned, n + 1)
                    for k in range(CT):
                        mm = nc.tensor.matmul(pR[:, k * P:(k + 1) * P], sc[:, k * P:(k + 1) * P], c.wp[:, k_hop, :], start=True, stop=True)
                    mm.then_inc(back, 1)
            turns(pe, PAIRS, body)

        if k_hop < 4:
            @block.scalar
            def _(act):
                def body(i):
                    for b in range(2):
                        act.wait_ge(finished, i * 2 + b + 1)
                        act.dma_start(p_out[0:SLOTS, :].rearrange("(p t) k -> p t k", p=P)[:, bass.ds((i * 2 + b) * CT, CT), :],
                                      o[b][:, :, :]).then_inc(stored[b], 16)
                turns(act, PAIRS, body)
                for b in range(2):
                    act.wait_ge(stored[b], 16 * PAIRS)

        @block.vector
        def _(dve):
            link = Link(dve, linked)
            v = nc.vector
            link(v.memset(ca[:, :], 0.0))

            def body(i):
                for b in range(2):
                    n = i * 2 + b
                    at = bass.ds((i * 2 + b) * CT * D, CT * D)
                    col = bass.ds((i * 2 + b) * CT, CT)
                    here = flat(t_here[:, :, :])[:, at]
                    link(v.tensor_scalar(nrm[:, :], c.norm[:, col], 1.0, None, ALU.mult))
                    link(v.tensor_scalar(nd[:, :], c.neg_dis[:, col], 1.0, None, ALU.mult))
                    if k_hop == 0:
                        link(v.tensor_scalar(flat(cur[:, :, :]), here, 1.0, None, ALU.mult))
                        row = cur
                    elif k_hop == 1:
                        g.wait(dve, i, b)
                        link(v.tensor_scalar(here, flat(g.buf[b][:, :, :]), 1.0, None, ALU.mult))
                        row = g.buf[b]
                    else:
                        g.wait(dve, i, b)
                        link(v.tensor_scalar(flat(tch[:, :, :]), here, 1.0, None, ALU.mult))
                        link(v.scalar_tensor_tensor(out=cur[:, :, :], in0=g.buf[b][:, :, :], scalar=2.0, in1=tch[:, :, :],
                                                    op0=ALU.mult, op1=ALU.subtract))
                        link(v.tensor_scalar(here, flat(cur[:, :, :]), 1.0, None, ALU.mult))
                        row = cur
                    v.tensor_tensor(msg[:, :, :], row[:, :, :], bc(nrm[:, :], D), ALU.mult).then_inc(fed, 1)
                    dve.wait_ge(turned, n + 1)
                    dve.wait_ge(loaded[b], i * 16 + 16)
                    link(v.tensor_tensor_scan(out=sc[:, :], data0=fl[b][0:D, :], data1=pT[:, 0:CW], initial=ca[:, :],
                                              op0=ALU.mult, op1=ALU.add))
                    v.tensor_copy(ca[:, :], sc[:, CW - 1:CW]).then_inc(scanned, 1)
                    dve.wait_ge(scanned, n + 1)
                    if k_hop < 4:
                        wait(dve, stored[b], i * 16)
                    dve.wait_ge(back, n + 1)
                    rows = pR[:, 0:CW].rearrange("p (t k) -> p t k", k=P)
                    link(v.tensor_tensor(o[b][:, :, :], rows[:, :, 0:D], bc(nd[:, :], D), ALU.mult))
                    link(v.tensor_tensor(msg[:, :, :], rows[:, :, D:P], bc(nd[:, :], D), ALU.mult))
                    acc = flat(c.acc[:, :, :])[:, at].rearrange("p (t k) -> p t k", k=D)
                    link(v.tensor_tensor(acc, acc, msg[:, :, :], ALU.add))
                    v.tensor_copy(nd[:, 0:1], nrm[:, 0:1]).then_inc(finished, 1)
                    dve.wait_ge(finished, n + 1)
            turns(dve, PAIRS, body, [link])


def chebyshev_end(nc, c, t0_src, x2_table, x3_table):
    with Scope(nc, "che_") as s:
        t0 = [s.sb(f"t0_{b}", [P, CT, D]) for b in range(2)]
        y = s.sb("y", [P, CT, D])
        ro = s.sb("root_out", [P, CT])
        o = [[s.sb(f"out{j}{b}", [P, CT, D]) for b in range(2)] for j in range(3)]
        norm = Norm(nc, s, c, CT)
        loaded = [s.sem(f"loaded{b}") for b in range(2)]
        stored = [s.sem(f"stored{b}") for b in range(2)]
        finished, linked = s.sem("finished"), s.sem("linked")
        block = s.block()

        @block.sync
        def _(sp):
            def body(i):
                for b in range(2):
                    wait(sp, finished, i * 2 + b - 1)
                    sp.dma_start(flat(t0[b][:, :, :]), chunk_of(t0_src, 0, i, b, D)).then_inc(loaded[b], 16)
            turns(sp, PAIRS, body)

        @block.scalar
        def _(act):
            def body(i):
                for b in range(2):
                    n = i * 2 + b
                    norm.root(act, 2 * n)
                    norm.root(act, 2 * n + 1)
                    act.wait_ge(finished, n + 1)
                    for j, (table, first) in enumerate(((x2_table, 0), (x2_table, SLOTS), (x3_table, SLOTS))):
                        act.dma_start(chunk_of(table, first, i, b, D), flat(o[j][b][:, :, :])).then_inc(stored[b], 16)
            turns(act, PAIRS, body)
            for b in range(2):
                act.wait_ge(stored[b], 48 * PAIRS)

        @block.vector
        def _(dve):
            link = Link(dve, linked)
            v = nc.vector

            def body(i):
                for b in range(2):
                    n = i * 2 + b
                    at = bass.ds((i * 2 + b) * CT * D, CT * D)
                    dve.wait_ge(loaded[b], i * 16 + 16)
                    wait(dve, stored[b], i * 48)
                    link(v.tensor_scalar(ro[:, :], c.inv_out[:, bass.ds((i * 2 + b) * CT, CT)], 1.0, None, ALU.mult))
                    link(v.scalar_tensor_tensor(out=flat(y[:, :, :]), in0=flat(c.acc[:, :, :])[:, at], scalar=0.0,
                                                in1=flat(t0[b][:, :, :]), op0=ALU.max, op1=ALU.add))
                    norm.dve(dve, link, 2 * n, y[:, :, :], o[1][b][:, :, :])
                    link(v.tensor_tensor(o[0][b][:, :, :], o[1][b][:, :, :], bc(ro[:, :], D), ALU.mult))
                    link(v.tensor_copy(y[:, :, :], o[1][b][:, :, :]))
                    norm.dve(dve, link, 2 * n + 1, y[:, :, :], o[2][b][:, :, :])
                    v.tensor_copy(y[:, 0, 0:1], o[2][b][:, 0, 0:1]).then_inc(finished, 1)
                    dve.wait_ge(finished, n + 1)
            turns(dve, PAIRS, body, [link])


class Scatter:

    def __init__(self, nc, s, out, index):
        self.nc, self.out, self.index = nc, out, index
        self.buf = [s.sb(f"final_rows{b}", [P, CT, D]) for b in range(2)]
        self.stage = [s.sb(f"target{b}", [P, CT], I32) for b in range(2)]
        self.gate = s.sb("gate_out", [P, 2], I32)
        self.gates = s.sem("gates_out")
        self.staged = [s.sem(f"targets{b}") for b in range(2)]
        self.done = [s.sem(f"scattered{b}") for b in range(2)]
        self.per = 16 * CT

    def targets(self, act, i, b):
        wait(act, self.done[b], i * self.per)
        act.dma_start(self.stage[b][:, :], self.index[:, bass.ds((i * 2 + b) * CT, CT)]).then_inc(self.staged[b], 16)

    def start(self, pool):
        self.nc.gpsimd.memset(self.gate[:, :], 0).then_inc(self.gates, 1)

    def pool(self, pool, i, b, n):
        pool.wait_ge(self.staged[b], i * 16 + 16)
        pass_gate(self.nc, pool, self.gate, self.gates, n + 1)
        for k in range(CT):
            self.nc.gpsimd.indirect_dma_start(
                out=self.out[:, :], out_offset=bass.IndirectOffsetOnAxis(ap=self.stage[b][:, k:k + 1].bitcast(U32), axis=0),
                in_=self.buf[b][:, k, :], in_offset=None, bounds_check=N - 1, oob_is_err=False).then_inc(self.done[b], 16)


def pool_gather_scatter(pool, g, sc, finished):
    g.start(pool)
    sc.start(pool)

    def body(i):
        for b in range(2):
            wait(pool, finished, i * 2 + b - 1)
            g.pool(pool, i, b)
            if b:
                pool.wait_ge(finished, i * 2 + 1)
                sc.pool(pool, i, 0, i * 2)
            elif not isinstance(i, int):
                pool.wait_ge(finished, i * 2)
                sc.pool(pool, i - 1, 1, i * 2 - 1)
    turns(pool, PAIRS, body)
    pool.wait_ge(finished, NCH)
    sc.pool(pool, PAIRS - 1, 1, NCH - 1)
    for b in range(2):
        pool.wait_ge(sc.done[b], sc.per * PAIRS)


def light_layer(nc, c, same, x2_table, x3_table, out):
    with Scope(nc, "lgt_") as s:
        g = Gather(nc, s, [(x2_table, c.idx["b2"], 0, D), (x2_table, c.idx["b3"], D, D)], 2 * D)
        sca = Scatter(nc, s, out, c.out_b)
        fl = [s.sb(f"same{b}", [P, CW]) for b in range(2)]
        sc = s.sb("scan", [D, CW])
        ca = s.sb("carry", [D, 1])
        ri = s.sb("root_in", [P, CT])
        y = s.sb("y", [P, CT, D])
        o = [s.sb(f"out{b}", [P, CT, D]) for b in range(2)]
        norm = Norm(nc, s, c, CT)
        pT = s.ps("pT", [D, 1024])
        pR = s.ps("pR", [P, 512])
        loaded = [s.sem(f"loaded{b}") for b in range(2)]
        stored = [s.sem(f"stored{b}") for b in range(2)]
        turned, scanned, back, finished, linked = (s.sem(n) for n in ("turned", "scanned", "back", "finished", "linked"))
        block = s.block()

        @block.sync
        def _(sp):
            def body(i):
                for b in range(2):
                    g.sp(sp, i, b)
                    wait(sp, finished, i * 2 + b - 1)
                    sp.dma_start(fl[b][:, :], flag_chunk(same, i, b)).then_inc(loaded[b], 16)
            turns(sp, PAIRS, body)

        @block.gpsimd
        def _(pool):
            pool_gather_scatter(pool, g, sca, finished)

        @block.tensor
        def _(pe):
            def body(i):
                for b in range(2):
                    n = i * 2 + b
                    g.wait(pe, i, b)
                    wait(pe, scanned, n)
                    for k in range(CT):
                        mm = turn_64(nc, pT[:, k * P:(k + 1) * P], g.buf[b][:, k, 0:D], c.ident, k == 0)
                    mm.then_inc(turned, 1)
                    pe.wait_ge(scanned, n + 1)
                    for k in range(CT):
                        mm = nc.tensor.matmul(pR[:, k * D:(k + 1) * D], sc[:, k * P:(k + 1) * P], c.ident[0:D, 0:D], start=True, stop=True)
                    mm.then_inc(back, 1)
            turns(pe, PAIRS, body)

        @block.scalar
        def _(act):
            def body(i):
                for b in range(2):
                    n = i * 2 + b
                    sca.targets(act, i, b)
                    norm.root(act, 2 * n)
                    norm.root(act, 2 * n + 1)
                    act.wait_ge(finished, n + 1)
                    act.dma_start(chunk_of(x3_table, 0, i, b, D), flat(o[b][:, :, :])).then_inc(stored[b], 16)
            turns(act, PAIRS, body)
            for b in range(2):
                act.wait_ge(stored[b], 16 * PAIRS)

        @block.vector
        def _(dve):
            link = Link(dve, linked)
            v = nc.vector
            link(v.memset(ca[:, :], 0.0))

            def body(i):
                for b in range(2):
                    n = i * 2 + b
                    link(v.tensor_scalar(ri[:, :], c.inv_in[:, bass.ds((i * 2 + b) * CT, CT)], 1.0, None, ALU.mult))
                    dve.wait_ge(turned, n + 1)
                    dve.wait_ge(loaded[b], i * 16 + 16)
                    link(v.tensor_tensor_scan(out=sc[:, :], data0=fl[b][0:D, :], data1=pT[:, 0:CW], initial=ca[:, :],
                                              op0=ALU.mult, op1=ALU.add))
                    v.tensor_copy(ca[:, :], sc[:, CW - 1:CW]).then_inc(scanned, 1)
                    dve.wait_ge(scanned, n + 1)
                    wait(dve, stored[b], i * 16)
                    wait(dve, sca.done[b], i * sca.per)
                    g.wait(dve, i, b)
                    dve.wait_ge(back, n + 1)
                    rows = pR[:, 0:CT * D].rearrange("p (t k) -> p t k", k=D)
                    link(v.tensor_tensor(y[:, :, :], rows, bc(ri[:, :], D), ALU.mult))
                    link(v.tensor_tensor(y[:, :, :], y[:, :, :], g.buf[b][:, :, D:2 * D], ALU.add))
                    norm.dve(dve, link, 2 * n, y[:, :, :], o[b][:, :, :])
                    link(v.tensor_copy(y[:, :, :], o[b][:, :, :]))
                    norm.dve(dve, link, 2 * n + 1, y[:, :, :], sca.buf[b][:, :, :])
                    v.tensor_copy(y[:, 0, 0:1], sca.buf[b][:, 0, 0:1]).then_inc(finished, 1)
                    dve.wait_ge(finished, n + 1)
            turns(dve, PAIRS, body, [link])


def edge_layer(nc, c, far, x3_table, out):
    with Scope(nc, "edg_") as s:
        g = Gather(nc, s, [(x3_table, c.idx["a6"], 0, D), (x3_table, c.idx["a5"], D, D)], 2 * D)
        sca = Scatter(nc, s, out, c.out_a)
        fl = [s.sb(f"far{b}", [P, CW]) for b in range(2)]
        hin = s.sb("hin", [P, CT, 2 * D])
        hT = s.sb("hT", [P, CW])
        h1 = s.sb("h1", [P, CW])
        sc = s.sb("scan", [D, CW])
        ca = s.sb("carry", [D, 1])
        y = s.sb("y", [P, CT, D])
        norm = Norm(nc, s, c, CT)
        pT = s.ps("pT", [P, 1024])
        pH = s.ps("pH", [P, 1024])
        pO = s.ps("pO", [D, 1024])
        pR = s.ps("pR", [P, 512])
        loaded = [s.sem(f"loaded{b}") for b in range(2)]
        fed, turned, evac, hid, act1, outp, scanned, back, finished, linked = (
            s.sem(n) for n in ("fed", "turned", "evac", "hidden", "relu", "product", "scanned", "back", "finished", "linked"))
        block = s.block()

        @block.sync
        def _(sp):
            def body(i):
                for b in range(2):
                    g.sp(sp, i, b)
                    wait(sp, finished, i * 2 + b - 1)
                    sp.dma_start(fl[b][:, :], flag_chunk(far, i, b)).then_inc(loaded[b], 16)
            turns(sp, PAIRS, body)

        @block.gpsimd
        def _(pool):
            pool_gather_scatter(pool, g, sca, finished)

        @block.tensor
        def _(pe):
            def body(i):
                for b in range(2):
                    n = i * 2 + b
                    pe.wait_ge(fed, n + 1)
                    for k in range(CT):
                        mm = nc.tensor.transpose(pT[:, k * P:(k + 1) * P], hin[:, k, :], c.ident[:, :])
                    mm.then_inc(turned, 1)
                    pe.wait_ge(evac, n + 1)
                    for a, z in pieces():
                        mm = nc.tensor.matmul(pH[:, a:z], c.w31[:, :], hT[:, a:z], start=True, stop=True)
                    mm.then_inc(hid, 1)
                    pe.wait_ge(act1, n + 1)
                    for a, z in pieces():
                        mm = nc.tensor.matmul(pO[:, a:z], c.w32[:, :], h1[:, a:z], start=True, stop=True)
                    mm.then_inc(outp, 1)
                    pe.wait_ge(scanned, n + 1)
                    for k in range(CT):
                        mm = nc.tensor.matmul(pR[:, k * D:(k + 1) * D], sc[:, k * P:(k + 1) * P], c.ident[0:D, 0:D], start=True, stop=True)
                    mm.then_inc(back, 1)
            turns(pe, PAIRS, body)

        @block.scalar
        def _(act):
            def body(i):
                for b in range(2):
                    n = i * 2 + b
                    sca.targets(act, i, b)
                    act.wait_ge(turned, n + 1)
                    nc.scalar.activation(hT[:, :], pT[:, 0:CW], ACT.Copy).then_inc(evac, 1)
                    act.wait_ge(hid, n + 1)
                    nc.scalar.activation(h1[:, :], pH[:, 0:CW], ACT.Relu, bias=c.b31[:, :]).then_inc(act1, 1)
                    norm.root(act, n)
            turns(act, PAIRS, body)

        @block.vector
        def _(dve):
            link = Link(dve, linked)
            v = nc.vector
            link(v.memset(ca[:, :], 0.0))

            def body(i):
                for b in range(2):
                    n = i * 2 + b
                    g.wait(dve, i, b)
                    link(v.tensor_copy(hin[:, :, 0:D], g.buf[b][:, :, 0:D]))
                    v.tensor_tensor(hin[:, :, D:2 * D], g.buf[b][:, :, D:2 * D], g.buf[b][:, :, 0:D], ALU.subtract).then_inc(fed, 1)
                    dve.wait_ge(outp, n + 1)
                    dve.wait_ge(loaded[b], i * 16 + 16)
                    link(v.tensor_tensor_scan(out=sc[:, :], data0=fl[b][0:D, :], data1=pO[:, 0:CW], initial=ca[:, :],
                                              op0=ALU.add, op1=ALU.max))
                    v.tensor_copy(ca[:, :], sc[:, CW - 1:CW]).then_inc(scanned, 1)
                    dve.wait_ge(scanned, n + 1)
                    wait(dve, sca.done[b], i * sca.per)
                    dve.wait_ge(back, n + 1)
                    rows = pR[:, 0:CT * D].rearrange("p (t k) -> p t k", k=D)
                    link(v.tensor_tensor(y[:, :, :], rows, c.b32[:, :].unsqueeze(1).to_broadcast([P, CT, D]), ALU.add))
                    link(v.tensor_tensor(y[:, :, :], y[:, :, :], g.buf[b][:, :, 0:D], ALU.add))
                    norm.dve(dve, link, n, y[:, :, :], sca.buf[b][:, :, :])
                    v.tensor_copy(y[:, 0, 0:1], sca.buf[b][:, 0, 0:1]).then_inc(finished, 1)
                    dve.wait_ge(finished, n + 1)
            turns(dve, PAIRS, body, [link])


def isolated_nodes(nc, c, x, out):
    R = 125
    CG = 8
    PER = N // R
    n_turns = PER // CG // 2
    with Scope(nc, "iso_") as s:
        xb = [s.sb(f"x{b}", [R, CG, D]) for b in range(2)]
        o = [s.sb(f"out{b}", [R, CG, D]) for b in range(2)]
        xn = s.sb("normed", [R, CG, D])
        low, high_, sm, vr, rt, r2 = (s.sb(n, [R, CG]) for n in ("low", "high", "sum", "var", "root", "root2"))
        sq = s.sb("sq", [R, CG, D])
        y = s.sb("y", [R, CG, D])
        x1 = s.sb("first", [R, CG, D])
        xT = s.sb("xT", [P, 4 * R])
        ones = s.sb("ones", [1, R])
        pT = s.ps("pT", [P, 512])
        pR = s.ps("pR", [R, 512])
        norm = Norm(nc, s, c, CG, rows=R)
        loaded = [s.sem(f"loaded{b}") for b in range(2)]
        stored = [s.sem(f"stored{b}") for b in range(2)]
        fed, turned, evac, product, finished, linked, ready, v_in, v_out = (
            s.sem(n) for n in ("fed", "turned", "evac", "product", "finished", "linked", "ready", "v_in", "v_out"))
        block = s.block()
        xv = x.rearrange("(p t) k -> p (t k)", p=R)
        ov = out.rearrange("(p t) k -> p (t k)", p=R)

        def at(i, b):
            return bass.ds((i * 2 + b) * (CG * D), CG * D)

        @block.sync
        def _(sp):
            def body(i):
                for b in range(2):
                    wait(sp, finished, i * 2 + b - 1)
                    sp.dma_start(flat(xb[b][:, :, :]), xv[:, at(i, b)]).then_inc(loaded[b], 16)
            turns(sp, n_turns, body)

        @block.gpsimd
        def _(pool):
            def body(i):
                for b in range(2):
                    pool.wait_ge(finished, i * 2 + b + 1)
                    pool.dma_start(ov[:, at(i, b)], flat(o[b][:, :, :])).then_inc(stored[b], 16)
            turns(pool, n_turns, body)
            for b in range(2):
                pool.wait_ge(stored[b], 16 * n_turns)

        @block.tensor
        def _(pe):
            def body(i):
                for b in range(2):
                    n = i * 2 + b
                    for j, (src, w, bias) in enumerate(((xn, c.wiso, c.biso), (x1, c.w1d, c.b1x))):
                        pe.wait_ge(fed, 2 * n + j + 1)
                        for k in range(CG // 2):
                            mm = nc.tensor.transpose(pT[:, k * R:(k + 1) * R],
                                                     src[:, 2 * k:2 * k + 2, :].rearrange("p a b -> p (a b)"), c.ident[0:R, 0:R])
                        mm.then_inc(turned, 1)
                        pe.wait_ge(evac, 2 * n + j + 1)
                        for k in range(CG // 2):
                            nc.tensor.matmul(pR[:, k * P:(k + 1) * P], xT[:, k * R:(k + 1) * R], w[:, :], start=True, stop=False)
                            mm = nc.tensor.matmul(pR[:, k * P:(k + 1) * P], ones[:, :], flat(bias[:, :, :]), start=False, stop=True)
                        mm.then_inc(product, 1)
            pe.wait_ge(ready, 1)
            turns(pe, n_turns, body)

        @block.scalar
        def _(act):
            def body(i):
                for b in range(2):
                    n = i * 2 + b
                    for j in range(2):
                        act.wait_ge(turned, 2 * n + j + 1)
                        nc.scalar.activation(xT[:, :], pT[:, 0:4 * R], ACT.Copy).then_inc(evac, 1)
                        if j == 0:
                            norm.root(act, n)
                    for j in range(3):
                        act.wait_ge(v_in, 3 * n + j + 1)
                        nc.scalar.activation(rt[:, :], vr[:, :], ACT.Sqrt, bias=c.eps[0:R, :]).then_inc(v_out, 1)
            turns(act, n_turns, body)

        @block.vector
        def _(dve):
            link = Link(dve, linked)
            v = nc.vector
            v.memset(ones[:, :], 1.0).then_inc(ready, 1)

            def body(i):
                for b in range(2):
                    n = i * 2 + b
                    dve.wait_ge(loaded[b], i * 16 + 16)
                    link(v.tensor_reduce(low[:, :], xb[b][:, :, :], AX.X, ALU.min))
                    link(v.tensor_reduce(high_[:, :], xb[b][:, :, :], AX.X, ALU.max))
                    link(v.scalar_tensor_tensor(out=high_[:, :], in0=high_[:, :], scalar=EPS, in1=low[:, :],
                                                op0=ALU.add, op1=ALU.subtract))
                    link(v.reciprocal(high_[:, :], high_[:, :]))
                    link(v.tensor_tensor(xn[:, :, :], xb[b][:, :, :], bc(low[:, :], D), ALU.subtract))
                    v.tensor_tensor(xn[:, :, :], xn[:, :, :], bc(high_[:, :], D), ALU.mult).then_inc(fed, 1)
                    dve.wait_ge(product, 2 * n + 1)
                    rows = pR[:, :].rearrange("p (t k) -> p t k", k=D)
                    link(v.tensor_tensor(y[:, :, :], rows, xb[b][:, :, :], ALU.add))
                    norm.dve(dve, link, n, y[:, :, :], x1[:, :, :])
                    v.tensor_copy(sq[:, 0, 0:1], x1[:, 0, 0:1]).then_inc(fed, 1)
                    dve.wait_ge(product, 2 * n + 2)
                    dve.wait_ge(fed, 2 * n + 2)
                    link(v.scalar_tensor_tensor(out=y[:, :, :], in0=rows, scalar=0.0, in1=x1[:, :, :], op0=ALU.max, op1=ALU.add))
                    link(v.tensor_reduce(sm[:, :], y[:, :, :], AX.X, ALU.add))
                    link(v.tensor_scalar(sm[:, :], sm[:, :], 1.0 / D, None, ALU.mult))
                    link(v.tensor_tensor(y[:, :, :], y[:, :, :], bc(sm[:, :], D), ALU.subtract))
                    link(v.tensor_tensor(sq[:, :, :], y[:, :, :], y[:, :, :], ALU.mult))
                    link(v.tensor_reduce(vr[:, :], sq[:, :, :], AX.X, ALU.add))
                    v.tensor_scalar(vr[:, :], vr[:, :], 1.0 / D, None, ALU.mult).then_inc(v_in, 1)
                    link(v.memset(high_[:, :], 1.0))
                    for j in range(3):
                        dve.wait_ge(v_out, 3 * n + j + 1)
                        link(v.reciprocal(r2[:, :], rt[:, :]))
                        link(v.tensor_tensor(high_[:, :], high_[:, :], r2[:, :], ALU.mult))
                        if j < 2:
                            link(v.tensor_tensor(vr[:, :], vr[:, :], r2[:, :], ALU.mult))
                            v.tensor_tensor(vr[:, :], vr[:, :], r2[:, :], ALU.mult).then_inc(v_in, 1)
                    wait(dve, stored[b], i * 16)
                    v.tensor_tensor(o[b][:, :, :], y[:, :, :], bc(high_[:, :], D), ALU.mult).then_inc(finished, 1)
                    dve.wait_ge(finished, n + 1)
            turns(dve, n_turns, body, [link])


def index_arrays(nc, c):
    with Scope(nc, "idx_") as s:
        ta, tb = s.sb("ta", [P, NT]), s.sb("tb", [P, NT])
        linked, vin, vout = s.sem("linked"), s.sem("vin"), s.sem("vout")
        block = s.block()
        FAR = float(4 * N)

        @block.scalar
        def _(act):
            for k, t in enumerate((c.inv_out, c.inv_in)):
                act.wait_ge(vin, k + 1)
                nc.scalar.activation(t[:, :], t[:, :], ACT.Sqrt).then_inc(vout, 1)

        @block.vector
        def _(dve):
            link = Link(dve, linked)
            v = nc.vector
            af, bf = c.rec_a[:, :, :].bitcast(FP32), c.rec_b[:, :, :].bitcast(FP32)
            for name, rec, col in (("b1", c.rec_b, 1), ("b2", c.rec_b, 2), ("b3", c.rec_b, 3), ("a2", c.rec_a, 2),
                                   ("a3", c.rec_a, 3), ("a4", c.rec_a, 4), ("a5", c.rec_a, 5), ("a6", c.rec_a, 6)):
                link(v.tensor_copy(c.idx[name][:, :], rec[:, :, col]))
            link(v.tensor_scalar(ta[:, :], c.last_a[:, :], -1.0, -FAR, ALU.add, ALU.mult))
            link(v.tensor_tensor(tb[:, :], af[:, :, 0], ta[:, :], ALU.add))
            link(v.tensor_copy(c.out_a[:, :], tb[:, :]))
            link(v.tensor_scalar(ta[:, :], c.last_b[:, :], -1.0, -FAR, ALU.add, ALU.mult))
            link(v.tensor_tensor(tb[:, :], bf[:, :, 0], ta[:, :], ALU.add))
            link(v.scalar_tensor_tensor(out=tb[:, :], in0=bf[:, :, 4], scalar=FAR, in1=tb[:, :], op0=ALU.mult, op1=ALU.add))
            link(v.tensor_copy(c.out_b[:, :], tb[:, :]))
            for k, (t, src) in enumerate(((c.inv_out, af[:, :, 7]), (c.inv_in, bf[:, :, 5]))):
                v.tensor_scalar(t[:, :], src, 1.0, None, ALU.max).then_inc(vin, 1)
                dve.wait_ge(vout, k + 1)
                link(v.reciprocal(t[:, :], t[:, :]))


def hop_norms(nc, c, dis):
    with Scope(nc, "nrm_") as s:
        linked = s.sem("linked")
        block = s.block()

        @block.vector
        def _(dve):
            Link(dve, linked)(nc.vector.tensor_tensor(c.norm[:, :], c.rec_a[:, :, :].bitcast(FP32)[:, :, 1], dis[:, :, 0], ALU.mult))


def zero_rows(nc, tables):
    with Scope(nc, "zr_") as s:
        z = s.sb("z", [1, D])
        a, b = s.sem("made"), s.sem("stored")
        block = s.block()

        @block.vector
        def _(dve):
            nc.vector.memset(z[:, :], 0.0).then_inc(a, 1)

        @block.sync
        def _(sp):
            sp.wait_ge(a, 1)
            for t in tables:
                sp.dma_start(t[ZERO:ZERO + 1, :], z[:, :]).then_inc(b, 16)
            sp.wait_ge(b, 16 * len(tables))


class Bag:
    pass


def build(nc, a, out):
    def dram(name, shape):
        return nc.dram_tensor(name, shape, FP32).ap()

    x = a["x"]
    entries = dram("node_entries", [P * LO, 4])
    by_dst = dram("by_dst", [SLOTS, 2 * D + META])
    by_src = dram("by_src", [SLOTS, META])
    v_a, v_b, w_a, w_b, same_a, same_b, far_a, far_b, deg_row = (
        dram(n, [SLOTS + 2 if n[0] == "v" else SLOTS]) for n in
        ("v_a", "v_b", "w_a", "w_b", "same_a", "same_b", "far_a", "far_b", "deg_row"))
    dis_t = dram("dis_t", [SLOTS + 1, 4])
    d_t = dram("d_t", [SLOTS + 1, D])
    stash = dram("stash", [SLOTS, 4 * D])
    x1_t = dram("x1_t", [2 * SLOTS, D])
    t0_s = dram("t0_s", [SLOTS, D])
    p_t = [dram(f"p_t{k}", [SLOTS + 1, D]) for k in range(2)]
    x2_t = dram("x2_t", [3 * SLOTS, D])
    x3_t = dram("x3_t", [2 * SLOTS, D])
    with Scope(nc) as s:
        c = Bag()
        c.ident = s.sb("ident", [P, P])
        c.eps = s.sb("eps", [P, 1])
        c.rec_a, c.rec_b = s.sb("rec_a", [P, NT, META], I32), s.sb("rec_b", [P, NT, META], I32)
        with Scope(nc) as r:
            c.ones, c.tri = r.sb("ones", [P, P]), r.sb("tri", [P, P])
            c.rank_mask = r.sb("rank_mask", [P, BLK * P])
            c.iota16, c.iota_part = r.sb("iota16", [P, LO], F16), r.sb("iota_part", [P, 1])
            c.ident16, c.ones16, c.w128_16 = r.sb("ident16", [P, P], F16), r.sb("ones16", [P, P], F16), r.sb("w128_16", [P, P], F16)
            c.src, c.dst, c.ew = r.sb("src", [P, NT], I32), r.sb("dst", [P, NT], I32), r.sb("ew", [P, NT])
            c.key_s, c.key_d = r.sb("key_s", [P, NT, 3]), r.sb("key_d", [P, NT, 3])
            c.node_s, c.node_d = r.sb("node_s", [P, NT], I32), r.sb("node_d", [P, NT], I32)
            c.safe_s, c.safe_d = r.sb("safe_s", [P, NT], I32), r.sb("safe_d", [P, NT], I32)
            c.rank_s, c.rank_d = r.sb("rank_s", [P, NT]), r.sb("rank_d", [P, NT])
            c.count_s, c.count_d = r.sb("count_s", [P, LO]), r.sb("count_d", [P, LO])
            c.seg_s, c.seg_d = r.sb("seg_s", [P, NT, 4]), r.sb("seg_d", [P, NT, 4])
            c.row_a, c.row_b = r.sb("row_a", [P, NT], I32), r.sb("row_b", [P, NT], I32)
            constants(nc, c)
            load_edges(nc, c, a["src"], a["dst"], a["edge_weight"])
            rank_edges(nc, c, c.key_s, c.rank_s, c.count_s, "rank_s_")
            rank_edges(nc, c, c.key_d, c.rank_d, c.count_d, "rank_d_")
            node_table(nc, c, entries)
            gather_small(nc, c, [(entries, c.node_s, c.seg_s), (entries, c.node_d, c.seg_d)], 4, "segs_")
            edge_records(nc, c)
            sort_edges(nc, c, x, by_dst, by_src)
        c.w0, c.b0, c.m0 = s.sb("w0", [P, 8, D]), s.sb("b0", [1, 8, D]), s.sb("m0", [P, D])
        c.wiso, c.biso = s.sb("wiso", [P, P]), s.sb("biso", [1, 2, D])
        c.w1d, c.b1x, c.wp = s.sb("w1d", [P, P]), s.sb("b1x", [1, 2, D]), s.sb("wp", [D, 5, 2 * D])
        c.w31, c.w32, c.b31, c.b32 = s.sb("w31", [P, P]), s.sb("w32", [P, D]), s.sb("b31", [P, 1]), s.sb("b32", [P, D])
        c.last_a, c.last_b = s.sb("last_a", [P, NT]), s.sb("last_b", [P, NT])
        c.neg_dis, c.norm = s.sb("neg_dis", [P, NT]), s.sb("norm", [P, NT])
        c.inv_out, c.inv_in = s.sb("inv_out", [P, NT]), s.sb("inv_in", [P, NT])
        c.out_a, c.out_b = s.sb("out_a", [P, NT], I32), s.sb("out_b", [P, NT], I32)
        c.idx = {n: s.sb("idx_" + n, [P, NT], I32) for n in ("b1", "b2", "b3", "a2", "a3", "a4", "a5", "a6")}
        load_weights(nc, c, a)
        isolated_nodes(nc, c, x, out)
        order_marks(nc, c, by_dst, c.rec_b, v_b, same_b, far_b, c.last_b, "mark_b_", w_b)
        order_marks(nc, c, by_src, c.rec_a, v_a, same_a, far_a, c.last_a, "mark_a_", w_a)
        source_scale(nc, c, same_a, w_a, deg_row, dis_t)
        index_arrays(nc, c)
        zero_rows(nc, p_t)
        with Scope(nc) as r:
            dis = r.sb("dis", [P, NT, 4])
            gather_small(nc, c, [(dis_t, c.idx["a4"], dis)], 4, "disg_")
            hop_norms(nc, c, dis)
        attention_sums(nc, c, by_dst, same_b, stash, d_t, x1_t)
        attention_out(nc, c, same_b, stash, d_t, x1_t)
        with Scope(nc) as r:
            c.acc, c.t_even, c.t_odd = (r.sb(n, [P, NT, D]) for n in ("acc", "t_even", "t_odd"))
            chebyshev_start(nc, c, x1_t, t0_s, x2_t)
            for k in range(5):
                chebyshev_hop(nc, c, k, same_a, p_t[(k + 1) % 2], p_t[k % 2])
            chebyshev_end(nc, c, t0_s, x2_t, x3_t)
        light_layer(nc, c, same_b, x2_t, x3_t, out)
        edge_layer(nc, c, far_a, x3_t, out)


_INS = ['x', 'src', 'dst', 'edge_weight', 'L0_gnn_W1', 'L0_gnn_b1', 'L0_gnn_W2', 'L0_gnn_b2', 'L0_gnn_Wres', 'L0_gnn_bres',
        'L0_gnn_m', 'L1_gnn_W', 'L1_gnn_b', 'L3_gnn_W1', 'L3_gnn_b1', 'L3_gnn_W2', 'L3_gnn_b2']


def kernel(**inputs):
    import numpy as _np
    import concourse.bacc as _bacc
    from concourse import mybir as _mybir
    from concourse.bass_utils import run_bass_kernel_spmd as _run

    nc = _bacc.Bacc("TRN2", target_bir_lowering=False, num_devices=1)
    arrays, args = {}, {}
    for name in _INS:
        a = _np.ascontiguousarray(inputs[name])
        arrays[f"in_{name}_dram"] = a
        args[name] = nc.dram_tensor(f"in_{name}_dram", a.shape, _mybir.dt.from_np(a.dtype), kind="ExternalInput").ap()
    out = nc.dram_tensor("out_0_dram", (N, D), _mybir.dt.float32, kind="ExternalOutput").ap()
    build(nc, args, out)
    r = _run(nc, [arrays], core_ids=[0])
    return r.results[0]["out_0_dram"]
```

```python
import concourse.bass as bass
from concourse import mybir
from contextlib import ExitStack

FP32 = mybir.dt.float32
I32 = mybir.dt.int32
U32 = mybir.dt.uint32
F16 = mybir.dt.float16
BF16 = mybir.dt.bfloat16
ALU = mybir.AluOpType
ACT = mybir.ActivationFunctionType
AX = mybir.AxisListType

P = 128
D = 64
N = 100000
E = 25000
NT = -(-E // P)
SLOTS = NT * P
CT = 7
NCH = NT // CT
NONE = N
LO = 784
BLK = 4
NBLK = NT // BLK
META = 8


class Link:

    def __init__(self, eng, sem):
        self.eng, self.sem, self.base, self.k = eng, sem, 0, 0

    def __call__(self, ins):
        self.k += 1
        ins.then_inc(self.sem, 1)
        self.eng.wait_ge(self.sem, self.base + self.k)
        return ins

    def go(self, ins):
        self.k += 1
        ins.then_inc(self.sem, 1)


def turns(eng, count, body, links=()):
    starts = [ln.base + ln.k for ln in links]
    body(0)
    per = [ln.base + ln.k - s for ln, s in zip(links, starts)]
    if count > 1:
        with eng.Fori(1, count) as i:
            for ln, s, n in zip(links, starts, per):
                ln.base, ln.k = i * n + s, 0
            body(i)
    for ln, s, n in zip(links, starts, per):
        ln.base, ln.k = s + n * count, 0


def staged(eng, count, stages, links=()):
    lag = max(d for d, _ in stages)
    first = 2 * ((lag + 3) // 2)

    def step(t):
        for d, fn in stages:
            if 0 <= t - d < count:
                fn(t - d, (t - d) // 2, (t - d) % 2)

    for t in range(first - 2):
        step(t)
    before = [ln.base + ln.k for ln in links]
    step(first - 2)
    step(first - 1)
    start = [ln.base + ln.k for ln in links]
    per = [z - a for a, z in zip(before, start)]
    with eng.Fori(first // 2, count // 2) as i:
        for ln, s, n in zip(links, start, per):
            ln.base, ln.k = i * n + (s - first // 2 * n), 0
        for bb in range(2):
            for d, fn in stages:
                b = (bb - d) % 2
                fn(i * 2 + (bb - d), i + (bb - d - b) // 2, b)
    for ln, s, n in zip(links, start, per):
        ln.base, ln.k = s + n * ((count - first) // 2), 0
    for t in range(count, count + lag):
        step(t)


def wait(eng, sem, value):
    if isinstance(value, int) and value <= 0:
        return
    eng.wait_ge(sem, value)


def pass_gate(nc, pool, gate, gates, value):
    pool.wait_ge(gates, value)
    nc.gpsimd.tensor_tensor(gate[:, 0:1], gate[:, 1:2], gate[:, 1:2], ALU.add).then_inc(gates, 1)


class Scope(ExitStack):
    def __init__(self, nc, tag=""):
        super().__init__()
        self.nc, self.tag, self.sems = nc, tag, []
        self.callback(self.clear)

    def sb(self, name, shape, dt=FP32):
        return self.enter_context(self.nc.sbuf_tensor(self.tag + name, shape, dt))

    def ps(self, name, shape, dt=FP32):
        return self.enter_context(self.nc.psum_tensor(self.tag + name, shape, dt))

    def sem(self, name):
        self.sems.append(self.nc.alloc_semaphore(self.tag + name))
        return self.sems[-1]

    def clear(self):
        if self.sems:
            self.nc.clear_and_free_semaphores(self.sems)
            self.nc.all_engine_barrier()

    def block(self):
        return self.enter_context(self.nc.Block())


def constants(nc, c):
    with Scope(nc, "const_") as s:
        io = s.sb("iota_i", [P, LO], I32)
        pi = s.sb("part_i", [P, 1], I32)
        made = s.sem("made")
        piped = s.sem("linked")
        block = s.block()

        @block.gpsimd
        def _(pool):
            link = Link(pool, piped)
            link(pool.iota(io[:, :], pattern=[[1, LO]], base=0, channel_multiplier=0))
            link(pool.iota(pi[:, :], pattern=[[0, 1]], base=0, channel_multiplier=1))
            for t in (c.ident, c.ones, c.tri, c.rank_mask):
                link(pool.memset(t[:, :], 1.0))
            link(pool.affine_select(out=c.ident[:, :], in_=c.ident[:, :], compare_op=ALU.is_equal, fill=0.0,
                                    base=0, pattern=[[-1, P]], channel_multiplier=1))
            link(pool.affine_select(out=c.tri[:, :], in_=c.tri[:, :], compare_op=ALU.is_gt, fill=0.0,
                                    base=0, pattern=[[1, P]], channel_multiplier=-1))
            own = c.rank_mask[:, (BLK - 1) * P:BLK * P]
            link(pool.affine_select(out=own, in_=own, compare_op=ALU.is_gt, fill=0.0,
                                    base=0, pattern=[[-1, P]], channel_multiplier=1))
            pool.nop().then_inc(made, 1)

        @block.vector
        def _(dve):
            dve.wait_ge(made, 1)
            link = Link(dve, s.sem("dve_linked"))
            link(nc.vector.tensor_copy(c.iota16[:, :], io[:, :]))
            link(nc.vector.tensor_copy(c.iota_part[:, :], pi[:, :]))
            link(nc.vector.tensor_copy(c.ident16[:, :], c.ident[:, :]))
            link(nc.vector.memset(c.ones16[:, :], 1.0))
            link(nc.vector.memset(c.w128_16[:, :], 128.0))


def load_edges(nc, c, src, dst, ew):
    full = E // NT
    rest = E - full * NT
    with Scope(nc, "edges_") as s:
        arrived = s.sem("arrived")
        cleared = s.sem("cleared")
        linked = s.sem("linked")
        hi_i = s.sb("hi_i", [P, NT], I32)
        lo_i = s.sb("lo_i", [P, NT], I32)
        block = s.block()

        @block.sync
        def _(sp):
            sp.wait_ge(cleared, 3)
            for a, t in ((src, c.src), (dst, c.dst), (ew, c.ew)):
                sp.dma_start(t[0:full, :], a[0:full * NT].rearrange("(p t) -> p t", t=NT)).then_inc(arrived, 16)
                sp.dma_start(t[full:full + 1, 0:rest], a[full * NT:E].rearrange("(a t) -> a t", a=1)).then_inc(arrived, 16)

        @block.vector
        def _(dve):
            link = Link(dve, linked)
            nc.vector.memset(c.src[:, :], NONE).then_inc(cleared, 1)
            nc.vector.memset(c.dst[:, :], NONE).then_inc(cleared, 1)
            nc.vector.memset(c.ew[:, :], 0.0).then_inc(cleared, 1)
            dve.wait_ge(cleared, 3)
            dve.wait_ge(arrived, 96)
            for v, key, u, g in ((c.src, c.key_s, c.node_s, c.safe_s), (c.dst, c.key_d, c.node_d, c.safe_d)):
                link(nc.vector.tensor_single_scalar(hi_i[:, :], v[:, :], 127, ALU.bitwise_and))
                link(nc.vector.tensor_single_scalar(lo_i[:, :], v[:, :], 7, ALU.logical_shift_right))
                link(nc.vector.tensor_copy(key[:, :, 0], hi_i[:, :]))
                link(nc.vector.tensor_copy(key[:, :, 1], lo_i[:, :]))
                link(nc.vector.tensor_copy(key[:, :, 2], v[:, :]))
                link(nc.vector.scalar_tensor_tensor(out=u[:, :], in0=key[:, :, 0], scalar=float(LO), in1=key[:, :, 1],
                                                    op0=ALU.mult, op1=ALU.add))
                link(nc.vector.tensor_scalar(g[:, :], key[:, :, 2], float(N - 1), None, ALU.min))


def rank_edges(nc, c, key, rank, count, tag):
    H = 512
    with Scope(nc, tag) as s:
        kc = s.sb("keys", [P, BLK, 3])
        oh_hi = s.sb("onehot_hi", [P, BLK, P], BF16)
        oh_lo = s.sb("onehot_lo", [P, BLK, LO], BF16)
        oh_hiT = s.sb("onehot_hiT", [P, BLK * P], BF16)
        diag_hi = s.sb("diag_hi", [P, BLK, P], F16)
        diag_lo = s.sb("diag_lo", [P, BLK, P], F16)
        tab_h = s.sb("count_high", [P, LO], BF16)
        tab_l = s.sb("count_low", [P, LO], BF16)
        near = s.sb("near", [P, BLK])
        far = s.sb("far", [P, BLK])
        junk = s.sb("junk", [P, LO])
        run = s.ps("running", [P, 1024])
        got = [s.ps(f"got{k}", [P, 1024]) for k in range(2)]
        row_hi = s.ps("row_hi", [P, 512])
        row_v = s.ps("row_v", [P, 512])
        keys_in = s.sem("keys_in")
        diags = s.sem("diags")
        rows = s.sem("rows")
        rows_used = s.sem("rows_used")
        hots = s.sem("hots")
        queried = s.sem("queried")
        extracted = s.sem("extracted")
        counted = s.sem("counted")
        high = s.sem("high")
        low = s.sem("low")
        dve_l = s.sem("dve_linked")
        cleared = s.sem("cleared")
        block = s.block()

        @block.scalar
        def _(act):
            def body(i):
                act.wait_ge(keys_in, i + 1)
                wait(act, rows, i)
                for k in range(BLK):
                    nc.scalar.activation(diag_hi[:, k, :], c.ident16[:, :], ACT.Copy, scale=kc[:, k, 0:1])
                    last = nc.scalar.activation(diag_lo[:, k, :], c.ident16[:, :], ACT.Copy, scale=kc[:, k, 1:2])
                last.then_inc(diags, 1)
                act.wait_ge(counted, i + 1)
                nc.scalar.activation(tab_h[:, :], run[:, 0:LO], ACT.Copy).then_inc(high, 1)
            turns(act, NBLK, body)

        @block.tensor
        def _(pe):
            pe.wait_ge(cleared, 1)
            nc.tensor.matmul(run[:, 0:H], tab_h[:, 0:P], tab_h[:, 0:H], start=True, stop=False, skip_group_check=True)
            nc.tensor.matmul(run[:, H:LO], tab_h[:, 0:P], tab_h[:, H:LO], start=True, stop=False, skip_group_check=True)

            def body(i):
                pe.wait_ge(diags, i + 1)
                wait(pe, rows_used, i)
                nc.tensor.matmul(row_hi[:, :], c.ones16[:, :], diag_hi[:, :, :].rearrange("p a b -> p (a b)"), start=True, stop=True)
                nc.tensor.matmul(row_v[:, :], c.ones16[:, :], diag_hi[:, :, :].rearrange("p a b -> p (a b)"), start=True, stop=False)
                nc.tensor.matmul(row_v[:, :], c.w128_16[:, :], diag_lo[:, :, :].rearrange("p a b -> p (a b)"), start=False, stop=True).then_inc(rows, 1)
                pe.wait_ge(hots, i + 1)
                wait(pe, low, i)
                for k in range(BLK):
                    n = i * BLK + k
                    wait(pe, extracted, n - 1)
                    hot = oh_hiT[:, k * P:(k + 1) * P]
                    for a, b in ((0, H), (H, LO)):
                        nc.tensor.matmul(got[k % 2][:, a:b], hot, tab_h[:, a:b], start=True, stop=False)
                        last = nc.tensor.matmul(got[k % 2][:, a:b], hot, tab_l[:, a:b], start=False, stop=True)
                    last.then_inc(queried, 1)
                for k in range(BLK):
                    for a, b in ((0, H), (H, LO)):
                        last = nc.tensor.matmul(run[:, a:b], oh_hi[:, k, :], oh_lo[:, k, a:b], start=False, stop=False,
                                                skip_group_check=True)
                last.then_inc(counted, 1)
            turns(pe, NBLK, body)

        @block.vector
        def _(dve):
            link = Link(dve, dve_l)
            link(nc.vector.memset(tab_l[:, :], 0.0))
            nc.vector.memset(tab_h[:, :], 0.0).then_inc(cleared, 1)

            def body(i):
                wait(dve, diags, i)
                link(nc.vector.tensor_scalar(kc[:, :, :].rearrange("p a b -> p (a b)"),
                                             key[:, :, :].rearrange("p a b -> p (a b)")[:, bass.ds(i * (3 * BLK), 3 * BLK)],
                                             1.0, None, ALU.mult))
                nc.vector.tensor_scalar(near[:, :], kc[:, :, 0], 0.0, None, ALU.mult).then_inc(keys_in, 1)
                dve.wait_ge(keys_in, i + 1)
                wait(dve, counted, i)
                link(nc.vector.tensor_tensor(oh_hi[:, :, :], c.iota16[:, 0:P].unsqueeze(1).to_broadcast([P, BLK, P]),
                                             kc[:, :, 0:1].to_broadcast([P, BLK, P]), ALU.is_equal))
                for k in range(BLK):
                    link(nc.vector.tensor_scalar(oh_lo[:, k, :], c.iota16[:, :], kc[:, k, 1:2], None, ALU.is_equal))
                dve.wait_ge(rows, i + 1)
                link(nc.vector.tensor_scalar(oh_hiT[:, :], row_hi[:, :], c.iota_part[:, :], None, ALU.is_equal))
                for k in range(BLK):
                    n = (k + 1) * P
                    last = link(nc.vector.scalar_tensor_tensor(out=junk[:, 0:n], in0=row_v[:, 0:n], scalar=kc[:, k, 2:3],
                                                        in1=c.rank_mask[:, BLK * P - n:BLK * P], op0=ALU.is_equal,
                                                        op1=ALU.mult, accum_out=near[:, k:k + 1]))
                nc.vector.tensor_scalar(junk[:, 0:1], near[:, 0:1], 0.0, None, ALU.mult).then_inc(rows_used, 1)
                dve.wait_ge(rows_used, i + 1)
                nc.vector.tensor_scalar(junk[:, 0:1], near[:, 0:1], 0.0, None, ALU.mult).then_inc(hots, 1)
                dve.wait_ge(hots, i + 1)
                for k in range(BLK):
                    n = i * BLK + k
                    dve.wait_ge(queried, n + 1)
                    nc.vector.tensor_tensor_reduce(out=junk[:, :], in0=got[k % 2][:, 0:LO], in1=oh_lo[:, k, :], scale=1.0,
                                                   scalar=0.0, op0=ALU.mult, op1=ALU.add,
                                                   accum_out=far[:, k:k + 1]).then_inc(extracted, 1)
                    dve.wait_ge(extracted, n + 1)
                link(nc.vector.tensor_tensor(rank[:, bass.ds(i * BLK, BLK)], near[:, :], far[:, :], ALU.add))
                dve.wait_ge(high, i + 1)
                nc.vector.tensor_tensor(tab_l[:, :], run[:, 0:LO], tab_h[:, :], ALU.subtract).then_inc(low, 1)
                dve.wait_ge(low, i + 1)
            turns(dve, NBLK, body, [link])
            link(nc.vector.tensor_copy(count[:, :], run[:, 0:LO]))


def node_table(nc, c, table):
    with Scope(nc, "nodes_") as s:
        ones = s.sb("ones", [P, LO])
        incl = s.sb("inclusive", [P, LO])
        has = s.sb("has", [P, LO])
        out = s.sb("entries", [P, LO, 4])
        base = [s.ps(f"base{k}", [P, 1]) for k in range(2)]
        summed = s.sem("summed")
        based = s.sem("based")
        dve_l = s.sem("dve_linked")
        stored = s.sem("stored")
        filled = s.sem("filled")
        block = s.block()

        @block.tensor
        def _(pe):
            for k in range(2):
                pe.wait_ge(summed, k + 1)
                nc.tensor.matmul(base[k][:, :], c.tri[:, :], incl[:, LO - 1:LO], start=True, stop=True).then_inc(based, 1)

        @block.vector
        def _(dve):
            link = Link(dve, dve_l)
            link(nc.vector.memset(ones[:, :], 1.0))
            for k, cnt in enumerate((c.count_s, c.count_d)):
                nc.vector.tensor_tensor_scan(out=incl[:, :], data0=ones[:, :], data1=cnt[:, :], initial=0.0,
                                             op0=ALU.mult, op1=ALU.add).then_inc(summed, 1)
                dve.wait_ge(summed, k + 1)
                dve.wait_ge(based, k + 1)
                link(nc.vector.tensor_scalar(incl[:, :], incl[:, :], base[k][:, :], None, ALU.add))
                link(nc.vector.tensor_tensor(out[:, :, 2 * k], incl[:, :], cnt[:, :], ALU.subtract))
                link(nc.vector.tensor_scalar(has[:, :], cnt[:, :], 0.0, None, ALU.is_gt))
                link(nc.vector.tensor_tensor(out[:, :, 2 * k + 1], incl[:, :], has[:, :], ALU.mult))
            nc.vector.tensor_copy(has[:, 0:1], incl[:, 0:1]).then_inc(filled, 1)

        @block.sync
        def _(sp):
            sp.wait_ge(filled, 1)
            sp.dma_start(table.rearrange("(p a) k -> p a k", p=P), out[:, :, :]).then_inc(stored, 16)
            sp.wait_ge(stored, 16)


class SmallGather:

    def __init__(self, nc, s, job, turn=0, shared=None):
        self.nc, (self.table, self.index, self.rows, self.words) = nc, job
        if shared:
            self.slots, self.got, self.gate, self.staged, self.gathered, self.taken, self.gates = shared
        else:
            self.slots = [s.sb(f"small_stage{b}", [P, CT], I32) for b in range(2)]
            self.got = [s.sb(f"small_rows{b}", [P, CT * self.words]) for b in range(2)]
            self.gate = s.sb("small_gate", [P, 2], I32)
            self.staged, self.gathered, self.taken = (
                [s.sem(f"small_{n}{b}") for b in range(2)] for n in ("staged", "gathered", "taken"))
            self.gates = s.sem("small_gates")
        self.before = turn

    def shared(self):
        return self.slots, self.got, self.gate, self.staged, self.gathered, self.taken, self.gates

    def stage(self, n, m, b):
        wait(self.nc.sync, self.gathered[b], (m + self.before * PAIRS) * (16 * CT))
        self.nc.sync.dma_start(self.slots[b][:, :], self.index[:, bass.ds(n * CT, CT)]).then_inc(self.staged[b], 16)

    def take(self, n, m, b):
        w = CT * self.words
        self.nc.sync.wait_ge(self.gathered[b], (m + self.before * PAIRS + 1) * (16 * CT))
        self.nc.sync.dma_start(self.rows.rearrange("p t k -> p (t k)")[:, bass.ds(n * w, w)],
                               self.got[b][:, :]).then_inc(self.taken[b], 16)

    def end(self, sp):
        for b in range(2):
            sp.wait_ge(self.taken[b], (self.before + 1) * PAIRS * 16)

    def start(self, pool):
        self.nc.gpsimd.memset(self.gate[:, :], 0).then_inc(self.gates, 1)

    def gather(self, n, m, b):
        pool, w = self.nc.gpsimd, self.words
        pool.wait_ge(self.staged[b], (m + self.before * PAIRS + 1) * 16)
        wait(pool, self.taken[b], (m + self.before * PAIRS) * 16)
        pass_gate(self.nc, pool, self.gate, self.gates, n + self.before * NCH + 1)
        for k in range(CT):
            pool.indirect_dma_start(
                out=self.got[b][:, k * w:(k + 1) * w], out_offset=None, in_=self.table[:, :],
                in_offset=bass.IndirectOffsetOnAxis(ap=self.slots[b][:, k:k + 1].bitcast(U32), axis=0),
            ).then_inc(self.gathered[b], 16)


def gather_segments(nc, c, job_s, job_d, x, out, iso):
    with Scope(nc, "segs_") as s:
        first = SmallGather(nc, s, job_s)
        second = SmallGather(nc, s, job_d, turn=1, shared=first.shared())
        isolated = Isolated(nc, s, c, x, out, *iso)
        block = s.block()

        @block.sync
        def _(sp):
            for g in (first, second):
                staged(sp, NCH, [(0, g.stage), (1, g.take)])
            second.end(sp)

        @block.gpsimd
        def _(pool):
            first.start(pool)
            for g in (first, second):
                staged(pool, NCH, [(0, g.gather)])

        isolated.engines(block)




CW = CT * P
ZERO = SLOTS
PAIRS = NCH // 2
EPS = 1e-5


def bc(ap, n):
    return ap.unsqueeze(2).to_broadcast([ap.shape[0], ap.shape[1], n])


def slot_rows(nc, link, row, slot, tmp_i, tmp_p, tmp_t):
    link(nc.vector.tensor_copy(tmp_i[:, :], slot))
    link(nc.vector.tensor_single_scalar(tmp_p[:, :], tmp_i[:, :], 127, ALU.bitwise_and))
    link(nc.vector.tensor_single_scalar(tmp_t[:, :], tmp_i[:, :], 7, ALU.logical_shift_right))
    link(nc.vector.scalar_tensor_tensor(out=row, in0=tmp_p[:, :], scalar=float(NT), in1=tmp_t[:, :],
                                        op0=ALU.mult, op1=ALU.add))


def edge_records(nc, c):
    with Scope(nc, "rec_") as s:
        ti, tp, tt = (s.sb(n, [P, NT], I32) for n in ("ti", "tp", "tt"))
        pa, pb, ea_s, eb_s, ea_d, eb_d, ta, tb, own = (s.sb(n, [P, NT]) for n in
                                                      ("pa", "pb", "ea_s", "eb_s", "ea_d", "eb_d", "ta", "tb", "own"))
        linked = s.sem("linked")
        block = s.block()

        @block.vector
        def _(dve):
            link = Link(dve, linked)
            v = nc.vector

            def tt_(o, a, b, op):
                link(v.tensor_tensor(o, a, b, op))

            def ts_(o, a, x, op):
                link(v.tensor_scalar(o, a, x, None, op))

            for out, seg, col, rank in ((pa, c.seg_s, 0, c.rank_s), (pb, c.seg_d, 2, c.rank_d)):
                tt_(ta[:, :], seg[:, :, col], rank[:, :], ALU.add)
                slot_rows(nc, link, out[:, :], ta[:, :], ti, tp, tt)
            for out, seg, col in ((ea_s, c.seg_s, 1), (eb_s, c.seg_s, 3), (ea_d, c.seg_d, 1), (eb_d, c.seg_d, 3)):
                link(v.tensor_scalar(ta[:, :], seg[:, :, col], -1.0, 0.0, ALU.add, ALU.max))
                slot_rows(nc, link, out[:, :], ta[:, :], ti, tp, tt)
            link(v.tensor_copy(c.row_a[:, :], pa[:, :]))
            link(v.tensor_copy(c.row_b[:, :], pb[:, :]))

            def choose(out, has, x, y, y_add):
                ts_(ta[:, :], has, 0.0, ALU.is_gt)
                if y is None:
                    link(v.tensor_scalar(tb[:, :], x, -float(y_add), None, ALU.add))
                    tt_(tb[:, :], tb[:, :], ta[:, :], ALU.mult)
                    ts_(out, tb[:, :], float(y_add), ALU.add)
                else:
                    link(v.scalar_tensor_tensor(out=tb[:, :], in0=x, scalar=-float(y_add), in1=y,
                                                op0=ALU.add, op1=ALU.subtract))
                    tt_(tb[:, :], tb[:, :], ta[:, :], ALU.mult)
                    link(v.scalar_tensor_tensor(out=out, in0=tb[:, :], scalar=float(y_add), in1=y,
                                                op0=ALU.add, op1=ALU.add))

            b, a = c.rec_b, c.rec_a
            bf, af = b[:, :, :].bitcast(FP32), a[:, :, :].bitcast(FP32)
            link(v.tensor_copy(bf[:, :, 0], c.dst[:, :]))
            choose(b[:, :, 1], c.seg_s[:, :, 3], eb_s[:, :], None, ZERO)
            link(v.tensor_copy(b[:, :, 2], ea_s[:, :]))
            ts_(pa[:, :], pa[:, :], 2.0 * SLOTS, ALU.add)
            ts_(own[:, :], ea_d[:, :], float(SLOTS), ALU.add)
            choose(b[:, :, 3], c.seg_d[:, :, 1], own[:, :], pa[:, :], 0.0)
            ts_(bf[:, :, 4], c.seg_d[:, :, 1], 0.0, ALU.is_gt)
            tt_(bf[:, :, 5], c.seg_d[:, :, 3], c.seg_d[:, :, 2], ALU.subtract)
            link(v.memset(b[:, :, 6:8], 0))
            link(v.tensor_copy(af[:, :, 0], c.src[:, :]))
            link(v.tensor_copy(af[:, :, 1], c.ew[:, :]))
            link(v.tensor_copy(a[:, :, 2], eb_d[:, :]))
            choose(a[:, :, 3], c.seg_s[:, :, 3], eb_s[:, :], pb[:, :], SLOTS)
            choose(a[:, :, 4], c.seg_d[:, :, 1], ea_d[:, :], None, ZERO)
            link(v.tensor_copy(a[:, :, 5], eb_d[:, :]))
            choose(a[:, :, 6], c.seg_s[:, :, 3], eb_s[:, :], ea_s[:, :], SLOTS)
            tt_(af[:, :, 7], c.seg_s[:, :, 1], c.seg_s[:, :, 0], ALU.subtract)


def sort_edges(nc, c, x, by_dst, by_src, out, iso):
    NB = 4
    W = 2 * D + META
    with Scope(nc, "sort_") as s:
        st_s, st_d, st_a, st_b = ([s.sb(f"{n}{b}", [P, CT], I32) for b in range(NB)] for n in ("st_s", "st_d", "st_a", "st_b"))
        pay = [s.sb(f"pay{b}", [P, CT, W]) for b in range(NB)]
        rec = [s.sb(f"rec{b}", [P, CT, META]) for b in range(NB)]
        gate = s.sb("gate", [P, 4], I32)
        gates_g, gates_s = s.sem("gates_gather"), s.sem("gates_scatter")
        staged_g, staged_s, gathered, scattered = ([s.sem(f"{n}{b}") for b in range(NB)] for n in
                                                   ("staged_gather", "staged_scatter", "gathered", "scattered"))
        turns_n = NCH // NB
        isolated = Isolated(nc, s, c, x, out, *iso)
        block = s.block()

        @block.sync
        def _(sp):
            def body(i):
                for b in range(NB):
                    at = bass.ds((i * NB + b) * CT, CT)
                    at_rec = bass.ds((i * NB + b) * (CT * META), CT * META)
                    wait(sp, scattered[b], i * (32 * CT))
                    sp.dma_start(st_s[b][:, :], c.safe_s[:, at]).then_inc(staged_g[b], 16)
                    sp.dma_start(st_d[b][:, :], c.safe_d[:, at]).then_inc(staged_g[b], 16)
                    sp.dma_start(st_b[b][:, :], c.row_b[:, at]).then_inc(staged_s[b], 16)
                    sp.dma_start(st_a[b][:, :], c.row_a[:, at]).then_inc(staged_s[b], 16)
                    sp.dma_start(pay[b][:, :, 2 * D:W].bitcast(I32), c.rec_b[:, :, :].rearrange("p t k -> p (t k)")[:, at_rec]
                                 .rearrange("p (t k) -> p t k", k=META)).then_inc(staged_s[b], 16)
                    sp.dma_start(rec[b][:, :, :].rearrange("p t k -> p (t k)").bitcast(I32),
                                 c.rec_a[:, :, :].rearrange("p t k -> p (t k)")[:, at_rec]).then_inc(staged_s[b], 16)
            turns(sp, turns_n, body)

        @block.gpsimd
        def _(pool):
            nc.gpsimd.memset(gate[:, :], 0).then_inc(gates_g, 1)
            pool.wait_ge(gates_g, 1)
            pool.nop().then_inc(gates_s, 1)

            def scatter(b, turn, n):
                pool.wait_ge(gathered[b], turn * (32 * CT) + 32 * CT)
                pool.wait_ge(staged_s[b], turn * 64 + 64)
                pool.wait_ge(gates_s, n + 1)
                nc.gpsimd.tensor_tensor(gate[:, 2:3], gate[:, 1:2], gate[:, 1:2], ALU.add).then_inc(gates_s, 1)
                for k in range(CT):
                    for table, stage, src in ((by_dst, st_b, pay), (by_src, st_a, rec)):
                        nc.gpsimd.indirect_dma_start(
                            out=table[:, :], out_offset=bass.IndirectOffsetOnAxis(ap=stage[b][:, k:k + 1].bitcast(U32), axis=0),
                            in_=src[b][:, k, :], in_offset=None).then_inc(scattered[b], 16)

            def body(i):
                for b in range(NB):
                    n = i * NB + b
                    pool.wait_ge(staged_g[b], i * 32 + 32)
                    wait(pool, scattered[b], i * (32 * CT))
                    pool.wait_ge(gates_g, n + 1)
                    nc.gpsimd.tensor_tensor(gate[:, 0:1], gate[:, 1:2], gate[:, 1:2], ALU.add).then_inc(gates_g, 1)
                    for k in range(CT):
                        for stage, at in ((st_s, 0), (st_d, D)):
                            nc.gpsimd.indirect_dma_start(
                                out=pay[b][:, k, at:at + D], out_offset=None, in_=x[:, :],
                                in_offset=bass.IndirectOffsetOnAxis(ap=stage[b][:, k:k + 1].bitcast(U32), axis=0),
                            ).then_inc(gathered[b], 16)
                    if b:
                        scatter(b - 1, i, n - 1)
                    elif not isinstance(i, int):
                        scatter(NB - 1, i - 1, n - 1)
            turns(pool, turns_n, body)
            scatter(NB - 1, turns_n - 1, NCH - 1)
            for b in range(NB):
                pool.wait_ge(scattered[b], turns_n * 32 * CT)

        isolated.engines(block)


def order_marks(nc, c, sorted_rows, rec, vrow, same_row, far_row, last, tag, val_row=None):
    T0, T1 = P, NT - P
    with Scope(nc, tag) as s:
        v = s.sb("v", [P, NT])
        w = s.sb("w", [P, NT])
        vT = [s.sb("vT0", [T0, P]), s.sb("vT1", [T1, P])]
        wT = [s.sb("wT0", [T0, P]), s.sb("wT1", [T1, P])]
        pv = [s.sb("pv0", [T0, P]), s.sb("pv1", [T1, P])]
        nx = [s.sb("nx0", [T0, P]), s.sb("nx1", [T1, P])]
        fl = [s.sb("fl0", [T0, P]), s.sb("fl1", [T1, P])]
        ng = [s.sb("ng0", [T0, P]), s.sb("ng1", [T1, P])]
        edge = s.sb("edge", [1, 2])
        tp = [s.ps("tp0", [T0, P]), s.ps("tp1", [T1, P])]
        wp = [s.ps("wp0", [T0, P]), s.ps("wp1", [T1, P])]
        bp = s.ps("bp", [P, NT])
        loaded, ready, turned, evac, stored, reread, marked, back, linked, kept = (
            s.sem(n) for n in ("loaded", "ready", "turned", "evac", "stored", "reread", "marked", "back", "linked", "kept"))
        cut = ((0, T0), (T0, NT))
        block = s.block()

        @block.sync
        def _(sp):
            sp.dma_start(rec[:, :, :], sorted_rows.rearrange("(p t) k -> p t k", p=P)[:, :, -META:].bitcast(I32)).then_inc(loaded, 16)
            sp.wait_ge(evac, 1)
            sp.dma_start(vrow[0:1].rearrange("(a n) -> a n", a=1), edge[0:1, 0:1]).then_inc(stored, 16)
            sp.dma_start(vrow[SLOTS + 1:SLOTS + 2].rearrange("(a n) -> a n", a=1), edge[0:1, 1:2]).then_inc(stored, 16)
            for k, (a, b) in enumerate(cut):
                sp.dma_start(vrow[1 + a * P:1 + b * P].rearrange("(t p) -> t p", p=P), vT[k][:, :]).then_inc(stored, 16)
                sp.dma_start(val_row[a * P:b * P].rearrange("(t p) -> t p", p=P), wT[k][:, :]).then_inc(stored, 16)
            sp.wait_ge(stored, 96)
            for k, (a, b) in enumerate(cut):
                sp.dma_start(pv[k][:, :], vrow[a * P:b * P].rearrange("(t p) -> t p", p=P)).then_inc(reread, 16)
                sp.dma_start(nx[k][:, :], vrow[2 + a * P:2 + b * P].rearrange("(t p) -> t p", p=P)).then_inc(reread, 16)
            sp.wait_ge(marked, 1)
            for k, (a, b) in enumerate(cut):
                sp.dma_start(same_row[a * P:b * P].rearrange("(t p) -> t p", p=P), fl[k][:, :]).then_inc(kept, 16)
                sp.dma_start(far_row[a * P:b * P].rearrange("(t p) -> t p", p=P), ng[k][:, :]).then_inc(kept, 16)
            sp.wait_ge(kept, 64)

        @block.vector
        def _(dve):
            link = Link(dve, linked)
            link(nc.vector.memset(edge[:, :], -1.0))
            dve.wait_ge(loaded, 16)
            link(nc.vector.tensor_copy(v[:, :], rec[:, :, 0].bitcast(FP32)))
            nc.vector.tensor_copy(w[:, :], rec[:, :, 1].bitcast(FP32)).then_inc(ready, 1)
            dve.wait_ge(turned, 1)
            for k in range(2):
                link(nc.vector.tensor_copy(vT[k][:, :], tp[k][:, :]))
                last_i = link(nc.vector.tensor_copy(wT[k][:, :], wp[k][:, :]))
            nc.vector.memset(edge[:, :], -1.0).then_inc(evac, 1)
            dve.wait_ge(evac, 1)
            dve.wait_ge(reread, 64)
            for k in range(2):
                link(nc.vector.tensor_tensor(fl[k][:, :], vT[k][:, :], pv[k][:, :], ALU.is_equal))
                link(nc.vector.tensor_scalar(ng[k][:, :], fl[k][:, :], -1.0, 1e30, ALU.add, ALU.mult))
                link(nc.vector.tensor_tensor(nx[k][:, :], vT[k][:, :], nx[k][:, :], ALU.not_equal))
            nc.vector.tensor_copy(pv[0][:, 0:1], nx[0][:, 0:1]).then_inc(marked, 1)
            dve.wait_ge(back, 1)
            link(nc.vector.tensor_copy(last[:, :], bp[:, :]))

        @block.tensor
        def _(pe):
            pe.wait_ge(ready, 1)
            for k, (a, b) in enumerate(cut):
                nc.tensor.transpose(tp[k][:, :], v[:, a:b], c.ident[:, :])
                mm = nc.tensor.transpose(wp[k][:, :], w[:, a:b], c.ident[:, :])
            mm.then_inc(turned, 1)
            pe.wait_ge(marked, 1)
            for k, (a, b) in enumerate(cut):
                mm = nc.tensor.transpose(bp[:, a:b], nx[k][:, :], c.ident[0:b - a, 0:b - a])
            mm.then_inc(back, 1)


def source_scale(nc, c, same_row, w_row, deg_row, dis_table):
    T0, T1 = P, NT - P
    HALF = SLOTS // 2
    with Scope(nc, "dis_") as s:
        fl = s.sb("fl", [1, HALF])
        wr = s.sb("wr", [1, HALF])
        carry = s.sb("carry", [1, 1])
        dT = [s.sb("dT0", [T0, P]), s.sb("dT1", [T1, P])]
        deg = s.sb("deg", [P, NT])
        pos = s.sb("pos", [P, NT])
        wide = s.sb("wide", [P, NT, 4])
        zero = s.sb("zero", [1, 4])
        bp = s.ps("bp", [P, NT])
        loaded, scanned, stored, reread, back, floored, rooted, filled, kept, linked = (
            s.sem(n) for n in ("loaded", "scanned", "stored", "reread", "back", "floored", "rooted", "filled", "kept", "linked"))
        cut = ((0, T0), (T0, NT))
        block = s.block()

        def row(a, h):
            return a[h * HALF:(h + 1) * HALF].rearrange("(a n) -> a n", a=1)

        @block.sync
        def _(sp):
            for h in range(2):
                wait(sp, stored, 16 * h)
                sp.dma_start(fl[:, :], row(same_row, h)).then_inc(loaded, 16)
                sp.dma_start(wr[:, :], row(w_row, h)).then_inc(loaded, 16)
                sp.wait_ge(scanned, h + 1)
                sp.dma_start(row(deg_row, h), wr[:, :]).then_inc(stored, 16)
            sp.wait_ge(stored, 32)
            for k, (a, b) in enumerate(cut):
                sp.dma_start(dT[k][:, :], deg_row[a * P:b * P].rearrange("(t p) -> t p", p=P)).then_inc(reread, 16)
            sp.wait_ge(filled, 1)
            sp.dma_start(dis_table[0:SLOTS, :].rearrange("(p t) k -> p t k", p=P), wide[:, :, :]).then_inc(kept, 16)
            sp.dma_start(dis_table[ZERO:ZERO + 1, :], zero[:, :]).then_inc(kept, 16)
            sp.wait_ge(kept, 32)

        @block.tensor
        def _(pe):
            pe.wait_ge(reread, 32)
            for k, (a, b) in enumerate(cut):
                mm = nc.tensor.transpose(bp[:, a:b], dT[k][:, :], c.ident[0:b - a, 0:b - a])
            mm.then_inc(back, 1)

        @block.scalar
        def _(act):
            act.wait_ge(floored, 1)
            nc.scalar.activation(deg[:, :], deg[:, :], ACT.Sqrt).then_inc(rooted, 1)

        @block.vector
        def _(dve):
            link = Link(dve, linked)
            link(nc.vector.memset(carry[:, :], 0.0))
            for h in range(2):
                dve.wait_ge(loaded, 32 * (h + 1))
                link(nc.vector.tensor_tensor_scan(out=wr[:, :], data0=fl[:, :], data1=wr[:, :], initial=carry[:, :],
                                                  op0=ALU.mult, op1=ALU.add))
                nc.vector.tensor_copy(carry[:, :], wr[:, HALF - 1:HALF]).then_inc(scanned, 1)
                dve.wait_ge(scanned, h + 1)
            link(nc.vector.memset(zero[:, :], 0.0))
            dve.wait_ge(back, 1)
            link(nc.vector.tensor_scalar(pos[:, :], bp[:, :], 0.0, None, ALU.is_gt))
            nc.vector.tensor_scalar(deg[:, :], bp[:, :], 1e-30, None, ALU.max).then_inc(floored, 1)
            dve.wait_ge(rooted, 1)
            link(nc.vector.reciprocal(deg[:, :], deg[:, :]))
            link(nc.vector.tensor_tensor(deg[:, :], deg[:, :], pos[:, :], ALU.mult))
            link(nc.vector.tensor_scalar(c.neg_dis[:, :], deg[:, :], -1.0, None, ALU.mult))
            nc.vector.tensor_copy(wide[:, :, :], bc(deg[:, :], 4)).then_inc(filled, 1)


class Norm:

    def __init__(self, nc, s, c, n, rows=P, tag=""):
        self.nc, self.c, self.n = nc, c, n
        self.sum = s.sb(tag + "ln_sum", [rows, n])
        self.sq = s.sb(tag + "ln_sq", [rows, n, D])
        self.std = s.sb(tag + "ln_std", [rows, n])
        self.var_ready, self.rooted = s.sem(tag + "var_ready"), s.sem(tag + "rooted")

    def dve(self, dve, link, turn, y, out):
        v = self.nc.vector
        link(v.tensor_reduce(self.sum[:, :], y, AX.X, ALU.add))
        link(v.tensor_scalar(self.sum[:, :], self.sum[:, :], 1.0 / D, None, ALU.mult))
        link(v.tensor_tensor(y, y, bc(self.sum[:, :], D), ALU.subtract))
        link(v.tensor_tensor(self.sq[:, :, :], y, y, ALU.mult))
        v.tensor_reduce(self.std[:, :], self.sq[:, :, :], AX.X, ALU.add).then_inc(self.var_ready, 1)
        dve.wait_ge(self.rooted, turn + 1)
        link(v.reciprocal(self.std[:, :], self.std[:, :]))
        link(v.tensor_tensor(out, y, bc(self.std[:, :], D), ALU.mult))

    def root(self, act, turn):
        act.wait_ge(self.var_ready, turn + 1)
        self.nc.scalar.activation(self.std[:, :], self.std[:, :], ACT.Sqrt, bias=self.c.eps[0:self.std.shape[0], :],
                                  scale=1.0 / D).then_inc(self.rooted, 1)


def chunk_of(table, first_row, n, words):
    t = table[first_row:first_row + SLOTS, :].rearrange("(p t) k -> p (t k)", p=P)
    return t[:, bass.ds(n * (CT * words), CT * words)]


def flag_chunk(row, n, parts=P):
    return row[bass.ds(n * CW, CW)].rearrange("(a n) -> a n", a=1).to_broadcast([parts, CW])


def flat(t):
    return t.rearrange("p t k -> p (t k)")


def pieces():
    return ((0, 512), (512, CW))


def turn_64(nc, out, rows, ident, waits):
    if waits:
        return nc.tensor.matmul(out, rows, ident[:, :], start=True, stop=True)
    return nc.tensor.transpose(out, rows, ident[:, :])


class Gather:

    def __init__(self, nc, s, jobs, width):
        self.nc, self.jobs = nc, jobs
        self.buf = [s.sb(f"gathered_rows{b}", [P, CT, width]) for b in range(2)]
        self.stage = [[s.sb(f"stage{j}_{b}", [P, CT], I32) for b in range(2)] for j in range(len(jobs))]
        self.gate = s.sb("gate", [P, 2], I32)
        self.gates = s.sem("gates")
        self.staged = [s.sem(f"staged{b}") for b in range(2)]
        self.done = [s.sem(f"gathered{b}") for b in range(2)]
        self.per = 16 * CT * len(jobs)

    def sp(self, sp, n, m, b):
        wait(sp, self.done[b], m * self.per)
        for j, job in enumerate(self.jobs):
            sp.dma_start(self.stage[j][b][:, :], job[1][:, bass.ds(n * CT, CT)]).then_inc(self.staged[b], 16)

    def start(self, pool):
        self.nc.gpsimd.memset(self.gate[:, :], 0).then_inc(self.gates, 1)

    def pool(self, pool, n, m, b):
        pool.wait_ge(self.staged[b], (m + 1) * (16 * len(self.jobs)))
        pass_gate(self.nc, pool, self.gate, self.gates, n + 1)
        for j, (table, _, at, words) in enumerate(self.jobs):
            for k in range(CT):
                self.nc.gpsimd.indirect_dma_start(
                    out=self.buf[b][:, k, at:at + words], out_offset=None, in_=table[:, :],
                    in_offset=bass.IndirectOffsetOnAxis(ap=self.stage[j][b][:, k:k + 1].bitcast(U32), axis=0),
                ).then_inc(self.done[b], 16)

    def wait(self, eng, m, b):
        eng.wait_ge(self.done[b], (m + 1) * self.per)


def load_weights(nc, c, a):
    with Scope(nc, "w_") as s:
        w = s.sb("l1w", [D, 6, D])
        half = s.sb("half", [P, 2, D])
        brow = s.sb("brow", [1, 4, D])
        b0 = s.sb("b0", [1, 8, D])
        b0_part = [s.sb(f"b0_part{k}", [1, 8 * D], BF16) for k in range(3)]
        loaded, linked = s.sem("loaded"), s.sem("linked")
        block = s.block()
        W1, W2, WR = a["L0_gnn_W1"], a["L0_gnn_W2"], a["L0_gnn_Wres"]
        loads = []

        def row(v):
            return v.rearrange("(a n) -> a n", a=1)

        src_part = [W1, W2, None, None, W2, None, None, None]
        dst_part = [W1, W2, W1, W2, None, W2, None, WR]
        for k in range(8):
            if src_part[k] is not None:
                loads.append((c.w0[0:D, k, :], src_part[k][:, :]))
            if dst_part[k] is not None:
                loads.append((c.w0[D:P, k, :], dst_part[k][:, :]))
        b1, b2, br = row(a["L0_gnn_b1"]), row(a["L0_gnn_b2"]), row(a["L0_gnn_bres"])
        for k, v in enumerate((b1, b2, b1, b2, b2, b2, br, br)):
            loads.append((b0[0:1, k, :], v))
        m0 = row(a["L0_gnn_m"][0, :, :].rearrange("h k -> (h k)"))
        loads.append((c.m0[:, :], m0.to_broadcast([P, D])))
        for h in range(2):
            loads.append((c.wiso[h * D:(h + 1) * D, h * D:(h + 1) * D], W2[:, :]))
            loads.append((half[h * D:(h + 1) * D, 0, :], WR[:, :]))
            loads.append((c.b1x[0:1, h, :], row(a["L1_gnn_b"])))
            loads.append((brow[0:1, h, :], b2))
            loads.append((brow[0:1, 2 + h, :], br))
        loads.append((w[:, :, :], a["L1_gnn_W"].rearrange("k i o -> i k o")))
        loads.append((c.w31[:, :], a["L3_gnn_W1"][:, :]))
        loads.append((c.w32[:, :], a["L3_gnn_W2"][:, :]))
        loads.append((c.b31[:, :], a["L3_gnn_b1"].rearrange("(n a) -> n a", a=1)))
        loads.append((c.b32[:, :], row(a["L3_gnn_b2"]).to_broadcast([P, D])))

        zeroed, copied, parted = s.sem("zeroed"), s.sem("copied"), s.sem("parted")

        @block.sync
        def _(sp):
            sp.wait_ge(zeroed, 3)
            for o, v in loads:
                sp.dma_start(o, v).then_inc(loaded, 16)
            sp.wait_ge(copied, 1)
            sp.dma_start(c.w1d[D:P, D:2 * D], c.w1d[0:D, 0:D]).then_inc(loaded, 16)
            sp.wait_ge(parted, 1)
            for k in range(3):
                sp.dma_start(c.b0[k:k + 1, :], b0_part[k][:, :]).then_inc(loaded, 16)
            sp.wait_ge(loaded, 16 * (len(loads) + 4))

        @block.vector
        def _(dve):
            link = Link(dve, linked)
            v = nc.vector
            v.memset(c.w0[:, :, :], 0.0).then_inc(zeroed, 1)
            v.memset(c.wiso[:, :], 0.0).then_inc(zeroed, 1)
            v.memset(c.w1d[:, :], 0.0).then_inc(zeroed, 1)
            link(v.memset(c.eps[:, :], EPS))
            dve.wait_ge(zeroed, 3)
            dve.wait_ge(loaded, 16 * len(loads))
            link(v.tensor_scalar(c.w0[D:P, 2:4, :], c.w0[D:P, 2:4, :], 2.0, None, ALU.mult))
            link(v.tensor_scalar(b0[:, 0:4, :], b0[:, 0:4, :], 2.0, None, ALU.mult))
            for h in range(2):
                q = c.wiso[h * D:(h + 1) * D, h * D:(h + 1) * D]
                link(v.tensor_tensor(q, q, c.m0[h * D:(h + 1) * D, :], ALU.mult))
                link(v.tensor_tensor(q, q, half[h * D:(h + 1) * D, 0, :], ALU.add))
                link(v.tensor_tensor(c.biso[:, h, :], brow[:, h, :], c.m0[0:1, :], ALU.mult))
                link(v.tensor_tensor(c.biso[:, h, :], c.biso[:, h, :], brow[:, 2 + h, :], ALU.add))
            link(v.tensor_copy(c.w0[0:D, 6, :], c.wiso[0:D, 0:D]))
            link(v.tensor_copy(b0[:, 6, :], c.biso[:, 0, :]))
            link(v.memset(c.ones3[:, :], 1.0))
            row0 = flat(b0[:, :, :])
            for k in range(3):
                link(v.tensor_copy(b0_part[k][:, :], row0))
                if k < 2:
                    link(v.tensor_tensor(row0, row0, b0_part[k][:, :], ALU.subtract))
            v.tensor_copy(brow[:, 0, 0:1], b0[:, 0, 0:1]).then_inc(parted, 1)
            link(v.tensor_tensor(c.w1d[0:D, 0:D], w[:, 0, :], w[:, 2, :], ALU.subtract))
            v.tensor_tensor(c.w1d[0:D, 0:D], c.w1d[0:D, 0:D], w[:, 4, :], ALU.add).then_inc(copied, 1)
            link(v.tensor_tensor(c.wp[:, 0, D:], w[:, 1, :], w[:, 3, :], ALU.subtract))
            link(v.tensor_tensor(c.wp[:, 0, D:], c.wp[:, 0, D:], w[:, 5, :], ALU.add))
            for k, hi in ((1, 4), (2, 5)):
                link(v.tensor_tensor(c.wp[:, k, D:], w[:, k + 1, :], w[:, hi, :], ALU.subtract))
                link(v.tensor_scalar(c.wp[:, k, D:], c.wp[:, k, D:], 2.0, None, ALU.mult))
            for k in (3, 4):
                link(v.tensor_scalar(c.wp[:, k, D:], w[:, k + 1, :], 2.0, None, ALU.mult))
            for k in range(5):
                link(v.tensor_copy(c.wp[:, k, 0:D], c.ident[0:D, 0:D]))


def attention_sums(nc, c, by_dst, same, stash, d_table, x1_table, small):
    H0 = 4
    with Scope(nc, "att_") as s:
        xb = [s.sb(f"ends{b}", [P, CT, 2 * D]) for b in range(2)]
        fl = [s.sb(f"same{b}", [P, CW]) for b in range(2)]
        xn = s.sb("normed", [P, CT, 2 * D])
        low, high_, rng = (s.sb(n, [P, 2 * CT]) for n in ("low", "high", "range"))
        xnT = s.sb("normedT", [P, CW])
        sg = s.sb("sigmoid", [P, CT, 4 * D])
        eb = [s.sb(f"exps{b}", [P, CT, 4 * D]) for b in range(2)]
        rr = [s.sb(f"rest{b}", [P, CT, 3 * D]) for b in range(2)]
        sca, scb = s.sb("scan_a", [P, CW]), s.sb("scan_b", [D, CW])
        ca, cb = s.sb("carry_a", [P, 1]), s.sb("carry_b", [D, 1])
        t1 = s.sb("t1", [P, CT, D])
        sl, sr = s.sb("sum_l", [P, CT, D]), s.sb("sum_r", [P, CT, D])
        sq = s.sb("squares", [P, CT, D])
        mean, std, rstd = (s.sb(n, [P, CT]) for n in ("mean", "std", "rstd"))
        dv = [s.sb(f"delta{b}", [P, CT, D]) for b in range(2)]
        st = [s.sb(f"stash{b}", [P, CT, 4 * D]) for b in range(2)]
        xs1 = [s.sb(f"x1_src{b}", [P, CT, D]) for b in range(2)]
        zero = s.sb("zero_row", [1, D])
        g = SmallGather(nc, s, small)
        pT = s.ps("pT", [P, 512])
        q = [s.ps(f"q{k}", [P, 512]) for k in range(2)]
        pA = s.ps("pA", [P, 1024])
        pB = s.ps("pB", [P, 1024])
        loaded = [s.sem(f"loaded{b}") for b in range(2)]
        flagged = [s.sem(f"flagged{b}") for b in range(2)]
        stored = [s.sem(f"stored{b}") for b in range(2)]
        (normed, turned, evac, product, read, expd, fed, rested, turned2, scanned, back, centred, squared, summed, rooted,
         finished, linked, zeroed) = (
            s.sem(n) for n in ("normed", "turned", "evac", "product", "read", "expd", "fed", "rested", "turned2", "scanned",
                               "back", "centred", "squared", "summed", "rooted", "finished", "linked", "zeroed"))
        block = s.block()
        src3 = by_dst.rearrange("(p t) k -> p t k", p=P)

        @block.sync
        def _(sp):
            sp.wait_ge(zeroed, 1)
            sp.dma_start(d_table[ZERO:ZERO + 1, :], zero[:, :]).then_inc(zeroed, 16)

            def ends(n, m, b):
                wait(sp, rested, n - 1)
                sp.dma_start(xb[b][:, :, :], src3[:, bass.ds(n * CT, CT), 0:2 * D]).then_inc(loaded[b], 16)

            def flags(n, m, b):
                wait(sp, scanned, n - 1)
                sp.dma_start(fl[b][:, :], flag_chunk(same, n)).then_inc(flagged[b], 16)

            staged(sp, NCH, [(0, ends), (0, flags), (0, g.stage), (1, g.take)])
            sp.wait_ge(zeroed, 17)
            g.end(sp)
            for b in range(2):
                sp.wait_ge(stored[b], 48 * PAIRS)

        @block.gpsimd
        def _(pool):
            g.start(pool)

            def store(n, m, b):
                pool.wait_ge(finished, n + 1)
                pool.dma_start(chunk_of(d_table, 0, n, D), flat(dv[b][:, :, :])).then_inc(stored[b], 16)
                pool.dma_start(chunk_of(stash, 0, n, 4 * D), flat(st[b][:, :, :])).then_inc(stored[b], 16)
                pool.dma_start(chunk_of(x1_table, SLOTS, n, D), flat(xs1[b][:, :, :])).then_inc(stored[b], 16)
            staged(pool, NCH, [(0, g.gather), (0, store)])

        @block.tensor
        def _(pe):
            def turn(n, m, b):
                pe.wait_ge(normed, n + 1)
                for h, (k0, k1) in enumerate(((0, H0), (H0, CT))):
                    wait(pe, evac, 2 * n + h)
                    for k in range(k0, k1):
                        mm = nc.tensor.transpose(pT[:, (k - k0) * P:(k - k0 + 1) * P], xn[:, k, :], c.ident[:, :])
                    mm.then_inc(turned, 1)

            def multiply(n, m, b):
                pe.wait_ge(evac, 2 * n + 2)
                for k in range(CT):
                    t = n * CT + k
                    wait(pe, read, t - 1)
                    par = (b * CT + k) % 2
                    nc.tensor.matmul(q[par][:, :], xnT[:, k * P:(k + 1) * P], c.w0[:, :, :].rearrange("p a b -> p (a b)"),
                                     start=True, stop=False)
                    nc.tensor.matmul(q[par][:, :], c.ones3[:, :], c.b0[:, :], start=False, stop=True).then_inc(product, 1)

            def turn_exps(n, m, b):
                pe.wait_ge(fed, n + 1)
                for k in range(CT):
                    nc.tensor.transpose(pA[:, k * P:(k + 1) * P], eb[b][:, k, 0:2 * D], c.ident[:, :])
                    mm = nc.tensor.transpose(pB[0:D, k * P:(k + 1) * P], st[b][:, k, 0:D], c.ident[:, :])
                mm.then_inc(turned2, 1)

            def turn_back(n, m, b):
                pe.wait_ge(scanned, n + 1)
                for k in range(CT):
                    nc.tensor.transpose(pA[:, k * P:(k + 1) * P], sca[:, k * P:(k + 1) * P], c.ident[:, :])
                    mm = nc.tensor.transpose(pB[:, k * D:(k + 1) * D], scb[:, k * P:(k + 1) * P], c.ident[0:D, 0:D])
                mm.then_inc(back, 1)

            staged(pe, NCH, [(0, turn), (1, turn_back), (0, multiply), (0, turn_exps)])

        @block.scalar
        def _(act):
            def evacuate(h, n):
                k0, k1 = ((0, H0), (H0, CT))[h]
                act.wait_ge(turned, 2 * n + h + 1)
                wait(act, product, n * CT)
                nc.scalar.activation(xnT[:, k0 * P:k1 * P], pT[:, 0:(k1 - k0) * P], ACT.Copy).then_inc(evac, 1)

            def square(n, m, b):
                act.wait_ge(centred, n + 1)
                nc.scalar.activation(sq[:, :, :], rr[b][:, :, D:2 * D], ACT.Square).then_inc(squared, 1)

            def root(n, m, b):
                act.wait_ge(summed, n + 1)
                nc.scalar.activation(std[:, :], std[:, :], ACT.Sqrt, bias=c.eps[:, :], scale=1.0 / D).then_inc(rooted, 1)

            def read_product(n, m, b):
                wait(act, expd, 3 * n)
                wait(act, finished, n - 1)
                wait(act, stored[b], m * 48)
                for k in range(CT):
                    par = (b * CT + k) % 2
                    act.wait_ge(product, n * CT + k + 1)
                    nc.scalar.activation(sg[:, k, :], q[par][:, 0:4 * D], ACT.Sigmoid)
                    nc.scalar.activation(st[b][:, k, D:2 * D], q[par][:, 4 * D:5 * D], ACT.Copy)
                    nc.scalar.activation(rr[b][:, k, :], q[par][:, 5 * D:8 * D], ACT.Copy).then_inc(read, 1)
                act.wait_ge(read, n * CT + CT)
                nc.scalar.activation(eb[b][:, :, D:2 * D], sg[:, :, 0:D], ACT.Exp).then_inc(expd, 1)
                nc.scalar.activation(st[b][:, :, 0:D], sg[:, :, D:2 * D], ACT.Exp).then_inc(expd, 1)
                nc.scalar.activation(eb[b][:, :, 2 * D:4 * D], sg[:, :, 2 * D:4 * D], ACT.Exp).then_inc(expd, 1)

            staged(act, NCH, [(0, lambda n, m, b: evacuate(0, n)), (1, square), (0, lambda n, m, b: evacuate(1, n)),
                              (1, root), (0, read_product)])

        @block.vector
        def _(dve):
            link = Link(dve, linked)
            v = nc.vector
            link(v.memset(ca[:, :], 0.0))
            link(v.memset(cb[:, :], 0.0))
            v.memset(zero[:, :], 0.0).then_inc(zeroed, 1)
            m0 = c.m0[:, :].unsqueeze(1).to_broadcast([P, CT, D])

            def scale(n, m, b):
                dve.wait_ge(loaded[b], m * 16 + 16)
                x2 = xb[b][:, :, :].rearrange("p t (e k) -> p (t e) k", e=2)
                n2 = xn[:, :, :].rearrange("p t (e k) -> p (t e) k", e=2)
                link.go(v.tensor_reduce(low[:, :], x2, AX.X, ALU.min))
                link(v.tensor_reduce(high_[:, :], x2, AX.X, ALU.max))
                link.go(v.scalar_tensor_tensor(out=rng[:, :], in0=high_[:, :], scalar=EPS, in1=low[:, :],
                                               op0=ALU.add, op1=ALU.subtract))
                wait(dve, turned, 2 * n)
                link(v.tensor_tensor(n2, x2, bc(low[:, :], D), ALU.subtract))
                link(v.reciprocal(rng[:, :], rng[:, :]))
                v.tensor_tensor(n2, n2, bc(rng[:, :], D), ALU.mult).then_inc(normed, 1)

            def centre_sources(n, m, b):
                y = rr[b][:, :, D:2 * D]
                link(v.tensor_reduce(mean[:, :], y, AX.X, ALU.add))
                link(v.tensor_scalar(mean[:, :], mean[:, :], 1.0 / D, None, ALU.mult))
                v.tensor_tensor(y, y, bc(mean[:, :], D), ALU.subtract).then_inc(centred, 1)

            def scan(n, m, b):
                dve.wait_ge(turned2, n + 1)
                dve.wait_ge(flagged[b], m * 16 + 16)
                link.go(v.tensor_tensor_scan(out=sca[:, :], data0=fl[b][:, :], data1=pA[:, 0:CW], initial=ca[:, :],
                                             op0=ALU.mult, op1=ALU.add))
                link(v.tensor_tensor_scan(out=scb[:, :], data0=fl[b][0:D, :], data1=pB[0:D, 0:CW], initial=cb[:, :],
                                          op0=ALU.mult, op1=ALU.add))
                link(v.tensor_copy(ca[:, :], sca[:, CW - 1:CW]))
                v.tensor_copy(cb[:, :], scb[:, CW - 1:CW]).then_inc(scanned, 1)
                dve.wait_ge(scanned, n + 1)

            def normalise_sources(n, m, b):
                dve.wait_ge(squared, n + 1)
                v.tensor_reduce(std[:, :], sq[:, :, :], AX.X, ALU.add).then_inc(summed, 1)
                link(v.tensor_tensor(t1[:, :, :], eb[b][:, :, 2 * D:3 * D], rr[b][:, :, 0:D], ALU.mult))
                dve.wait_ge(rooted, n + 1)
                link(v.reciprocal(rstd[:, :], std[:, :]))
                wait(dve, stored[b], m * 48)
                link(v.tensor_tensor(xs1[b][:, :, :], rr[b][:, :, D:2 * D], bc(rstd[:, :], D), ALU.mult))

            def conclude(n, m, b):
                rd, res = rr[b][:, :, 0:D], rr[b][:, :, 2 * D:3 * D]
                sel, ser = eb[b][:, :, 2 * D:3 * D], eb[b][:, :, 3 * D:4 * D]
                w3, rest = st[b][:, :, 2 * D:3 * D], st[b][:, :, 3 * D:4 * D]
                dve.wait_ge(back, n + 1)
                back_a = pA[:, 0:CW].rearrange("p (t k) -> p t k", k=P)
                back_b = pB[:, 0:CT * D].rearrange("p (t k) -> p t k", k=D)
                link.go(v.tensor_tensor(t1[:, :, :], back_a[:, :, 0:D], t1[:, :, :], ALU.add))
                link.go(v.tensor_tensor(sl[:, :, :], back_a[:, :, D:P], sel, ALU.add))
                link(v.tensor_tensor(sr[:, :, :], back_b, ser, ALU.add))
                link.go(v.reciprocal(sl[:, :, :], sl[:, :, :]))
                link(v.reciprocal(sr[:, :, :], sr[:, :, :]))
                link.go(v.tensor_tensor(t1[:, :, :], t1[:, :, :], sl[:, :, :], ALU.mult))
                link(v.tensor_tensor(w3, sr[:, :, :], m0, ALU.mult))
                link.go(v.tensor_tensor(dv[b][:, :, :], t1[:, :, :], rd, ALU.subtract))
                link(v.tensor_tensor(sl[:, :, :], t1[:, :, :], ser, ALU.mult))
                link(v.tensor_tensor(sl[:, :, :], sl[:, :, :], w3, ALU.mult))
                v.tensor_tensor(rest, sl[:, :, :], res, ALU.add).then_inc(finished, 1)
                dve.wait_ge(finished, n + 1)

            def weigh(n, m, b):
                dve.wait_ge(expd, 3 * n + 3)
                v.tensor_tensor(eb[b][:, :, 0:D], eb[b][:, :, D:2 * D], st[b][:, :, D:2 * D], ALU.mult).then_inc(fed, 1)
                v.tensor_tensor(rr[b][:, :, D:3 * D], rr[b][:, :, D:3 * D], xb[b][:, :, :], ALU.add).then_inc(rested, 1)
                dve.wait_ge(rested, n + 1)
            staged(dve, NCH, [(0, scale), (1, centre_sources), (1, scan), (1, normalise_sources), (1, conclude), (0, weigh)],
                   [link])


def attention_out(nc, c, same, stash, d_table, x1_table):
    with Scope(nc, "ato_") as s:
        g = Gather(nc, s, [(d_table, c.idx["b1"], 0, D)], D)
        st = [s.sb(f"stash{b}", [P, CT, 4 * D]) for b in range(2)]
        fl = [s.sb(f"same{b}", [P, CW]) for b in range(2)]
        t = s.sb("t", [P, CT, D])
        sc = s.sb("scan", [D, CW])
        ca = s.sb("carry", [D, 1])
        y = s.sb("y", [P, CT, D])
        o = [s.sb(f"out{b}", [P, CT, D]) for b in range(2)]
        norm = Norm(nc, s, c, CT)
        pT = s.ps("pT", [D, 1024])
        pR = s.ps("pR", [P, 512])
        loaded = [s.sem(f"loaded{b}") for b in range(2)]
        stored = [s.sem(f"stored{b}") for b in range(2)]
        fed, turned, scanned, back, finished, linked = (s.sem(n) for n in ("fed", "turned", "scanned", "back", "finished", "linked"))
        block = s.block()

        @block.sync
        def _(sp):
            def body(n, m, b):
                g.sp(sp, n, m, b)
                wait(sp, finished, n - 1)
                sp.dma_start(flat(st[b][:, :, :]), chunk_of(stash, 0, n, 4 * D)).then_inc(loaded[b], 16)
                sp.dma_start(fl[b][:, :], flag_chunk(same, n)).then_inc(loaded[b], 16)
            staged(sp, NCH, [(0, body)])

        @block.gpsimd
        def _(pool):
            g.start(pool)

            def body(n, m, b):
                wait(pool, finished, n - 1)
                g.pool(pool, n, m, b)
            staged(pool, NCH, [(0, body)])

        @block.tensor
        def _(pe):
            def body(n, m, b):
                pe.wait_ge(fed, n + 1)
                for k in range(CT):
                    mm = turn_64(nc, pT[:, k * P:(k + 1) * P], t[:, k, :], c.ident, k == 0)
                mm.then_inc(turned, 1)
                pe.wait_ge(scanned, n + 1)
                for k in range(CT):
                    mm = nc.tensor.matmul(pR[:, k * D:(k + 1) * D], sc[:, k * P:(k + 1) * P], c.ident[0:D, 0:D], start=True, stop=True)
                mm.then_inc(back, 1)
            staged(pe, NCH, [(0, body)])

        @block.scalar
        def _(act):
            def body(n, m, b):
                norm.root(act, n)
                act.wait_ge(finished, n + 1)
                act.dma_start(chunk_of(x1_table, 0, n, D), flat(o[b][:, :, :])).then_inc(stored[b], 16)
            staged(act, NCH, [(0, body)])
            for b in range(2):
                act.wait_ge(stored[b], 16 * PAIRS)

        @block.vector
        def _(dve):
            link = Link(dve, linked)
            v = nc.vector
            link(v.memset(ca[:, :], 0.0))

            def body(n, m, b):
                g.wait(dve, m, b)
                dve.wait_ge(loaded[b], m * 32 + 32)
                so = st[b]
                link(v.tensor_tensor(t[:, :, :], g.buf[b][:, :, :], so[:, :, D:2 * D], ALU.add))
                v.tensor_tensor(t[:, :, :], t[:, :, :], so[:, :, 0:D], ALU.mult).then_inc(fed, 1)
                dve.wait_ge(turned, n + 1)
                link(v.tensor_tensor_scan(out=sc[:, :], data0=fl[b][0:D, :], data1=pT[:, 0:CW], initial=ca[:, :],
                                          op0=ALU.mult, op1=ALU.add))
                v.tensor_copy(ca[:, :], sc[:, CW - 1:CW]).then_inc(scanned, 1)
                dve.wait_ge(scanned, n + 1)
                wait(dve, stored[b], m * 16)
                dve.wait_ge(back, n + 1)
                rows = pR[:, 0:CT * D].rearrange("p (t k) -> p t k", k=D)
                link(v.tensor_tensor(y[:, :, :], rows, so[:, :, 2 * D:3 * D], ALU.mult))
                link(v.tensor_tensor(y[:, :, :], y[:, :, :], so[:, :, 3 * D:4 * D], ALU.add))
                norm.dve(dve, link, n, y[:, :, :], o[b][:, :, :])
                v.tensor_copy(t[:, 0, 0:1], y[:, 0, 0:1]).then_inc(finished, 1)
                dve.wait_ge(finished, n + 1)
            staged(dve, NCH, [(0, body)], [link])


def chebyshev_start(nc, c, x1_table, t0_src, x2_table):
    with Scope(nc, "ch0_") as s:
        g = Gather(nc, s, [(x1_table, c.idx["a3"], 0, D), (x1_table, c.idx["a2"], D, D)], 2 * D)
        xT = s.sb("rowsT", [P, CW])
        y = s.sb("y", [P, CT, D])
        o = [s.sb(f"out{b}", [P, CT, D]) for b in range(2)]
        ones = s.sb("ones_row", [1, P])
        norm = Norm(nc, s, c, CT)
        pT = s.ps("pT", [P, 1024])
        pR = s.ps("pR", [P, 1024])
        stored = [s.sem(f"stored{b}") for b in range(2)]
        kept = [s.sem(f"kept{b}") for b in range(2)]
        turned, evac, product, finished, linked, ready = (s.sem(n) for n in ("turned", "evac", "product", "finished", "linked", "ready"))
        block = s.block()
        t0v = t0_src.rearrange("(p t) k -> p t k", p=P)

        @block.sync
        def _(sp):
            def body(n, m, b):
                g.sp(sp, n, m, b)
            staged(sp, NCH, [(0, body)])

        @block.gpsimd
        def _(pool):
            g.start(pool)

            def body(n, m, b):
                wait(pool, finished, n - 1)
                wait(pool, kept[b], m * 16)
                g.pool(pool, n, m, b)
            staged(pool, NCH, [(0, body)])

        @block.tensor
        def _(pe):
            def body(n, m, b):
                g.wait(pe, m, b)
                wait(pe, evac, n)
                for k in range(CT):
                    mm = nc.tensor.transpose(pT[:, k * P:(k + 1) * P], g.buf[b][:, k, :], c.ident[:, :])
                mm.then_inc(turned, 1)
                pe.wait_ge(evac, n + 1)
                wait(pe, finished, n)
                for k in range(CT):
                    nc.tensor.matmul(pR[:, k * P:(k + 1) * P], xT[:, k * P:(k + 1) * P], c.w1d[:, :], start=True, stop=False)
                    mm = nc.tensor.matmul(pR[:, k * P:(k + 1) * P], ones[:, :], flat(c.b1x[:, :, :]), start=False, stop=True)
                mm.then_inc(product, 1)
            pe.wait_ge(ready, 1)
            staged(pe, NCH, [(0, body)])

        @block.scalar
        def _(act):
            def body(n, m, b):
                act.wait_ge(turned, n + 1)
                wait(act, product, n)
                nc.scalar.activation(xT[:, :], pT[:, 0:CW], ACT.Copy).then_inc(evac, 1)
                g.wait(act, m, b)
                act.dma_start(t0v[:, bass.ds(n * CT, CT), :], g.buf[b][:, :, 0:D]).then_inc(kept[b], 16)
                norm.root(act, n)
                act.wait_ge(finished, n + 1)
                act.dma_start(chunk_of(x2_table, 2 * SLOTS, n, D), flat(o[b][:, :, :])).then_inc(stored[b], 16)
            staged(act, NCH, [(0, body)])
            for b in range(2):
                act.wait_ge(kept[b], 16 * PAIRS)
                act.wait_ge(stored[b], 16 * PAIRS)

        @block.vector
        def _(dve):
            link = Link(dve, linked)
            v = nc.vector
            v.memset(ones[:, :], 1.0).then_inc(ready, 1)

            def body(n, m, b):
                dve.wait_ge(product, n + 1)
                g.wait(dve, m, b)
                wait(dve, stored[b], m * 16)
                rows = pR[:, 0:CW].rearrange("p (t k) -> p t k", k=P)
                at = bass.ds(n * (CT * D), CT * D)
                link(v.tensor_scalar(flat(c.acc[:, :, :])[:, at].rearrange("p (t k) -> p t k", k=D), rows[:, :, 0:D], 1.0, None, ALU.mult))
                link(v.tensor_scalar(flat(c.t_even[:, :, :])[:, at].rearrange("p (t k) -> p t k", k=D), g.buf[b][:, :, D:2 * D], 1.0, None, ALU.mult))
                link(v.scalar_tensor_tensor(out=y[:, :, :], in0=rows[:, :, D:P], scalar=0.0, in1=g.buf[b][:, :, D:2 * D],
                                            op0=ALU.max, op1=ALU.add))
                norm.dve(dve, link, n, y[:, :, :], o[b][:, :, :])
                v.tensor_copy(y[:, 0, 0:1], o[b][:, 0, 0:1]).then_inc(finished, 1)
                dve.wait_ge(finished, n + 1)
            staged(dve, NCH, [(0, body)], [link])


def chebyshev_hop(nc, c, k_hop, same, p_in, p_out):
    with Scope(nc, f"hop{k_hop}_") as s:
        g = Gather(nc, s, [(p_in, c.idx["a4"], 0, D)], D) if k_hop else None
        fl = [s.sb(f"same{b}", [D, CW]) for b in range(2)]
        msg = [s.sb(f"messages{b}", [P, CT, D]) for b in range(2)]
        sc = s.sb("scan", [D, CW])
        ca = s.sb("carry", [D, 1])
        o = [s.sb(f"out{b}", [P, CT, D]) for b in range(2)] if k_hop < 4 else None
        sums_tmp = s.sb("product", [P, CT, D])
        pT = [s.ps(f"pT{b}", [D, 1024]) for b in range(2)]
        pR = s.ps("pR", [P, 1024])
        loaded = [s.sem(f"loaded{b}") for b in range(2)]
        stored = [s.sem(f"stored{b}") for b in range(2)]
        fed, turned, scanned, back, finished, linked = (s.sem(n) for n in ("fed", "turned", "scanned", "back", "finished", "linked"))
        t_here = c.t_odd if k_hop % 2 else c.t_even
        block = s.block()

        @block.sync
        def _(sp):
            def body(n, m, b):
                if g:
                    g.sp(sp, n, m, b)
                wait(sp, scanned, n - 1)
                sp.dma_start(fl[b][:, :], flag_chunk(same, n, D)).then_inc(loaded[b], 16)
            staged(sp, NCH, [(0, body)])

        if g:
            @block.gpsimd
            def _(pool):
                g.start(pool)

                def body(n, m, b):
                    wait(pool, fed, n - 1)
                    g.pool(pool, n, m, b)
                staged(pool, NCH, [(0, body)])

        @block.tensor
        def _(pe):
            def turn(n, m, b):
                pe.wait_ge(fed, n + 1)
                wait(pe, scanned, n - 1)
                for k in range(CT):
                    mm = turn_64(nc, pT[b][:, k * P:(k + 1) * P], msg[b][:, k, :], c.ident, k == 0)
                mm.then_inc(turned, 1)

            def rows(n, m, b):
                pe.wait_ge(scanned, n + 1)
                wait(pe, finished, n)
                for k in range(CT):
                    mm = nc.tensor.matmul(pR[:, k * P:(k + 1) * P], sc[:, k * P:(k + 1) * P], c.wp[:, k_hop, :], start=True, stop=True)
                mm.then_inc(back, 1)
            staged(pe, NCH, [(0, turn), (1, rows)])

        if k_hop < 4:
            @block.scalar
            def _(act):
                def body(n, m, b):
                    act.wait_ge(finished, n + 1)
                    act.dma_start(chunk_of(p_out, 0, n, D), flat(o[b][:, :, :])).then_inc(stored[b], 16)
                staged(act, NCH, [(0, body)])
                for b in range(2):
                    act.wait_ge(stored[b], 16 * PAIRS)

        @block.vector
        def _(dve):
            link = Link(dve, linked)
            v = nc.vector
            link(v.memset(ca[:, :], 0.0))

            def messages(n, m, b):
                at = bass.ds(n * (CT * D), CT * D)
                here = flat(t_here[:, :, :])[:, at]
                if k_hop == 1:
                    g.wait(dve, m, b)
                    link(v.tensor_scalar(here, flat(g.buf[b][:, :, :]), 1.0, None, ALU.mult))
                elif k_hop > 1:
                    g.wait(dve, m, b)
                    link(v.scalar_tensor_tensor(out=here, in0=flat(g.buf[b][:, :, :]), scalar=2.0, in1=here,
                                                op0=ALU.mult, op1=ALU.subtract))
                v.tensor_tensor(msg[b][:, :, :], here.rearrange("p (t k) -> p t k", k=D),
                                bc(c.norm[:, bass.ds(n * CT, CT)], D), ALU.mult).then_inc(fed, 1)

            def scan(n, m, b):
                dve.wait_ge(turned, n + 1)
                dve.wait_ge(loaded[b], m * 16 + 16)
                wait(dve, back, n)
                link(v.tensor_tensor_scan(out=sc[:, :], data0=fl[b][:, :], data1=pT[b][:, 0:CW], initial=ca[:, :],
                                          op0=ALU.mult, op1=ALU.add))
                v.tensor_copy(ca[:, :], sc[:, CW - 1:CW]).then_inc(scanned, 1)
                dve.wait_ge(scanned, n + 1)

            def sums(n, m, b):
                if k_hop < 4:
                    wait(dve, stored[b], m * 16)
                dve.wait_ge(back, n + 1)
                got = pR[:, 0:CW].rearrange("p (t k) -> p t k", k=P)
                nd = bc(c.neg_dis[:, bass.ds(n * CT, CT)], D)
                tmp = sums_tmp[:, :, :]
                if k_hop < 4:
                    link(v.tensor_tensor(o[b][:, :, :], got[:, :, 0:D], nd, ALU.mult))
                link(v.tensor_tensor(tmp, got[:, :, D:P], nd, ALU.mult))
                acc = flat(c.acc[:, :, :])[:, bass.ds(n * (CT * D), CT * D)]
                v.tensor_tensor(acc, acc, flat(tmp), ALU.add).then_inc(finished, 1)
                dve.wait_ge(finished, n + 1)
            staged(dve, NCH, [(0, messages), (2, sums), (1, scan)], [link])


def chebyshev_end(nc, c, t0_src, x2_table, x3_table):
    with Scope(nc, "che_") as s:
        t0 = [s.sb(f"t0_{b}", [P, CT, D]) for b in range(2)]
        y = s.sb("y", [P, CT, D])
        ro = s.sb("root_out", [P, CT])
        o = [[s.sb(f"out{j}{b}", [P, CT, D]) for b in range(2)] for j in range(3)]
        norm = Norm(nc, s, c, CT)
        loaded = [s.sem(f"loaded{b}") for b in range(2)]
        stored = [s.sem(f"stored{b}") for b in range(2)]
        finished, linked = s.sem("finished"), s.sem("linked")
        block = s.block()

        @block.sync
        def _(sp):
            def body(n, m, b):
                wait(sp, finished, n - 1)
                sp.dma_start(flat(t0[b][:, :, :]), chunk_of(t0_src, 0, n, D)).then_inc(loaded[b], 16)
            staged(sp, NCH, [(0, body)])

        @block.scalar
        def _(act):
            def body(n, m, b):
                norm.root(act, 2 * n)
                norm.root(act, 2 * n + 1)
                act.wait_ge(finished, n + 1)
                for j, (table, first) in enumerate(((x2_table, 0), (x2_table, SLOTS), (x3_table, SLOTS))):
                    act.dma_start(chunk_of(table, first, n, D), flat(o[j][b][:, :, :])).then_inc(stored[b], 16)
            staged(act, NCH, [(0, body)])
            for b in range(2):
                act.wait_ge(stored[b], 48 * PAIRS)

        @block.vector
        def _(dve):
            link = Link(dve, linked)
            v = nc.vector

            def body(n, m, b):
                at = bass.ds(n * (CT * D), CT * D)
                dve.wait_ge(loaded[b], m * 16 + 16)
                wait(dve, stored[b], m * 48)
                link(v.tensor_scalar(ro[:, :], c.inv_out[:, bass.ds(n * CT, CT)], 1.0, None, ALU.mult))
                link(v.scalar_tensor_tensor(out=flat(y[:, :, :]), in0=flat(c.acc[:, :, :])[:, at], scalar=0.0,
                                            in1=flat(t0[b][:, :, :]), op0=ALU.max, op1=ALU.add))
                norm.dve(dve, link, 2 * n, y[:, :, :], o[1][b][:, :, :])
                link(v.tensor_tensor(o[0][b][:, :, :], o[1][b][:, :, :], bc(ro[:, :], D), ALU.mult))
                link(v.tensor_copy(y[:, :, :], o[1][b][:, :, :]))
                norm.dve(dve, link, 2 * n + 1, y[:, :, :], o[2][b][:, :, :])
                v.tensor_copy(y[:, 0, 0:1], o[2][b][:, 0, 0:1]).then_inc(finished, 1)
                dve.wait_ge(finished, n + 1)
            staged(dve, NCH, [(0, body)], [link])


class Scatter:

    def __init__(self, nc, s, out, index):
        self.nc, self.out, self.index = nc, out, index
        self.buf = [s.sb(f"final_rows{b}", [P, CT, D]) for b in range(2)]
        self.stage = [s.sb(f"target{b}", [P, CT], I32) for b in range(2)]
        self.gate = s.sb("gate_out", [P, 2], I32)
        self.gates = s.sem("gates_out")
        self.staged = [s.sem(f"targets{b}") for b in range(2)]
        self.done = [s.sem(f"scattered{b}") for b in range(2)]
        self.per = 16 * CT

    def targets(self, act, n, m, b):
        wait(act, self.done[b], m * self.per)
        act.dma_start(self.stage[b][:, :], self.index[:, bass.ds(n * CT, CT)]).then_inc(self.staged[b], 16)

    def start(self, pool):
        self.nc.gpsimd.memset(self.gate[:, :], 0).then_inc(self.gates, 1)

    def pool(self, pool, n, m, b):
        pool.wait_ge(self.staged[b], m * 16 + 16)
        pass_gate(self.nc, pool, self.gate, self.gates, n + 1)
        for k in range(CT):
            self.nc.gpsimd.indirect_dma_start(
                out=self.out[:, :], out_offset=bass.IndirectOffsetOnAxis(ap=self.stage[b][:, k:k + 1].bitcast(U32), axis=0),
                in_=self.buf[b][:, k, :], in_offset=None, bounds_check=N - 1, oob_is_err=False).then_inc(self.done[b], 16)


def pool_gather_scatter(pool, g, sc, finished):
    g.start(pool)
    sc.start(pool)

    def gather(n, m, b):
        wait(pool, finished, n - 1)
        g.pool(pool, n, m, b)

    def scatter(n, m, b):
        pool.wait_ge(finished, n + 1)
        sc.pool(pool, n, m, b)
    staged(pool, NCH, [(2, scatter), (0, gather)])
    for b in range(2):
        pool.wait_ge(sc.done[b], sc.per * PAIRS)


def light_layer(nc, c, same, x2_table, x3_table, out):
    with Scope(nc, "lgt_") as s:
        g = Gather(nc, s, [(x2_table, c.idx["b2"], 0, D), (x2_table, c.idx["b3"], D, D)], 2 * D)
        sca = Scatter(nc, s, out, c.out_b)
        fl = [s.sb(f"same{b}", [P, CW]) for b in range(2)]
        sc = s.sb("scan", [D, CW])
        ca = s.sb("carry", [D, 1])
        ri = s.sb("root_in", [P, CT])
        y = s.sb("y", [P, CT, D])
        o = [s.sb(f"out{b}", [P, CT, D]) for b in range(2)]
        norm = Norm(nc, s, c, CT)
        pT = s.ps("pT", [D, 1024])
        pR = s.ps("pR", [P, 512])
        loaded = [s.sem(f"loaded{b}") for b in range(2)]
        stored = [s.sem(f"stored{b}") for b in range(2)]
        turned, scanned, back, finished, linked = (s.sem(n) for n in ("turned", "scanned", "back", "finished", "linked"))
        block = s.block()

        @block.sync
        def _(sp):
            def body(n, m, b):
                g.sp(sp, n, m, b)
                wait(sp, finished, n - 1)
                sp.dma_start(fl[b][:, :], flag_chunk(same, n)).then_inc(loaded[b], 16)
            staged(sp, NCH, [(0, body)])

        @block.gpsimd
        def _(pool):
            pool_gather_scatter(pool, g, sca, finished)

        @block.tensor
        def _(pe):
            def body(n, m, b):
                g.wait(pe, m, b)
                wait(pe, scanned, n)
                for k in range(CT):
                    mm = turn_64(nc, pT[:, k * P:(k + 1) * P], g.buf[b][:, k, 0:D], c.ident, k == 0)
                mm.then_inc(turned, 1)
                pe.wait_ge(scanned, n + 1)
                for k in range(CT):
                    mm = nc.tensor.matmul(pR[:, k * D:(k + 1) * D], sc[:, k * P:(k + 1) * P], c.ident[0:D, 0:D], start=True, stop=True)
                mm.then_inc(back, 1)
            staged(pe, NCH, [(0, body)])

        @block.scalar
        def _(act):
            def body(n, m, b):
                sca.targets(act, n, m, b)
                norm.root(act, 2 * n)
                norm.root(act, 2 * n + 1)
                act.wait_ge(finished, n + 1)
                act.dma_start(chunk_of(x3_table, 0, n, D), flat(o[b][:, :, :])).then_inc(stored[b], 16)
            staged(act, NCH, [(0, body)])
            for b in range(2):
                act.wait_ge(stored[b], 16 * PAIRS)

        @block.vector
        def _(dve):
            link = Link(dve, linked)
            v = nc.vector
            link(v.memset(ca[:, :], 0.0))

            def body(n, m, b):
                link(v.tensor_scalar(ri[:, :], c.inv_in[:, bass.ds(n * CT, CT)], 1.0, None, ALU.mult))
                dve.wait_ge(turned, n + 1)
                dve.wait_ge(loaded[b], m * 16 + 16)
                link(v.tensor_tensor_scan(out=sc[:, :], data0=fl[b][0:D, :], data1=pT[:, 0:CW], initial=ca[:, :],
                                          op0=ALU.mult, op1=ALU.add))
                v.tensor_copy(ca[:, :], sc[:, CW - 1:CW]).then_inc(scanned, 1)
                dve.wait_ge(scanned, n + 1)
                wait(dve, stored[b], m * 16)
                wait(dve, sca.done[b], m * sca.per)
                g.wait(dve, m, b)
                dve.wait_ge(back, n + 1)
                rows = pR[:, 0:CT * D].rearrange("p (t k) -> p t k", k=D)
                link(v.tensor_tensor(y[:, :, :], rows, bc(ri[:, :], D), ALU.mult))
                link(v.tensor_tensor(y[:, :, :], y[:, :, :], g.buf[b][:, :, D:2 * D], ALU.add))
                norm.dve(dve, link, 2 * n, y[:, :, :], o[b][:, :, :])
                link(v.tensor_copy(y[:, :, :], o[b][:, :, :]))
                norm.dve(dve, link, 2 * n + 1, y[:, :, :], sca.buf[b][:, :, :])
                v.tensor_copy(y[:, 0, 0:1], sca.buf[b][:, 0, 0:1]).then_inc(finished, 1)
                dve.wait_ge(finished, n + 1)
            staged(dve, NCH, [(0, body)], [link])


def edge_layer(nc, c, far, x3_table, out):
    with Scope(nc, "edg_") as s:
        g = Gather(nc, s, [(x3_table, c.idx["a6"], 0, D), (x3_table, c.idx["a5"], D, D)], 2 * D)
        sca = Scatter(nc, s, out, c.out_a)
        fl = [s.sb(f"far{b}", [P, CW]) for b in range(2)]
        hin = s.sb("hin", [P, CT, 2 * D])
        hT = s.sb("hT", [P, CW])
        h1 = s.sb("h1", [P, CW])
        sc = s.sb("scan", [D, CW])
        ca = s.sb("carry", [D, 1])
        y = s.sb("y", [P, CT, D])
        norm = Norm(nc, s, c, CT)
        pT = s.ps("pT", [P, 1024])
        pH = s.ps("pH", [P, 1024])
        pO = s.ps("pO", [D, 1024])
        pR = s.ps("pR", [P, 512])
        loaded = [s.sem(f"loaded{b}") for b in range(2)]
        fed, turned, evac, hid, act1, outp, scanned, back, finished, linked = (
            s.sem(n) for n in ("fed", "turned", "evac", "hidden", "relu", "product", "scanned", "back", "finished", "linked"))
        block = s.block()

        @block.sync
        def _(sp):
            def body(n, m, b):
                g.sp(sp, n, m, b)
                wait(sp, finished, n - 1)
                sp.dma_start(fl[b][:, :], flag_chunk(far, n)).then_inc(loaded[b], 16)
            staged(sp, NCH, [(0, body)])

        @block.gpsimd
        def _(pool):
            pool_gather_scatter(pool, g, sca, finished)

        @block.tensor
        def _(pe):
            def body(n, m, b):
                pe.wait_ge(fed, n + 1)
                for k in range(CT):
                    mm = nc.tensor.transpose(pT[:, k * P:(k + 1) * P], hin[:, k, :], c.ident[:, :])
                mm.then_inc(turned, 1)
                pe.wait_ge(evac, n + 1)
                for a, z in pieces():
                    mm = nc.tensor.matmul(pH[:, a:z], c.w31[:, :], hT[:, a:z], start=True, stop=True)
                mm.then_inc(hid, 1)
                pe.wait_ge(act1, n + 1)
                for a, z in pieces():
                    mm = nc.tensor.matmul(pO[:, a:z], c.w32[:, :], h1[:, a:z], start=True, stop=True)
                mm.then_inc(outp, 1)
                pe.wait_ge(scanned, n + 1)
                for k in range(CT):
                    mm = nc.tensor.matmul(pR[:, k * D:(k + 1) * D], sc[:, k * P:(k + 1) * P], c.ident[0:D, 0:D], start=True, stop=True)
                mm.then_inc(back, 1)
            staged(pe, NCH, [(0, body)])

        @block.scalar
        def _(act):
            def body(n, m, b):
                sca.targets(act, n, m, b)
                act.wait_ge(turned, n + 1)
                nc.scalar.activation(hT[:, :], pT[:, 0:CW], ACT.Copy).then_inc(evac, 1)
                act.wait_ge(hid, n + 1)
                nc.scalar.activation(h1[:, :], pH[:, 0:CW], ACT.Relu, bias=c.b31[:, :]).then_inc(act1, 1)
                norm.root(act, n)
            staged(act, NCH, [(0, body)])

        @block.vector
        def _(dve):
            link = Link(dve, linked)
            v = nc.vector
            link(v.memset(ca[:, :], 0.0))

            def body(n, m, b):
                g.wait(dve, m, b)
                link(v.tensor_copy(hin[:, :, 0:D], g.buf[b][:, :, 0:D]))
                v.tensor_tensor(hin[:, :, D:2 * D], g.buf[b][:, :, D:2 * D], g.buf[b][:, :, 0:D], ALU.subtract).then_inc(fed, 1)
                dve.wait_ge(outp, n + 1)
                dve.wait_ge(loaded[b], m * 16 + 16)
                link(v.tensor_tensor_scan(out=sc[:, :], data0=fl[b][0:D, :], data1=pO[:, 0:CW], initial=ca[:, :],
                                          op0=ALU.add, op1=ALU.max))
                v.tensor_copy(ca[:, :], sc[:, CW - 1:CW]).then_inc(scanned, 1)
                dve.wait_ge(scanned, n + 1)
                wait(dve, sca.done[b], m * sca.per)
                dve.wait_ge(back, n + 1)
                rows = pR[:, 0:CT * D].rearrange("p (t k) -> p t k", k=D)
                link(v.tensor_tensor(y[:, :, :], rows, c.b32[:, :].unsqueeze(1).to_broadcast([P, CT, D]), ALU.add))
                link(v.tensor_tensor(y[:, :, :], y[:, :, :], g.buf[b][:, :, 0:D], ALU.add))
                norm.dve(dve, link, n, y[:, :, :], sca.buf[b][:, :, :])
                v.tensor_copy(y[:, 0, 0:1], sca.buf[b][:, 0, 0:1]).then_inc(finished, 1)
                dve.wait_ge(finished, n + 1)
            staged(dve, NCH, [(0, body)], [link])


class Isolated:

    R = 125
    CG = 16
    CHUNKS = N // (R * CG)

    def __init__(self, nc, s, c, x, out, first, count):
        R, CG = self.R, self.CG
        self.nc, self.c, self.first, self.count = nc, c, first, count
        self.xb = [s.sb(f"iso_x{b}", [R, CG, D]) for b in range(2)]
        self.o = [s.sb(f"iso_out{b}", [R, CG, D]) for b in range(2)]
        self.xn, self.x1 = s.sb("iso_scaled", [R, CG, D]), s.sb("iso_first", [R, CG, D])
        self.y = [s.sb(f"iso_centred{j}", [R, CG, D]) for j in range(2)]
        self.sq = [s.sb(f"iso_squares{j}", [R, CG, D]) for j in range(2)]
        self.low, self.inv = s.sb("iso_low", [R, CG]), s.sb("iso_inv", [R, CG])
        self.mean = [s.sb(f"iso_mean{j}", [R, CG]) for j in range(2)]
        self.std = [s.sb(f"iso_std{j}", [R, CG]) for j in range(2)]
        self.rstd = [s.sb(f"iso_rstd{j}", [R, CG]) for j in range(2)]
        self.xT = [s.sb(f"iso_xT{j}", [P, 2, 4 * R]) for j in range(2)]
        self.ones = s.sb("iso_ones", [1, R])
        self.eps3 = s.sb("iso_eps3", [R, 1])
        self.pT = [s.ps(f"iso_pT{j}", [P, 2, 512]) for j in range(2)]
        self.pR = [s.ps(f"iso_pR{j}", [R, 1024]) for j in range(2)]
        self.loaded = [s.sem(f"iso_loaded{b}") for b in range(2)]
        self.stored = [s.sem(f"iso_stored{b}") for b in range(2)]
        self.ready, self.linked, self.finished = s.sem("iso_ready"), s.sem("iso_linked"), s.sem("iso_finished")
        (self.fed, self.turned, self.evac, self.product, self.centred, self.squared, self.summed, self.rooted) = (
            [s.sem(f"iso_{n}{j}") for j in range(2)] for n in
            ("fed", "turned", "evac", "product", "centred", "squared", "summed", "rooted"))
        self.xv = x.rearrange("(p t) k -> p (t k)", p=R)
        self.ov = out.rearrange("(p t) k -> p (t k)", p=R)

    def at(self, n):
        w = self.CG * D
        return bass.ds(n * w + self.first * w, w)

    def tensor(self, pe):
        nc, R, CG = self.nc, self.R, self.CG
        pe.wait_ge(self.ready, 2)

        def turn_and_multiply(j, src, w, bias, n):
            pe.wait_ge(self.fed[j], n + 1)
            wait(pe, self.evac[j], n)
            for k in range(CG // 2):
                mm = nc.tensor.transpose(self.pT[j][:, k // 4, k % 4 * R:(k % 4 + 1) * R],
                                         src[:, 2 * k:2 * k + 2, :].rearrange("p a b -> p (a b)"), self.c.ident[0:R, 0:R])
            mm.then_inc(self.turned[j], 1)
            pe.wait_ge(self.evac[j], n + 1)
            wait(pe, self.centred[j], n)
            for k in range(CG // 2):
                mine = self.pR[j][:, k * P:(k + 1) * P]
                nc.tensor.matmul(mine, self.xT[j][:, k // 4, k % 4 * R:(k % 4 + 1) * R], w[:, :], start=True, stop=False)
                mm = nc.tensor.matmul(mine, self.ones[:, :], flat(bias[:, :, :]), start=False, stop=True)
            mm.then_inc(self.product[j], 1)

        staged(pe, self.count, [
            (0, lambda n, m, b: turn_and_multiply(0, self.xn, self.c.wiso, self.c.biso, n)),
            (1, lambda n, m, b: turn_and_multiply(1, self.x1, self.c.w1d, self.c.b1x, n))])

    def scalar(self, act):
        nc, R, CG = self.nc, self.R, self.CG

        def load(n, b):
            act.dma_start(flat(self.xb[b][:, :, :]), self.xv[:, self.at(n)]).then_inc(self.loaded[b], 16)

        def evacuate(j, n):
            act.wait_ge(self.turned[j], n + 1)
            wait(act, self.product[j], n)
            nc.scalar.activation(self.xT[j][:, :, :], self.pT[j][:, :, 0:4 * R], ACT.Copy).then_inc(self.evac[j], 1)

        def square(j, n):
            act.wait_ge(self.centred[j], n + 1)
            nc.scalar.activation(self.sq[j][:, :, :], self.y[j][:, :, :], ACT.Square).then_inc(self.squared[j], 1)

        def root(j, n):
            act.wait_ge(self.summed[j], n + 1)
            if j == 0:
                nc.scalar.activation(self.std[0][:, :], self.std[0][:, :], ACT.Sqrt, bias=self.c.eps[0:R, :],
                                     scale=1.0 / D).then_inc(self.rooted[0], 1)
            else:
                nc.scalar.activation(self.std[1][:, :], self.std[1][:, :], ACT.Sqrt, bias=self.eps3[:, :],
                                     scale=(1.0 + EPS + EPS * EPS) / D).then_inc(self.rooted[1], 1)

        def store(n, b):
            act.wait_ge(self.finished, n + 1)
            act.dma_start(self.ov[:, self.at(n)], flat(self.o[b][:, :, :])).then_inc(self.stored[b], 16)

        act.wait_ge(self.ready, 2)
        staged(act, self.count, [
            (1, lambda n, m, b: evacuate(0, n)),
            (2, lambda n, m, b: square(0, n)),
            (0, lambda n, m, b: load(n, b)),
            (3, lambda n, m, b: square(1, n)),
            (2, lambda n, m, b: root(0, n)),
            (3, lambda n, m, b: root(1, n)),
            (2, lambda n, m, b: evacuate(1, n)),
            (3, lambda n, m, b: store(n, b))])
        for b in range(2):
            act.wait_ge(self.stored[b], self.count // 2 * 16)

    def vector(self, dve):
        nc, v = self.nc, self.nc.vector
        link = Link(dve, self.linked)
        v.memset(self.ones[:, :], 1.0).then_inc(self.ready, 1)
        v.memset(self.eps3[:, :], EPS ** 3).then_inc(self.ready, 1)

        def scale(n, m, b):
            x = self.xb[b][:, :, :]
            dve.wait_ge(self.loaded[b], m * 16 + 16)
            link.go(v.tensor_reduce(self.low[:, :], x, AX.X, ALU.min))
            link(v.tensor_reduce(self.inv[:, :], x, AX.X, ALU.max))
            link.go(v.scalar_tensor_tensor(out=self.inv[:, :], in0=self.inv[:, :], scalar=EPS, in1=self.low[:, :],
                                           op0=ALU.add, op1=ALU.subtract))
            wait(dve, self.turned[0], n)
            link(v.tensor_tensor(self.xn[:, :, :], x, bc(self.low[:, :], D), ALU.subtract))
            link(v.reciprocal(self.inv[:, :], self.inv[:, :]))
            v.tensor_tensor(self.xn[:, :, :], self.xn[:, :, :], bc(self.inv[:, :], D), ALU.mult).then_inc(self.fed[0], 1)

        def centre(j, n):
            y, mean = self.y[j], self.mean[j]
            link(v.tensor_reduce(mean[:, :], y[:, :, :], AX.X, ALU.add))
            link(v.tensor_scalar(mean[:, :], mean[:, :], 1.0 / D, None, ALU.mult))
            v.tensor_tensor(y[:, :, :], y[:, :, :], bc(mean[:, :], D), ALU.subtract).then_inc(self.centred[j], 1)

        def first_sum(n, m, b):
            dve.wait_ge(self.product[0], n + 1)
            rows = self.pR[0][:, :].rearrange("p (t k) -> p t k", k=D)
            link(v.tensor_tensor(self.y[0][:, :, :], rows, self.xb[b][:, :, :], ALU.add))
            centre(0, n)

        def second_sum(n, m, b):
            dve.wait_ge(self.product[1], n + 1)
            rows = self.pR[1][:, :].rearrange("p (t k) -> p t k", k=D)
            link(v.scalar_tensor_tensor(out=self.y[1][:, :, :], in0=rows, scalar=0.0, in1=self.x1[:, :, :],
                                        op0=ALU.max, op1=ALU.add))
            centre(1, n)

        def variance(j, n):
            dve.wait_ge(self.squared[j], n + 1)
            v.tensor_reduce(self.std[j][:, :], self.sq[j][:, :, :], AX.X, ALU.add).then_inc(self.summed[j], 1)

        def normalise(j, n, b):
            dve.wait_ge(self.rooted[j], n + 1)
            link(v.reciprocal(self.rstd[j][:, :], self.std[j][:, :]))
            scale_of = bc(self.rstd[j][:, :], D)
            if j == 0:
                v.tensor_tensor(self.x1[:, :, :], self.y[0][:, :, :], scale_of, ALU.mult).then_inc(self.fed[1], 1)
                dve.wait_ge(self.fed[1], n + 1)
            else:
                v.tensor_tensor(self.o[b][:, :, :], self.y[1][:, :, :], scale_of, ALU.mult).then_inc(self.finished, 1)
                dve.wait_ge(self.finished, n + 1)

        def last_scale(n, m, b):
            wait(dve, self.stored[b], m * 16)
            normalise(1, n, b)

        staged(dve, self.count, [
            (0, scale),
            (1, first_sum),
            (2, second_sum),
            (1, lambda n, m, b: variance(0, n)),
            (2, lambda n, m, b: variance(1, n)),
            (1, lambda n, m, b: normalise(0, n, b)),
            (2, last_scale)], [link])

    def engines(self, block):
        @block.tensor
        def _(pe):
            self.tensor(pe)

        @block.scalar
        def _(act):
            self.scalar(act)

        @block.vector
        def _(dve):
            self.vector(dve)


def index_arrays(nc, c):
    with Scope(nc, "idx_") as s:
        ta, tb = s.sb("ta", [P, NT]), s.sb("tb", [P, NT])
        linked, vin, vout = s.sem("linked"), s.sem("vin"), s.sem("vout")
        block = s.block()
        FAR = float(4 * N)

        @block.scalar
        def _(act):
            for k, t in enumerate((c.inv_out, c.inv_in)):
                act.wait_ge(vin, k + 1)
                nc.scalar.activation(t[:, :], t[:, :], ACT.Sqrt).then_inc(vout, 1)

        @block.vector
        def _(dve):
            link = Link(dve, linked)
            v = nc.vector
            af, bf = c.rec_a[:, :, :].bitcast(FP32), c.rec_b[:, :, :].bitcast(FP32)
            for name, rec, col in (("b1", c.rec_b, 1), ("b2", c.rec_b, 2), ("b3", c.rec_b, 3), ("a2", c.rec_a, 2),
                                   ("a3", c.rec_a, 3), ("a4", c.rec_a, 4), ("a5", c.rec_a, 5), ("a6", c.rec_a, 6)):
                link(v.tensor_copy(c.idx[name][:, :], rec[:, :, col]))
            link(v.tensor_scalar(ta[:, :], c.last_a[:, :], -1.0, -FAR, ALU.add, ALU.mult))
            link(v.tensor_tensor(tb[:, :], af[:, :, 0], ta[:, :], ALU.add))
            link(v.tensor_copy(c.out_a[:, :], tb[:, :]))
            link(v.tensor_scalar(ta[:, :], c.last_b[:, :], -1.0, -FAR, ALU.add, ALU.mult))
            link(v.tensor_tensor(tb[:, :], bf[:, :, 0], ta[:, :], ALU.add))
            link(v.scalar_tensor_tensor(out=tb[:, :], in0=bf[:, :, 4], scalar=FAR, in1=tb[:, :], op0=ALU.mult, op1=ALU.add))
            link(v.tensor_copy(c.out_b[:, :], tb[:, :]))
            for k, (t, src) in enumerate(((c.inv_out, af[:, :, 7]), (c.inv_in, bf[:, :, 5]))):
                v.tensor_scalar(t[:, :], src, 1.0, None, ALU.max).then_inc(vin, 1)
                dve.wait_ge(vout, k + 1)
                link(v.reciprocal(t[:, :], t[:, :]))


def hop_norms(nc, c, dis):
    with Scope(nc, "nrm_") as s:
        linked = s.sem("linked")
        block = s.block()

        @block.vector
        def _(dve):
            Link(dve, linked)(nc.vector.tensor_tensor(c.norm[:, :], c.rec_a[:, :, :].bitcast(FP32)[:, :, 1], dis[:, :, 0], ALU.mult))


def zero_rows(nc, tables):
    with Scope(nc, "zr_") as s:
        z = s.sb("z", [1, D])
        a, b = s.sem("made"), s.sem("stored")
        block = s.block()

        @block.vector
        def _(dve):
            nc.vector.memset(z[:, :], 0.0).then_inc(a, 1)

        @block.sync
        def _(sp):
            sp.wait_ge(a, 1)
            for t in tables:
                sp.dma_start(t[ZERO:ZERO + 1, :], z[:, :]).then_inc(b, 16)
            sp.wait_ge(b, 16 * len(tables))


FIRST_ISO = 18


class Bag:
    pass


def build(nc, a, out):
    def dram(name, shape):
        return nc.dram_tensor(name, shape, FP32).ap()

    x = a["x"]
    entries = dram("node_entries", [P * LO, 4])
    by_dst = dram("by_dst", [SLOTS, 2 * D + META])
    by_src = dram("by_src", [SLOTS, META])
    v_a, v_b, w_a, w_b, same_a, same_b, far_a, far_b, deg_row = (
        dram(n, [SLOTS + 2 if n[0] == "v" else SLOTS]) for n in
        ("v_a", "v_b", "w_a", "w_b", "same_a", "same_b", "far_a", "far_b", "deg_row"))
    dis_t = dram("dis_t", [SLOTS + 1, 4])
    d_t = dram("d_t", [SLOTS + 1, D])
    stash = dram("stash", [SLOTS, 4 * D])
    x1_t = dram("x1_t", [2 * SLOTS, D])
    t0_s = dram("t0_s", [SLOTS, D])
    p_t = [dram(f"p_t{k}", [SLOTS + 1, D]) for k in range(2)]
    x2_t = dram("x2_t", [3 * SLOTS, D])
    x3_t = dram("x3_t", [2 * SLOTS, D])
    with Scope(nc) as s:
        c = Bag()
        c.ident = s.sb("ident", [P, P])
        c.eps = s.sb("eps", [P, 1])
        c.rec_a, c.rec_b = s.sb("rec_a", [P, NT, META], I32), s.sb("rec_b", [P, NT, META], I32)
        c.w0, c.b0, c.m0 = s.sb("w0", [P, 8, D]), s.sb("b0", [3, 8 * D], BF16), s.sb("m0", [P, D])
        c.ones3 = s.sb("ones3", [3, P], BF16)
        c.wiso, c.biso = s.sb("wiso", [P, P]), s.sb("biso", [1, 2, D])
        c.w1d, c.b1x, c.wp = s.sb("w1d", [P, P]), s.sb("b1x", [1, 2, D]), s.sb("wp", [D, 5, 2 * D])
        c.w31, c.w32, c.b31, c.b32 = s.sb("w31", [P, P]), s.sb("w32", [P, D]), s.sb("b31", [P, 1]), s.sb("b32", [P, D])
        with Scope(nc) as r:
            c.ones, c.tri = r.sb("ones", [P, P]), r.sb("tri", [P, P])
            c.rank_mask = r.sb("rank_mask", [P, BLK * P])
            c.iota16, c.iota_part = r.sb("iota16", [P, LO], F16), r.sb("iota_part", [P, 1])
            c.ident16, c.ones16, c.w128_16 = r.sb("ident16", [P, P], F16), r.sb("ones16", [P, P], F16), r.sb("w128_16", [P, P], F16)
            c.src, c.dst, c.ew = r.sb("src", [P, NT], I32), r.sb("dst", [P, NT], I32), r.sb("ew", [P, NT])
            c.key_s, c.key_d = r.sb("key_s", [P, NT, 3]), r.sb("key_d", [P, NT, 3])
            c.node_s, c.node_d = r.sb("node_s", [P, NT], I32), r.sb("node_d", [P, NT], I32)
            c.safe_s, c.safe_d = r.sb("safe_s", [P, NT], I32), r.sb("safe_d", [P, NT], I32)
            c.rank_s, c.rank_d = r.sb("rank_s", [P, NT]), r.sb("rank_d", [P, NT])
            c.count_s, c.count_d = r.sb("count_s", [P, LO]), r.sb("count_d", [P, LO])
            c.seg_s, c.seg_d = r.sb("seg_s", [P, NT, 4]), r.sb("seg_d", [P, NT, 4])
            c.row_a, c.row_b = r.sb("row_a", [P, NT], I32), r.sb("row_b", [P, NT], I32)
            constants(nc, c)
            load_edges(nc, c, a["src"], a["dst"], a["edge_weight"])
            load_weights(nc, c, a)
            rank_edges(nc, c, c.key_s, c.rank_s, c.count_s, "rank_s_")
            rank_edges(nc, c, c.key_d, c.rank_d, c.count_d, "rank_d_")
            node_table(nc, c, entries)
            gather_segments(nc, c, (entries, c.node_s, c.seg_s, 4), (entries, c.node_d, c.seg_d, 4), x, out, (0, FIRST_ISO))
            edge_records(nc, c)
            sort_edges(nc, c, x, by_dst, by_src, out, (FIRST_ISO, Isolated.CHUNKS - FIRST_ISO))
        c.last_a, c.last_b = s.sb("last_a", [P, NT]), s.sb("last_b", [P, NT])
        c.neg_dis, c.norm = s.sb("neg_dis", [P, NT]), s.sb("norm", [P, NT])
        c.inv_out, c.inv_in = s.sb("inv_out", [P, NT]), s.sb("inv_in", [P, NT])
        c.out_a, c.out_b = s.sb("out_a", [P, NT], I32), s.sb("out_b", [P, NT], I32)
        c.idx = {n: s.sb("idx_" + n, [P, NT], I32) for n in ("b1", "b2", "b3", "a2", "a3", "a4", "a5", "a6")}
        order_marks(nc, c, by_dst, c.rec_b, v_b, same_b, far_b, c.last_b, "mark_b_", w_b)
        order_marks(nc, c, by_src, c.rec_a, v_a, same_a, far_a, c.last_a, "mark_a_", w_a)
        source_scale(nc, c, same_a, w_a, deg_row, dis_t)
        index_arrays(nc, c)
        zero_rows(nc, p_t)
        with Scope(nc) as r:
            dis = r.sb("dis", [P, NT, 4])
            attention_sums(nc, c, by_dst, same_b, stash, d_t, x1_t, (dis_t, c.idx["a4"], dis, 4))
            hop_norms(nc, c, dis)
        attention_out(nc, c, same_b, stash, d_t, x1_t)
        with Scope(nc) as r:
            c.acc, c.t_even, c.t_odd = (r.sb(n, [P, NT, D]) for n in ("acc", "t_even", "t_odd"))
            chebyshev_start(nc, c, x1_t, t0_s, x2_t)
            for k in range(5):
                chebyshev_hop(nc, c, k, same_a, p_t[(k + 1) % 2], p_t[k % 2])
            chebyshev_end(nc, c, t0_s, x2_t, x3_t)
        light_layer(nc, c, same_b, x2_t, x3_t, out)
        edge_layer(nc, c, far_a, x3_t, out)


_INS = ['x', 'src', 'dst', 'edge_weight', 'L0_gnn_W1', 'L0_gnn_b1', 'L0_gnn_W2', 'L0_gnn_b2', 'L0_gnn_Wres', 'L0_gnn_bres',
        'L0_gnn_m', 'L1_gnn_W', 'L1_gnn_b', 'L3_gnn_W1', 'L3_gnn_b1', 'L3_gnn_W2', 'L3_gnn_b2']


def kernel(**inputs):
    import numpy as _np
    import concourse.bacc as _bacc
    from concourse import mybir as _mybir
    from concourse.bass_utils import run_bass_kernel_spmd as _run

    nc = _bacc.Bacc("TRN2", target_bir_lowering=False, num_devices=1)
    arrays, args = {}, {}
    for name in _INS:
        a = _np.ascontiguousarray(inputs[name])
        arrays[f"in_{name}_dram"] = a
        args[name] = nc.dram_tensor(f"in_{name}_dram", a.shape, _mybir.dt.from_np(a.dtype), kind="ExternalInput").ap()
    out = nc.dram_tensor("out_0_dram", (N, D), _mybir.dt.float32, kind="ExternalOutput").ap()
    build(nc, args, out)
    r = _run(nc, [arrays], core_ids=[0])
    return r.results[0]["out_0_dram"]
```

```python
import concourse.bass as bass
from concourse import mybir
from contextlib import ExitStack

FP32 = mybir.dt.float32
I32 = mybir.dt.int32
U32 = mybir.dt.uint32
F16 = mybir.dt.float16
BF16 = mybir.dt.bfloat16
ALU = mybir.AluOpType
ACT = mybir.ActivationFunctionType
AX = mybir.AxisListType

P = 128
D = 64
N = 100000
E = 25000
NT = -(-E // P)
SLOTS = NT * P
CT = 7
NCH = NT // CT
NONE = N
LO = 784
BLK = 4
NBLK = NT // BLK
META = 8


class Link:

    def __init__(self, eng, sem):
        self.eng, self.sem, self.base, self.k = eng, sem, 0, 0

    def __call__(self, ins):
        self.k += 1
        ins.then_inc(self.sem, 1)
        self.eng.wait_ge(self.sem, self.base + self.k)
        return ins

    def go(self, ins):
        self.k += 1
        ins.then_inc(self.sem, 1)


def turns(eng, count, body, links=()):
    starts = [ln.base + ln.k for ln in links]
    body(0)
    per = [ln.base + ln.k - s for ln, s in zip(links, starts)]
    if count > 1:
        with eng.Fori(1, count) as i:
            for ln, s, n in zip(links, starts, per):
                ln.base, ln.k = i * n + s, 0
            body(i)
    for ln, s, n in zip(links, starts, per):
        ln.base, ln.k = s + n * count, 0


def staged(eng, count, stages, links=()):
    lag = max(d for d, _ in stages)
    first = 2 * ((lag + 3) // 2)

    def step(t):
        for d, fn in stages:
            if 0 <= t - d < count:
                fn(t - d, (t - d) // 2, (t - d) % 2)

    for t in range(first - 2):
        step(t)
    before = [ln.base + ln.k for ln in links]
    step(first - 2)
    step(first - 1)
    start = [ln.base + ln.k for ln in links]
    per = [z - a for a, z in zip(before, start)]
    with eng.Fori(first // 2, count // 2) as i:
        for ln, s, n in zip(links, start, per):
            ln.base, ln.k = i * n + (s - first // 2 * n), 0
        for bb in range(2):
            for d, fn in stages:
                b = (bb - d) % 2
                fn(i * 2 + (bb - d), i + (bb - d - b) // 2, b)
    for ln, s, n in zip(links, start, per):
        ln.base, ln.k = s + n * (count // 2 - first // 2), 0
    for t in range(count // 2 * 2, count + lag):
        step(t)


def wait(eng, sem, value):
    if isinstance(value, int) and value <= 0:
        return
    eng.wait_ge(sem, value)


def pass_gate(nc, pool, gate, gates, value):
    pool.wait_ge(gates, value)
    nc.gpsimd.tensor_tensor(gate[:, 0:1], gate[:, 1:2], gate[:, 1:2], ALU.add).then_inc(gates, 1)


class Scope(ExitStack):
    def __init__(self, nc, tag=""):
        super().__init__()
        self.nc, self.tag, self.sems = nc, tag, []
        self.callback(self.clear)

    def sb(self, name, shape, dt=FP32):
        return self.enter_context(self.nc.sbuf_tensor(self.tag + name, shape, dt))

    def ps(self, name, shape, dt=FP32):
        return self.enter_context(self.nc.psum_tensor(self.tag + name, shape, dt))

    def sem(self, name):
        self.sems.append(self.nc.alloc_semaphore(self.tag + name))
        return self.sems[-1]

    def clear(self):
        if self.sems:
            self.nc.clear_and_free_semaphores(self.sems)
            self.nc.all_engine_barrier()

    def block(self):
        return self.enter_context(self.nc.Block())


def constants(nc, c):
    with Scope(nc, "const_") as s:
        io = s.sb("iota_i", [P, LO], I32)
        pi = s.sb("part_i", [P, 1], I32)
        made = s.sem("made")
        piped = s.sem("linked")
        block = s.block()

        @block.gpsimd
        def _(pool):
            link = Link(pool, piped)
            link(pool.iota(io[:, :], pattern=[[1, LO]], base=0, channel_multiplier=0))
            link(pool.iota(pi[:, :], pattern=[[0, 1]], base=0, channel_multiplier=1))
            for t in (c.ident, c.ones, c.tri, c.rank_mask):
                link(pool.memset(t[:, :], 1.0))
            link(pool.affine_select(out=c.ident[:, :], in_=c.ident[:, :], compare_op=ALU.is_equal, fill=0.0,
                                    base=0, pattern=[[-1, P]], channel_multiplier=1))
            link(pool.affine_select(out=c.tri[:, :], in_=c.tri[:, :], compare_op=ALU.is_gt, fill=0.0,
                                    base=0, pattern=[[1, P]], channel_multiplier=-1))
            own = c.rank_mask[:, (BLK - 1) * P:BLK * P]
            link(pool.affine_select(out=own, in_=own, compare_op=ALU.is_gt, fill=0.0,
                                    base=0, pattern=[[-1, P]], channel_multiplier=1))
            pool.nop().then_inc(made, 1)

        @block.vector
        def _(dve):
            dve.wait_ge(made, 1)
            link = Link(dve, s.sem("dve_linked"))
            link(nc.vector.tensor_copy(c.iota16[:, :], io[:, :]))
            link(nc.vector.tensor_copy(c.iota_part[:, :], pi[:, :]))
            link(nc.vector.tensor_copy(c.ident16[:, :], c.ident[:, :]))
            link(nc.vector.memset(c.ones16[:, :], 1.0))
            link(nc.vector.memset(c.w128_16[:, :], 128.0))


def load_edges(nc, c, src, dst, ew):
    full = E // NT
    rest = E - full * NT
    with Scope(nc, "edges_") as s:
        arrived = s.sem("arrived")
        cleared = s.sem("cleared")
        linked = s.sem("linked")
        hi_i = s.sb("hi_i", [P, NT], I32)
        lo_i = s.sb("lo_i", [P, NT], I32)
        block = s.block()

        @block.sync
        def _(sp):
            sp.wait_ge(cleared, 3)
            for a, t in ((src, c.src), (dst, c.dst), (ew, c.ew)):
                sp.dma_start(t[0:full, :], a[0:full * NT].rearrange("(p t) -> p t", t=NT)).then_inc(arrived, 16)
                sp.dma_start(t[full:full + 1, 0:rest], a[full * NT:E].rearrange("(a t) -> a t", a=1)).then_inc(arrived, 16)

        @block.vector
        def _(dve):
            link = Link(dve, linked)
            nc.vector.memset(c.src[:, :], NONE).then_inc(cleared, 1)
            nc.vector.memset(c.dst[:, :], NONE).then_inc(cleared, 1)
            nc.vector.memset(c.ew[:, :], 0.0).then_inc(cleared, 1)
            dve.wait_ge(cleared, 3)
            dve.wait_ge(arrived, 96)
            for v, key, u, g in ((c.src, c.key_s, c.node_s, c.safe_s), (c.dst, c.key_d, c.node_d, c.safe_d)):
                link(nc.vector.tensor_single_scalar(hi_i[:, :], v[:, :], 127, ALU.bitwise_and))
                link(nc.vector.tensor_single_scalar(lo_i[:, :], v[:, :], 7, ALU.logical_shift_right))
                link(nc.vector.tensor_copy(key[:, :, 0], hi_i[:, :]))
                link(nc.vector.tensor_copy(key[:, :, 1], lo_i[:, :]))
                link(nc.vector.tensor_copy(key[:, :, 2], v[:, :]))
                link(nc.vector.scalar_tensor_tensor(out=u[:, :], in0=key[:, :, 0], scalar=float(LO), in1=key[:, :, 1],
                                                    op0=ALU.mult, op1=ALU.add))
                link(nc.vector.tensor_scalar(g[:, :], key[:, :, 2], float(N - 1), None, ALU.min))


def rank_edges(nc, c, key, rank, count, tag):
    H = 512
    with Scope(nc, tag) as s:
        kc = [s.sb(f"keys{b}", [P, BLK, 3]) for b in range(2)]
        oh_hi = [s.sb(f"onehot_hi{b}", [P, BLK, P], BF16) for b in range(2)]
        oh_lo = [s.sb(f"onehot_lo{b}", [P, BLK, LO], BF16) for b in range(2)]
        oh_hiT = [s.sb(f"onehot_hiT{b}", [P, BLK * P], BF16) for b in range(2)]
        diag_hi = s.sb("diag_hi", [P, BLK, P], F16)
        diag_lo = s.sb("diag_lo", [P, BLK, P], F16)
        tab_h = [s.sb(f"count_high{b}", [P, LO], BF16) for b in range(2)]
        tab_l = [s.sb(f"count_low{b}", [P, LO], BF16) for b in range(2)]
        near = [s.sb(f"near{b}", [P, BLK]) for b in range(2)]
        far = s.sb("far", [P, BLK])
        read_mark = s.sb("read_mark", [P, 4])
        equal = [s.sb(f"equal{k}", [P, BLK * P]) for k in range(BLK)]
        picked = [s.sb(f"picked{k}", [P, LO]) for k in range(2)]
        run = s.ps("running", [P, 1024])
        got = [s.ps(f"got{k}", [P, 1024]) for k in range(2)]
        row_hi = s.ps("row_hi", [P, 512])
        row_v = s.ps("row_v", [P, 512])
        keys_in, diags, rows, rows_used, hots, queried, extracted, counted, high, low, dve_l, cleared = (s.sem(n) for n in (
            "keys_in", "diags", "rows", "rows_used", "hots", "queried", "extracted", "counted", "high", "low", "dve_linked", "cleared"))
        block = s.block()

        @block.scalar
        def _(act):
            def diagonals(n, m, b):
                act.wait_ge(keys_in, n + 1)
                wait(act, rows, n)
                for k in range(BLK):
                    nc.scalar.activation(diag_hi[:, k, :], c.ident16[:, :], ACT.Copy, scale=kc[b][:, k, 0:1])
                    last = nc.scalar.activation(diag_lo[:, k, :], c.ident16[:, :], ACT.Copy, scale=kc[b][:, k, 1:2])
                last.then_inc(diags, 1)

            def high_part(n, m, b):
                act.wait_ge(counted, n + 1)
                wait(act, queried, n * BLK)
                nc.scalar.activation(tab_h[b][:, :], run[:, 0:LO], ACT.Copy).then_inc(high, 1)
            staged(act, NBLK, [(0, diagonals), (2, high_part)])

        @block.tensor
        def _(pe):
            pe.wait_ge(cleared, 1)
            for a, z in ((0, H), (H, LO)):
                nc.tensor.matmul(run[:, a:z], tab_h[1][:, 0:P], tab_h[1][:, a:z], start=True, stop=False,
                                 skip_group_check=True)

            def add_counts(n, m, b):
                wait(pe, low, n)
                for k in range(BLK):
                    for a, z in ((0, H), (H, LO)):
                        last = nc.tensor.matmul(run[:, a:z], oh_hi[b][:, k, :], oh_lo[b][:, k, a:z], start=False, stop=False,
                                                skip_group_check=True)
                last.then_inc(counted, 1)

            def query(n, b, k0, k1):
                for k in range(k0, k1):
                    wait(pe, extracted, n * BLK + k - 1)
                    hot = oh_hiT[b][:, k * P:(k + 1) * P]
                    for a, z in ((0, H), (H, LO)):
                        nc.tensor.matmul(got[k % 2][:, a:z], hot, tab_h[1 - b][:, a:z], start=True, stop=False)
                        last = nc.tensor.matmul(got[k % 2][:, a:z], hot, tab_l[1 - b][:, a:z], start=False, stop=True)
                    last.then_inc(queried, 1)

            def first_queries(n, m, b):
                pe.wait_ge(hots, n + 1)
                wait(pe, low, n)
                query(n, b, 0, 2)

            def spread(n, m, b):
                pe.wait_ge(diags, n + 1)
                wait(pe, rows_used, n)
                hi, lo = (d[:, :, :].rearrange("p a b -> p (a b)") for d in (diag_hi, diag_lo))
                nc.tensor.matmul(row_hi[:, :], c.ones16[:, :], hi, start=True, stop=True)
                nc.tensor.matmul(row_v[:, :], c.ones16[:, :], hi, start=True, stop=False)
                nc.tensor.matmul(row_v[:, :], c.w128_16[:, :], lo, start=False, stop=True).then_inc(rows, 1)
            staged(pe, NBLK, [(2, first_queries), (2, add_counts), (2, lambda n, m, b: query(n, b, 2, BLK)), (0, spread)])

        @block.vector
        def _(dve):
            v = nc.vector
            link = Link(dve, dve_l)
            for b in range(2):
                link(v.memset(tab_l[b][:, :], 0.0))
                link(v.memset(tab_h[b][:, :], 0.0))
            v.memset(far[:, :], 0.0).then_inc(cleared, 1)
            dve.wait_ge(cleared, 1)

            def take_keys(n, m, b):
                wait(dve, diags, n - 1)
                v.tensor_scalar(kc[b][:, :, :].rearrange("p a b -> p (a b)"),
                                key[:, :, :].rearrange("p a b -> p (a b)")[:, bass.ds(n * (3 * BLK), 3 * BLK)],
                                1.0, None, ALU.mult).then_inc(keys_in, 1)
                dve.wait_ge(keys_in, n + 1)

            def hot_hi(n, m, b):
                wait(dve, counted, n - 1)
                link.go(v.tensor_tensor(oh_hi[b][:, :, :], c.iota16[:, 0:P].unsqueeze(1).to_broadcast([P, BLK, P]),
                                        kc[b][:, :, 0:1].to_broadcast([P, BLK, P]), ALU.is_equal))

            def hot_lo(k):
                step = link.go if k < BLK - 1 else link
                return lambda n, m, b: step(v.tensor_scalar(oh_lo[b][:, k, :], c.iota16[:, :], kc[b][:, k, 1:2], None,
                                                            ALU.is_equal))

            def hot_rows(n, m, b):
                dve.wait_ge(rows, n + 1)
                link.go(v.tensor_scalar(oh_hiT[b][:, :], row_hi[:, :], c.iota_part[:, :], None, ALU.is_equal))
                for k in range(BLK):
                    w = (k + 1) * P
                    step = link.go if k < BLK - 1 else link
                    step(v.scalar_tensor_tensor(out=equal[k][:, 0:w], in0=row_v[:, 0:w], scalar=kc[b][:, k, 2:3],
                                                in1=c.rank_mask[:, BLK * P - w:BLK * P], op0=ALU.is_equal,
                                                op1=ALU.mult, accum_out=near[b][:, k:k + 1]))
                v.tensor_copy(read_mark[:, 0:1], near[b][:, 0:1]).then_inc(rows_used, 1)

            def extract(k):
                def fn(n, m, b):
                    dve.wait_ge(queried, n * BLK + k + 1)
                    wait(dve, extracted, n * BLK + k - 1)
                    v.tensor_tensor_reduce(out=picked[k % 2][:, :], in0=got[k % 2][:, 0:LO], in1=oh_lo[b][:, k, :], scale=1.0,
                                           scalar=0.0, op0=ALU.mult, op1=ALU.add,
                                           accum_out=far[:, k:k + 1]).then_inc(extracted, 1)
                return fn

            def hots_made(n, m, b):
                dve.wait_ge(rows_used, n + 1)
                v.tensor_copy(read_mark[:, 2:3], near[b][:, 0:1]).then_inc(hots, 1)

            def low_part(n, m, b):
                dve.wait_ge(extracted, n * BLK + BLK)
                link.go(v.tensor_tensor(rank[:, bass.ds(n * BLK, BLK)], near[b][:, :], far[:, :], ALU.add))
                dve.wait_ge(high, n + 1)
                v.tensor_tensor(tab_l[b][:, :], run[:, 0:LO], tab_h[b][:, :], ALU.subtract).then_inc(low, 1)
                dve.wait_ge(low, n + 1)

            staged(dve, NBLK, [(0, take_keys), (1, hot_hi), (1, hot_lo(0)), (1, hot_rows), (2, extract(0)), (1, hot_lo(1)),
                               (2, extract(1)), (1, hot_lo(2)), (2, extract(2)), (1, hot_lo(3)), (2, extract(3)),
                               (1, hots_made), (2, low_part)], [link])
            link(v.tensor_copy(count[:, :], run[:, 0:LO]))


def node_table(nc, c, table):
    with Scope(nc, "nodes_") as s:
        ones = s.sb("ones", [P, LO])
        incl = s.sb("inclusive", [P, LO])
        has = s.sb("has", [P, LO])
        out = s.sb("entries", [P, LO, 4])
        base = [s.ps(f"base{k}", [P, 1]) for k in range(2)]
        summed = s.sem("summed")
        based = s.sem("based")
        dve_l = s.sem("dve_linked")
        stored = s.sem("stored")
        filled = s.sem("filled")
        block = s.block()

        @block.tensor
        def _(pe):
            for k in range(2):
                pe.wait_ge(summed, k + 1)
                nc.tensor.matmul(base[k][:, :], c.tri[:, :], incl[:, LO - 1:LO], start=True, stop=True).then_inc(based, 1)

        @block.vector
        def _(dve):
            link = Link(dve, dve_l)
            link(nc.vector.memset(ones[:, :], 1.0))
            for k, cnt in enumerate((c.count_s, c.count_d)):
                nc.vector.tensor_tensor_scan(out=incl[:, :], data0=ones[:, :], data1=cnt[:, :], initial=0.0,
                                             op0=ALU.mult, op1=ALU.add).then_inc(summed, 1)
                dve.wait_ge(summed, k + 1)
                dve.wait_ge(based, k + 1)
                link(nc.vector.tensor_scalar(incl[:, :], incl[:, :], base[k][:, :], None, ALU.add))
                link(nc.vector.tensor_tensor(out[:, :, 2 * k], incl[:, :], cnt[:, :], ALU.subtract))
                link(nc.vector.tensor_scalar(has[:, :], cnt[:, :], 0.0, None, ALU.is_gt))
                link(nc.vector.tensor_tensor(out[:, :, 2 * k + 1], incl[:, :], has[:, :], ALU.mult))
            nc.vector.tensor_copy(has[:, 0:1], incl[:, 0:1]).then_inc(filled, 1)

        @block.sync
        def _(sp):
            sp.wait_ge(filled, 1)
            sp.dma_start(table.rearrange("(p a) k -> p a k", p=P), out[:, :, :]).then_inc(stored, 16)
            sp.wait_ge(stored, 16)


class SmallGather:

    def __init__(self, nc, s, job, turn=0, shared=None):
        self.nc, (self.table, self.index, self.rows, self.words) = nc, job
        if shared:
            self.slots, self.got, self.gate, self.staged, self.gathered, self.taken, self.gates = shared
        else:
            self.slots = [s.sb(f"small_stage{b}", [P, CT], I32) for b in range(2)]
            self.got = [s.sb(f"small_rows{b}", [P, CT * self.words]) for b in range(2)]
            self.gate = s.sb("small_gate", [P, 2], I32)
            self.staged, self.gathered, self.taken = (
                [s.sem(f"small_{n}{b}") for b in range(2)] for n in ("staged", "gathered", "taken"))
            self.gates = s.sem("small_gates")
        self.before = turn

    def shared(self):
        return self.slots, self.got, self.gate, self.staged, self.gathered, self.taken, self.gates

    def stage(self, n, m, b, eng=None):
        eng = eng or self.nc.sync
        wait(eng, self.gathered[b], (m + self.before * PAIRS) * (16 * CT))
        eng.dma_start(self.slots[b][:, :], self.index[:, bass.ds(n * CT, CT)]).then_inc(self.staged[b], 16)

    def take(self, n, m, b):
        w = CT * self.words
        self.nc.sync.wait_ge(self.gathered[b], (m + self.before * PAIRS + 1) * (16 * CT))
        self.nc.sync.dma_start(self.rows.rearrange("p t k -> p (t k)")[:, bass.ds(n * w, w)],
                               self.got[b][:, :]).then_inc(self.taken[b], 16)

    def end(self, sp):
        for b in range(2):
            sp.wait_ge(self.taken[b], (self.before + 1) * PAIRS * 16)

    def start(self, pool):
        self.nc.gpsimd.memset(self.gate[:, :], 0).then_inc(self.gates, 1)

    def gather(self, n, m, b):
        pool, w = self.nc.gpsimd, self.words
        pool.wait_ge(self.staged[b], (m + self.before * PAIRS + 1) * 16)
        wait(pool, self.taken[b], (m + self.before * PAIRS) * 16)
        pass_gate(self.nc, pool, self.gate, self.gates, n + self.before * NCH + 1)
        for k in range(CT):
            pool.indirect_dma_start(
                out=self.got[b][:, k * w:(k + 1) * w], out_offset=None, in_=self.table[:, :],
                in_offset=bass.IndirectOffsetOnAxis(ap=self.slots[b][:, k:k + 1].bitcast(U32), axis=0),
            ).then_inc(self.gathered[b], 16)


def gather_segments(nc, c, job_s, job_d, x, out, iso):
    with Scope(nc, "segs_") as s:
        first = SmallGather(nc, s, job_s)
        second = SmallGather(nc, s, job_d, turn=1, shared=first.shared())
        isolated = Isolated(nc, s, c, x, out, *iso)
        block = s.block()

        @block.sync
        def _(sp):
            for g in (first, second):
                staged(sp, NCH, [(0, g.stage), (1, g.take)])
            second.end(sp)

        @block.gpsimd
        def _(pool):
            first.start(pool)
            for g in (first, second):
                staged(pool, NCH, [(0, g.gather)])

        isolated.engines(block)




CW = CT * P
ZERO = SLOTS
PAIRS = NCH // 2
EPS = 1e-5


def bc(ap, n):
    return ap.unsqueeze(2).to_broadcast([ap.shape[0], ap.shape[1], n])


def slot_rows(nc, link, row, slot, tmp_i, tmp_p, tmp_t):
    link(nc.vector.tensor_copy(tmp_i[:, :], slot))
    link(nc.vector.tensor_single_scalar(tmp_p[:, :], tmp_i[:, :], 127, ALU.bitwise_and))
    link(nc.vector.tensor_single_scalar(tmp_t[:, :], tmp_i[:, :], 7, ALU.logical_shift_right))
    link(nc.vector.scalar_tensor_tensor(out=row, in0=tmp_p[:, :], scalar=float(NT), in1=tmp_t[:, :],
                                        op0=ALU.mult, op1=ALU.add))


def edge_records(nc, c):
    with Scope(nc, "rec_") as s:
        ti, tp, tt = (s.sb(n, [P, NT], I32) for n in ("ti", "tp", "tt"))
        pa, pb, ea_s, eb_s, ea_d, eb_d, ta, tb, own = (s.sb(n, [P, NT]) for n in
                                                      ("pa", "pb", "ea_s", "eb_s", "ea_d", "eb_d", "ta", "tb", "own"))
        linked = s.sem("linked")
        block = s.block()

        @block.vector
        def _(dve):
            link = Link(dve, linked)
            v = nc.vector

            def tt_(o, a, b, op):
                link(v.tensor_tensor(o, a, b, op))

            def ts_(o, a, x, op):
                link(v.tensor_scalar(o, a, x, None, op))

            for out, seg, col, rank in ((pa, c.seg_s, 0, c.rank_s), (pb, c.seg_d, 2, c.rank_d)):
                tt_(ta[:, :], seg[:, :, col], rank[:, :], ALU.add)
                slot_rows(nc, link, out[:, :], ta[:, :], ti, tp, tt)
            for out, seg, col in ((ea_s, c.seg_s, 1), (eb_s, c.seg_s, 3), (ea_d, c.seg_d, 1), (eb_d, c.seg_d, 3)):
                link(v.tensor_scalar(ta[:, :], seg[:, :, col], -1.0, 0.0, ALU.add, ALU.max))
                slot_rows(nc, link, out[:, :], ta[:, :], ti, tp, tt)
            link(v.tensor_copy(c.row_a[:, :], pa[:, :]))
            link(v.tensor_copy(c.row_b[:, :], pb[:, :]))

            def choose(out, has, x, y, y_add):
                ts_(ta[:, :], has, 0.0, ALU.is_gt)
                if y is None:
                    link(v.tensor_scalar(tb[:, :], x, -float(y_add), None, ALU.add))
                    tt_(tb[:, :], tb[:, :], ta[:, :], ALU.mult)
                    ts_(out, tb[:, :], float(y_add), ALU.add)
                else:
                    link(v.scalar_tensor_tensor(out=tb[:, :], in0=x, scalar=-float(y_add), in1=y,
                                                op0=ALU.add, op1=ALU.subtract))
                    tt_(tb[:, :], tb[:, :], ta[:, :], ALU.mult)
                    link(v.scalar_tensor_tensor(out=out, in0=tb[:, :], scalar=float(y_add), in1=y,
                                                op0=ALU.add, op1=ALU.add))

            b, a = c.rec_b, c.rec_a
            bf, af = b[:, :, :].bitcast(FP32), a[:, :, :].bitcast(FP32)
            link(v.tensor_copy(bf[:, :, 0], c.dst[:, :]))
            choose(b[:, :, 1], c.seg_s[:, :, 3], eb_s[:, :], None, ZERO)
            link(v.tensor_copy(b[:, :, 2], ea_s[:, :]))
            ts_(pa[:, :], pa[:, :], 2.0 * SLOTS, ALU.add)
            ts_(own[:, :], ea_d[:, :], float(SLOTS), ALU.add)
            choose(b[:, :, 3], c.seg_d[:, :, 1], own[:, :], pa[:, :], 0.0)
            ts_(bf[:, :, 4], c.seg_d[:, :, 1], 0.0, ALU.is_gt)
            tt_(bf[:, :, 5], c.seg_d[:, :, 3], c.seg_d[:, :, 2], ALU.subtract)
            link(v.tensor_copy(b[:, :, 6], c.safe_s[:, :]))
            link(v.tensor_copy(b[:, :, 7], c.safe_d[:, :]))
            link(v.tensor_copy(af[:, :, 0], c.src[:, :]))
            link(v.tensor_copy(af[:, :, 1], c.ew[:, :]))
            link(v.tensor_copy(a[:, :, 2], eb_d[:, :]))
            choose(a[:, :, 3], c.seg_s[:, :, 3], eb_s[:, :], pb[:, :], SLOTS)
            choose(a[:, :, 4], c.seg_d[:, :, 1], ea_d[:, :], None, ZERO)
            link(v.tensor_copy(a[:, :, 5], eb_d[:, :]))
            choose(a[:, :, 6], c.seg_s[:, :, 3], eb_s[:, :], ea_s[:, :], SLOTS)
            tt_(af[:, :, 7], c.seg_s[:, :, 1], c.seg_s[:, :, 0], ALU.subtract)


def sort_edges(nc, c, x, by_dst, by_src, out, iso):
    NB = 4
    with Scope(nc, "sort_") as s:
        orders = []
        for name, table, row, rec in (("b", by_dst, c.row_b, c.rec_b), ("a", by_src, c.row_a, c.rec_a)):
            slots = [s.sb(f"target_{name}{b}", [P, CT], I32) for b in range(NB)]
            recs = [s.sb(f"record_{name}{b}", [P, CT * META], I32) for b in range(NB)]
            orders.append((table, row, rec.rearrange("p t k -> p (t k)"), slots, recs))
        gate = s.sb("gate", [P, 2], I32)
        gates = s.sem("gates")
        staged_in, scattered = ([s.sem(f"{n}{b}") for b in range(NB)] for n in ("staged", "scattered"))
        isolated = Isolated(nc, s, c, x, out, *iso)
        block = s.block()

        @block.sync
        def _(sp):
            def body(i):
                for b in range(NB):
                    n = i * NB + b
                    wait(sp, scattered[b], i * (32 * CT))
                    for _, row, rec, slots, recs in orders:
                        sp.dma_start(slots[b][:, :], row[:, bass.ds(n * CT, CT)]).then_inc(staged_in[b], 16)
                        sp.dma_start(recs[b][:, :], rec[:, bass.ds(n * (CT * META), CT * META)]).then_inc(staged_in[b], 16)
            turns(sp, NCH // NB, body)

        @block.gpsimd
        def _(pool):
            nc.gpsimd.memset(gate[:, :], 0).then_inc(gates, 1)

            def body(i):
                for b in range(NB):
                    pool.wait_ge(staged_in[b], i * 64 + 64)
                    pass_gate(nc, pool, gate, gates, i * NB + b + 1)
                    for k in range(CT):
                        for table, _, _, slots, recs in orders:
                            nc.gpsimd.indirect_dma_start(
                                out=table[:, :], out_offset=bass.IndirectOffsetOnAxis(ap=slots[b][:, k:k + 1].bitcast(U32), axis=0),
                                in_=recs[b][:, k * META:(k + 1) * META].bitcast(FP32), in_offset=None).then_inc(scattered[b], 16)
            turns(pool, NCH // NB, body)
            for b in range(NB):
                pool.wait_ge(scattered[b], NCH // NB * 32 * CT)

        isolated.engines(block)


def order_marks(nc, c, sorted_rows, rec, vrow, same_row, far_row, last, tag, val_row=None):
    T0, T1 = P, NT - P
    with Scope(nc, tag) as s:
        v = s.sb("v", [P, NT])
        w = s.sb("w", [P, NT])
        vT = [s.sb("vT0", [T0, P]), s.sb("vT1", [T1, P])]
        wT = [s.sb("wT0", [T0, P]), s.sb("wT1", [T1, P])]
        pv = [s.sb("pv0", [T0, P]), s.sb("pv1", [T1, P])]
        nx = [s.sb("nx0", [T0, P]), s.sb("nx1", [T1, P])]
        fl = [s.sb("fl0", [T0, P]), s.sb("fl1", [T1, P])]
        ng = [s.sb("ng0", [T0, P]), s.sb("ng1", [T1, P])]
        edge = s.sb("edge", [1, 2])
        tp = [s.ps("tp0", [T0, P]), s.ps("tp1", [T1, P])]
        wp = [s.ps("wp0", [T0, P]), s.ps("wp1", [T1, P])]
        bp = s.ps("bp", [P, NT])
        loaded, ready, turned, evac, stored, reread, marked, back, linked, kept = (
            s.sem(n) for n in ("loaded", "ready", "turned", "evac", "stored", "reread", "marked", "back", "linked", "kept"))
        cut = ((0, T0), (T0, NT))
        block = s.block()

        @block.sync
        def _(sp):
            sp.dma_start(rec[:, :, :], sorted_rows.rearrange("(p t) k -> p t k", p=P)[:, :, -META:].bitcast(I32)).then_inc(loaded, 16)
            sp.wait_ge(evac, 1)
            sp.dma_start(vrow[0:1].rearrange("(a n) -> a n", a=1), edge[0:1, 0:1]).then_inc(stored, 16)
            sp.dma_start(vrow[SLOTS + 1:SLOTS + 2].rearrange("(a n) -> a n", a=1), edge[0:1, 1:2]).then_inc(stored, 16)
            for k, (a, b) in enumerate(cut):
                sp.dma_start(vrow[1 + a * P:1 + b * P].rearrange("(t p) -> t p", p=P), vT[k][:, :]).then_inc(stored, 16)
                sp.dma_start(val_row[a * P:b * P].rearrange("(t p) -> t p", p=P), wT[k][:, :]).then_inc(stored, 16)
            sp.wait_ge(stored, 96)
            for k, (a, b) in enumerate(cut):
                sp.dma_start(pv[k][:, :], vrow[a * P:b * P].rearrange("(t p) -> t p", p=P)).then_inc(reread, 16)
                sp.dma_start(nx[k][:, :], vrow[2 + a * P:2 + b * P].rearrange("(t p) -> t p", p=P)).then_inc(reread, 16)
            sp.wait_ge(marked, 1)
            for k, (a, b) in enumerate(cut):
                sp.dma_start(same_row[a * P:b * P].rearrange("(t p) -> t p", p=P), fl[k][:, :]).then_inc(kept, 16)
                sp.dma_start(far_row[a * P:b * P].rearrange("(t p) -> t p", p=P), ng[k][:, :]).then_inc(kept, 16)
            sp.wait_ge(kept, 64)

        @block.vector
        def _(dve):
            link = Link(dve, linked)
            link(nc.vector.memset(edge[:, :], -1.0))
            dve.wait_ge(loaded, 16)
            link(nc.vector.tensor_copy(v[:, :], rec[:, :, 0].bitcast(FP32)))
            nc.vector.tensor_copy(w[:, :], rec[:, :, 1].bitcast(FP32)).then_inc(ready, 1)
            dve.wait_ge(turned, 1)
            for k in range(2):
                link(nc.vector.tensor_copy(vT[k][:, :], tp[k][:, :]))
                link(nc.vector.tensor_copy(wT[k][:, :], wp[k][:, :]))
            nc.vector.memset(edge[:, :], -1.0).then_inc(evac, 1)
            dve.wait_ge(evac, 1)
            dve.wait_ge(reread, 64)
            for k in range(2):
                link(nc.vector.tensor_tensor(fl[k][:, :], vT[k][:, :], pv[k][:, :], ALU.is_equal))
                link(nc.vector.tensor_scalar(ng[k][:, :], fl[k][:, :], -1.0, 1e30, ALU.add, ALU.mult))
                link(nc.vector.tensor_tensor(nx[k][:, :], vT[k][:, :], nx[k][:, :], ALU.not_equal))
            nc.vector.tensor_copy(pv[0][:, 0:1], nx[0][:, 0:1]).then_inc(marked, 1)
            dve.wait_ge(back, 1)
            link(nc.vector.tensor_copy(last[:, :], bp[:, :]))

        @block.tensor
        def _(pe):
            pe.wait_ge(ready, 1)
            for k, (a, b) in enumerate(cut):
                nc.tensor.transpose(tp[k][:, :], v[:, a:b], c.ident[:, :])
                mm = nc.tensor.transpose(wp[k][:, :], w[:, a:b], c.ident[:, :])
            mm.then_inc(turned, 1)
            pe.wait_ge(marked, 1)
            for k, (a, b) in enumerate(cut):
                mm = nc.tensor.transpose(bp[:, a:b], nx[k][:, :], c.ident[0:b - a, 0:b - a])
            mm.then_inc(back, 1)


def source_scale(nc, c, same_row, w_row, deg_row, dis_table):
    T0, T1 = P, NT - P
    HALF = SLOTS // 2
    with Scope(nc, "dis_") as s:
        fl = s.sb("fl", [1, HALF])
        wr = s.sb("wr", [1, HALF])
        carry = s.sb("carry", [1, 1])
        dT = [s.sb("dT0", [T0, P]), s.sb("dT1", [T1, P])]
        deg = s.sb("deg", [P, NT])
        pos = s.sb("pos", [P, NT])
        wide = s.sb("wide", [P, NT, 4])
        zero = s.sb("zero", [1, 4])
        bp = s.ps("bp", [P, NT])
        loaded, scanned, stored, reread, back, floored, rooted, filled, kept, linked = (
            s.sem(n) for n in ("loaded", "scanned", "stored", "reread", "back", "floored", "rooted", "filled", "kept", "linked"))
        cut = ((0, T0), (T0, NT))
        block = s.block()

        def row(a, h):
            return a[h * HALF:(h + 1) * HALF].rearrange("(a n) -> a n", a=1)

        @block.sync
        def _(sp):
            for h in range(2):
                wait(sp, stored, 16 * h)
                sp.dma_start(fl[:, :], row(same_row, h)).then_inc(loaded, 16)
                sp.dma_start(wr[:, :], row(w_row, h)).then_inc(loaded, 16)
                sp.wait_ge(scanned, h + 1)
                sp.dma_start(row(deg_row, h), wr[:, :]).then_inc(stored, 16)
            sp.wait_ge(stored, 32)
            for k, (a, b) in enumerate(cut):
                sp.dma_start(dT[k][:, :], deg_row[a * P:b * P].rearrange("(t p) -> t p", p=P)).then_inc(reread, 16)
            sp.wait_ge(filled, 1)
            sp.dma_start(dis_table[0:SLOTS, :].rearrange("(p t) k -> p t k", p=P), wide[:, :, :]).then_inc(kept, 16)
            sp.dma_start(dis_table[ZERO:ZERO + 1, :], zero[:, :]).then_inc(kept, 16)
            sp.wait_ge(kept, 32)

        @block.tensor
        def _(pe):
            pe.wait_ge(reread, 32)
            for k, (a, b) in enumerate(cut):
                mm = nc.tensor.transpose(bp[:, a:b], dT[k][:, :], c.ident[0:b - a, 0:b - a])
            mm.then_inc(back, 1)

        @block.scalar
        def _(act):
            act.wait_ge(floored, 1)
            nc.scalar.activation(deg[:, :], deg[:, :], ACT.Sqrt).then_inc(rooted, 1)

        @block.vector
        def _(dve):
            link = Link(dve, linked)
            link(nc.vector.memset(carry[:, :], 0.0))
            for h in range(2):
                dve.wait_ge(loaded, 32 * (h + 1))
                link(nc.vector.tensor_tensor_scan(out=wr[:, :], data0=fl[:, :], data1=wr[:, :], initial=carry[:, :],
                                                  op0=ALU.mult, op1=ALU.add))
                nc.vector.tensor_copy(carry[:, :], wr[:, HALF - 1:HALF]).then_inc(scanned, 1)
                dve.wait_ge(scanned, h + 1)
            link(nc.vector.memset(zero[:, :], 0.0))
            dve.wait_ge(back, 1)
            link(nc.vector.tensor_scalar(pos[:, :], bp[:, :], 0.0, None, ALU.is_gt))
            nc.vector.tensor_scalar(deg[:, :], bp[:, :], 1e-30, None, ALU.max).then_inc(floored, 1)
            dve.wait_ge(rooted, 1)
            link(nc.vector.reciprocal(deg[:, :], deg[:, :]))
            link(nc.vector.tensor_tensor(deg[:, :], deg[:, :], pos[:, :], ALU.mult))
            link(nc.vector.tensor_scalar(c.neg_dis[:, :], deg[:, :], -1.0, None, ALU.mult))
            nc.vector.tensor_copy(wide[:, :, :], bc(deg[:, :], 4)).then_inc(filled, 1)


class Norm:

    def __init__(self, nc, s, c, n, rows=P, tag=""):
        self.nc, self.c, self.n = nc, c, n
        self.sum = s.sb(tag + "ln_sum", [rows, n])
        self.sq = s.sb(tag + "ln_sq", [rows, n, D])
        self.std = s.sb(tag + "ln_std", [rows, n])
        self.std2 = s.sb(tag + "ln_std_twice", [rows, n])
        self.rstd = s.sb(tag + "ln_rstd", [rows, n])
        self.rstd2 = s.sb(tag + "ln_rstd_twice", [rows, n])
        self.var = s.sb(tag + "ln_var", [rows, n])
        self.var_ready, self.rooted = s.sem(tag + "var_ready"), s.sem(tag + "rooted")

    def centre(self, link, y):
        link(self.nc.vector.tensor_reduce(self.sum[:, :], y, AX.X, ALU.add))
        return self.nc.vector.scalar_tensor_tensor(out=y, in0=bc(self.sum[:, :], D), scalar=-1.0 / D, in1=y,
                                                   op0=ALU.mult, op1=ALU.add)

    def variance(self):
        self.nc.vector.tensor_reduce(self.var[:, :], self.sq[:, :, :], AX.X, ALU.add).then_inc(self.var_ready, 1)

    def normalise(self, dve, link, turn, y, out, out2=None):
        v = self.nc.vector
        dve.wait_ge(self.rooted, turn + 1)
        if out2 is not None:
            link.go(v.reciprocal(self.rstd2[:, :], self.std2[:, :]))
        link(v.reciprocal(self.rstd[:, :], self.std[:, :]))
        if out2 is not None:
            link.go(v.tensor_tensor(out2, y, bc(self.rstd2[:, :], D), ALU.mult))
        link(v.tensor_tensor(out, y, bc(self.rstd[:, :], D), ALU.mult))

    def dve(self, dve, link, turn, y, out, out2=None):
        link(self.centre(link, y))
        link(self.nc.vector.tensor_tensor(self.sq[:, :, :], y, y, ALU.mult))
        self.variance()
        self.normalise(dve, link, turn, y, out, out2)

    def root(self, act, turn, twice=False):
        act.wait_ge(self.var_ready, turn + 1)
        if twice:
            self.nc.scalar.activation(self.std2[:, :], self.var[:, :], ACT.Sqrt, bias=self.c.eps_eps[:, :],
                                      scale=(1.0 + EPS) / D)
        self.nc.scalar.activation(self.std[:, :], self.var[:, :], ACT.Sqrt, bias=self.c.eps[0:self.std.shape[0], :],
                                  scale=1.0 / D).then_inc(self.rooted, 1)


def chunk_of(table, first_row, n, words):
    t = table[first_row:first_row + SLOTS, :].rearrange("(p t) k -> p (t k)", p=P)
    return t[:, bass.ds(n * (CT * words), CT * words)]


def flag_chunk(row, n, parts=P):
    return row[bass.ds(n * CW, CW)].rearrange("(a n) -> a n", a=1).to_broadcast([parts, CW])


def flat(t):
    return t.rearrange("p t k -> p (t k)")


def pieces():
    return ((0, 512), (512, CW))


def turn_64(nc, out, rows, ident, waits):
    if waits:
        return nc.tensor.matmul(out, rows, ident[:, :], start=True, stop=True)
    return nc.tensor.transpose(out, rows, ident[:, :])


class Gather:

    def __init__(self, nc, s, jobs, width):
        self.nc, self.jobs = nc, jobs
        self.buf = [s.sb(f"gathered_rows{b}", [P, CT, width]) for b in range(2)]
        self.stage = [[s.sb(f"stage{j}_{b}", [P, CT], I32) for b in range(2)] for j in range(len(jobs))]
        self.gate = s.sb("gate", [P, 2], I32)
        self.gates = s.sem("gates")
        self.staged = [s.sem(f"staged{b}") for b in range(2)]
        self.done = [s.sem(f"gathered{b}") for b in range(2)]
        self.per = 16 * CT * len(jobs)

    def sp(self, sp, n, m, b):
        wait(sp, self.done[b], m * self.per)
        for j, job in enumerate(self.jobs):
            sp.dma_start(self.stage[j][b][:, :], job[1][:, bass.ds(n * CT, CT)]).then_inc(self.staged[b], 16)

    def start(self, pool):
        self.nc.gpsimd.memset(self.gate[:, :], 0).then_inc(self.gates, 1)

    def pool(self, pool, n, m, b):
        pool.wait_ge(self.staged[b], (m + 1) * (16 * len(self.jobs)))
        pass_gate(self.nc, pool, self.gate, self.gates, n + 1)
        for j, (table, _, at, words) in enumerate(self.jobs):
            for k in range(CT):
                self.nc.gpsimd.indirect_dma_start(
                    out=self.buf[b][:, k, at:at + words], out_offset=None, in_=table[:, :],
                    in_offset=bass.IndirectOffsetOnAxis(ap=self.stage[j][b][:, k:k + 1].bitcast(U32), axis=0),
                ).then_inc(self.done[b], 16)

    def wait(self, eng, m, b):
        eng.wait_ge(self.done[b], (m + 1) * self.per)


def load_weights(nc, c, a):
    with Scope(nc, "w_") as s:
        w = s.sb("l1w", [D, 6, D])
        half = s.sb("half", [P, 2, D])
        brow = s.sb("brow", [1, 4, D])
        b0 = s.sb("b0", [1, 8, D])
        biso, b1x = s.sb("biso", [1, 2, D]), s.sb("b1x", [1, 2, D])
        split = [(row_, [s.sb(f"{n}_part{k}", [1, w_], BF16) for k in range(3)], to) for n, row_, w_, to in (
            ("b0", b0, 8 * D, c.b0), ("biso", biso, 2 * D, c.biso), ("b1x", b1x, 2 * D, c.b1x))]
        loaded, linked = s.sem("loaded"), s.sem("linked")
        block = s.block()
        W1, W2, WR = a["L0_gnn_W1"], a["L0_gnn_W2"], a["L0_gnn_Wres"]
        loads = []

        def row(v):
            return v.rearrange("(a n) -> a n", a=1)

        src_part = [W1, W2, None, None, W2, None, None, None]
        dst_part = [W1, W2, W1, W2, None, W2, None, WR]
        for k in range(8):
            if src_part[k] is not None:
                loads.append((c.w0[0:D, k, :], src_part[k][:, :]))
            if dst_part[k] is not None:
                loads.append((c.w0[D:P, k, :], dst_part[k][:, :]))
        b1, b2, br = row(a["L0_gnn_b1"]), row(a["L0_gnn_b2"]), row(a["L0_gnn_bres"])
        for k, v in enumerate((b1, b2, b1, b2, b2, b2, br, br)):
            loads.append((b0[0:1, k, :], v))
        m0 = row(a["L0_gnn_m"][0, :, :].rearrange("h k -> (h k)"))
        loads.append((c.m0[:, :], m0.to_broadcast([P, D])))
        for h in range(2):
            loads.append((c.wiso[h * D:(h + 1) * D, h * D:(h + 1) * D], W2[:, :]))
            loads.append((half[h * D:(h + 1) * D, 0, :], WR[:, :]))
            loads.append((b1x[0:1, h, :], row(a["L1_gnn_b"])))
            loads.append((brow[0:1, h, :], b2))
            loads.append((brow[0:1, 2 + h, :], br))
        loads.append((w[:, :, :], a["L1_gnn_W"].rearrange("k i o -> i k o")))
        loads.append((c.w31[:, :], a["L3_gnn_W1"][:, :]))
        loads.append((c.w32[:, :], a["L3_gnn_W2"][:, :]))
        loads.append((c.b31[:, :], a["L3_gnn_b1"].rearrange("(n a) -> n a", a=1)))
        loads.append((c.b32[:, :], row(a["L3_gnn_b2"]).to_broadcast([P, D])))

        zeroed, copied, parted = s.sem("zeroed"), s.sem("copied"), s.sem("parted")

        @block.sync
        def _(sp):
            sp.wait_ge(zeroed, 3)
            for o, v in loads:
                sp.dma_start(o, v).then_inc(loaded, 16)
            sp.wait_ge(copied, 1)
            sp.dma_start(c.w1d[D:P, D:2 * D], c.w1d[0:D, 0:D]).then_inc(loaded, 16)
            sp.wait_ge(parted, 1)
            for _, parts, to in split:
                for k in range(3):
                    sp.dma_start(to[k:k + 1, :], parts[k][:, :]).then_inc(loaded, 16)
            sp.wait_ge(loaded, 16 * (len(loads) + 10))

        @block.vector
        def _(dve):
            link = Link(dve, linked)
            v = nc.vector
            v.memset(c.w0[:, :, :], 0.0).then_inc(zeroed, 1)
            v.memset(c.wiso[:, :], 0.0).then_inc(zeroed, 1)
            v.memset(c.w1d[:, :], 0.0).then_inc(zeroed, 1)
            link(v.memset(c.eps[:, :], EPS))
            link(v.memset(c.eps_eps[:, :], EPS * EPS))
            dve.wait_ge(zeroed, 3)
            dve.wait_ge(loaded, 16 * len(loads))
            link(v.tensor_scalar(c.w0[D:P, 2:4, :], c.w0[D:P, 2:4, :], 2.0, None, ALU.mult))
            link(v.tensor_scalar(b0[:, 0:4, :], b0[:, 0:4, :], 2.0, None, ALU.mult))
            for h in range(2):
                q = c.wiso[h * D:(h + 1) * D, h * D:(h + 1) * D]
                link(v.tensor_tensor(q, q, c.m0[h * D:(h + 1) * D, :], ALU.mult))
                link(v.tensor_tensor(q, q, half[h * D:(h + 1) * D, 0, :], ALU.add))
                link(v.tensor_tensor(biso[:, h, :], brow[:, h, :], c.m0[0:1, :], ALU.mult))
                link(v.tensor_tensor(biso[:, h, :], biso[:, h, :], brow[:, 2 + h, :], ALU.add))
            link(v.tensor_copy(c.w0[0:D, 6, :], c.wiso[0:D, 0:D]))
            link(v.tensor_copy(b0[:, 6, :], biso[:, 0, :]))
            link(v.memset(c.ones3[:, :], 1.0))
            for row_, parts, _ in split:
                for k in range(3):
                    link(v.tensor_copy(parts[k][:, :], flat(row_[:, :, :])))
                    if k < 2:
                        link(v.tensor_tensor(flat(row_[:, :, :]), flat(row_[:, :, :]), parts[k][:, :], ALU.subtract))
            v.tensor_copy(brow[:, 0, 0:1], b0[:, 0, 0:1]).then_inc(parted, 1)
            link(v.tensor_tensor(c.w1d[0:D, 0:D], w[:, 0, :], w[:, 2, :], ALU.subtract))
            v.tensor_tensor(c.w1d[0:D, 0:D], c.w1d[0:D, 0:D], w[:, 4, :], ALU.add).then_inc(copied, 1)
            link(v.tensor_tensor(c.wp[:, 0, D:], w[:, 1, :], w[:, 3, :], ALU.subtract))
            link(v.tensor_tensor(c.wp[:, 0, D:], c.wp[:, 0, D:], w[:, 5, :], ALU.add))
            for k, hi in ((1, 4), (2, 5)):
                link(v.tensor_tensor(c.wp[:, k, D:], w[:, k + 1, :], w[:, hi, :], ALU.subtract))
                link(v.tensor_scalar(c.wp[:, k, D:], c.wp[:, k, D:], 2.0, None, ALU.mult))
            for k in (3, 4):
                link(v.tensor_scalar(c.wp[:, k, D:], w[:, k + 1, :], 2.0, None, ALU.mult))
            for k in range(5):
                link(v.tensor_copy(c.wp[:, k, 0:D], c.ident[0:D, 0:D]))


def attention_sums(nc, c, x, same, stash, d_table, x1_table, small):
    H0 = 4
    EARLY = 1
    with Scope(nc, "att_") as s:
        ends = Gather(nc, s, [(x, c.idx["bs"], 0, D), (x, c.idx["bd"], D, D)], 2 * D)
        xb = ends.buf
        fl = [s.sb(f"same{b}", [P, CW]) for b in range(2)]
        xn = s.sb("normed", [P, CT, 2 * D])
        low, high_, rng = (s.sb(n, [P, 2 * CT]) for n in ("low", "high", "range"))
        xnT = s.sb("normedT", [P, CW])
        sg = s.sb("sigmoid", [P, CT, 4 * D])
        eb = [s.sb(f"exps{b}", [P, CT, 4 * D]) for b in range(2)]
        rr = [s.sb(f"rest{b}", [P, CT, 3 * D]) for b in range(2)]
        sca, scb = s.sb("scan_a", [P, CW]), s.sb("scan_b", [D, CW])
        t1 = s.sb("t1", [P, CT, D])
        sl, sr = s.sb("sum_l", [P, CT, D]), s.sb("sum_r", [P, CT, D])
        both = s.sb("sum_product", [P, CT, D])
        sq = s.sb("squares", [P, CT, D])
        total, std, rstd = (s.sb(n, [P, CT]) for n in ("total", "std", "rstd"))
        dv = [s.sb(f"delta{b}", [P, CT, D]) for b in range(2)]
        st = [s.sb(f"stash{b}", [P, CT, 4 * D]) for b in range(2)]
        xs1 = [s.sb(f"x1_src{b}", [P, CT, D]) for b in range(2)]
        zero = s.sb("zero_row", [1, D])
        g = SmallGather(nc, s, small)
        pT = s.ps("pT", [P, 512])
        q = [s.ps(f"q{k}", [P, 512]) for k in range(2)]
        pA = s.ps("pA", [P, 1024])
        pB = s.ps("pB", [P, 1024])
        flagged = [s.sem(f"flagged{b}") for b in range(2)]
        stored = [s.sem(f"stored{b}") for b in range(2)]
        (normed, turned, evac, product, read, expd, fed, rested, turned2, scanned, back, centred, squared, summed, rooted,
         finished, linked, zeroed) = (
            s.sem(n) for n in ("normed", "turned", "evac", "product", "read", "expd", "fed", "rested", "turned2", "scanned",
                               "back", "centred", "squared", "summed", "rooted", "finished", "linked", "zeroed"))
        block = s.block()

        @block.sync
        def _(sp):
            sp.wait_ge(zeroed, 1)
            sp.dma_start(d_table[ZERO:ZERO + 1, :], zero[:, :]).then_inc(zeroed, 16)

            def flags(n, m, b):
                wait(sp, scanned, n - 1)
                sp.dma_start(fl[b][:, :], flag_chunk(same, n)).then_inc(flagged[b], 16)

            staged(sp, NCH, [(0, lambda n, m, b: ends.sp(sp, n, m, b)), (2, flags), (3, g.take)])
            sp.wait_ge(zeroed, 17)
            g.end(sp)
            for b in range(2):
                sp.wait_ge(stored[b], 48 * PAIRS)

        @block.gpsimd
        def _(pool):
            g.start(pool)
            ends.start(pool)

            def gather_ends(n, m, b):
                wait(pool, rested, n - 1)
                ends.pool(pool, n, m, b)
            staged(pool, NCH, [(0, gather_ends), (2, g.gather)])

        @block.tensor
        def _(pe):
            def turn(n, m, b):
                pe.wait_ge(normed, n + 1)
                for h, (k0, k1) in enumerate(((0, H0), (H0, CT))):
                    wait(pe, evac, 2 * n + h)
                    for k in range(k0, k1):
                        mm = nc.tensor.transpose(pT[:, (k - k0) * P:(k - k0 + 1) * P], xn[:, k, :], c.ident[:, :])
                    mm.then_inc(turned, 1)

            def multiply(n, b, k0, k1):
                pe.wait_ge(evac, 2 * n + (1 if k1 <= H0 else 2))
                for k in range(k0, k1):
                    t = n * CT + k
                    wait(pe, read, t - 1)
                    par = (b * CT + k) % 2
                    nc.tensor.matmul(q[par][:, :], xnT[:, k * P:(k + 1) * P], c.w0[:, :, :].rearrange("p a b -> p (a b)"),
                                     start=True, stop=False)
                    nc.tensor.matmul(q[par][:, :], c.ones3[:, :], c.b0[:, :], start=False, stop=True).then_inc(product, 1)

            def turn_exps(n, m, b):
                pe.wait_ge(fed, n + 1)
                for k in range(CT):
                    nc.tensor.transpose(pA[:, k * P:(k + 1) * P], eb[b][:, k, 0:2 * D], c.ident[:, :])
                    mm = nc.tensor.transpose(pB[0:D, k * P:(k + 1) * P], st[b][:, k, 0:D], c.ident[:, :])
                mm.then_inc(turned2, 1)

            def turn_back(n, m, b):
                pe.wait_ge(scanned, n + 1)
                for k in range(CT):
                    nc.tensor.transpose(pA[:, k * P:(k + 1) * P], sca[:, k * P:(k + 1) * P], c.ident[:, :])
                    mm = nc.tensor.transpose(pB[:, k * D:(k + 1) * D], scb[:, k * P:(k + 1) * P], c.ident[0:D, 0:D])
                mm.then_inc(back, 1)

            staged(pe, NCH, [(0, turn), (0, lambda n, m, b: multiply(n, b, 0, EARLY)), (1, turn_back),
                             (0, lambda n, m, b: multiply(n, b, EARLY, CT)), (0, turn_exps)])

        @block.scalar
        def _(act):
            def evacuate(h, n):
                k0, k1 = ((0, H0), (H0, CT))[h]
                act.wait_ge(turned, 2 * n + h + 1)
                wait(act, product, n * CT)
                nc.scalar.activation(xnT[:, k0 * P:k1 * P], pT[:, 0:(k1 - k0) * P], ACT.Copy).then_inc(evac, 1)

            def square(n, m, b):
                act.wait_ge(centred, n + 1)
                nc.scalar.activation(sq[:, :, :], rr[b][:, :, D:2 * D], ACT.Square).then_inc(squared, 1)

            def root(n, m, b):
                act.wait_ge(summed, n + 1)
                nc.scalar.activation(std[:, :], std[:, :], ACT.Sqrt, bias=c.eps[:, :], scale=1.0 / D).then_inc(rooted, 1)

            def read_product(n, m, b):
                wait(act, expd, 3 * n)
                wait(act, finished, n - 1)
                wait(act, stored[b], m * 48)
                for k in range(CT):
                    par = (b * CT + k) % 2
                    act.wait_ge(product, n * CT + k + 1)
                    nc.scalar.activation(sg[:, k, :], q[par][:, 0:4 * D], ACT.Sigmoid)
                    nc.scalar.activation(st[b][:, k, D:2 * D], q[par][:, 4 * D:5 * D], ACT.Copy)
                    nc.scalar.activation(rr[b][:, k, :], q[par][:, 5 * D:8 * D], ACT.Copy).then_inc(read, 1)
                act.wait_ge(read, n * CT + CT)
                nc.scalar.activation(eb[b][:, :, D:2 * D], sg[:, :, 0:D], ACT.Exp).then_inc(expd, 1)
                nc.scalar.activation(st[b][:, :, 0:D], sg[:, :, D:2 * D], ACT.Exp).then_inc(expd, 1)
                nc.scalar.activation(eb[b][:, :, 2 * D:4 * D], sg[:, :, 2 * D:4 * D], ACT.Exp).then_inc(expd, 1)

            def store(n, m, b):
                act.wait_ge(finished, n + 1)
                act.dma_start(chunk_of(d_table, 0, n, D), flat(dv[b][:, :, :])).then_inc(stored[b], 16)
                act.dma_start(chunk_of(stash, 0, n, 4 * D), flat(st[b][:, :, :])).then_inc(stored[b], 16)
                act.dma_start(chunk_of(x1_table, SLOTS, n, D), flat(xs1[b][:, :, :])).then_inc(stored[b], 16)

            staged(act, NCH, [(0, lambda n, m, b: g.stage(n, m, b, act)), (2, store), (0, lambda n, m, b: evacuate(0, n)), (1, square),
                              (0, lambda n, m, b: evacuate(1, n)),
                              (1, root), (0, read_product)])

        @block.vector
        def _(dve):
            link = Link(dve, linked)
            v = nc.vector
            link(v.memset(sca[:, CW - 1:CW], 0.0))
            link(v.memset(scb[:, CW - 1:CW], 0.0))
            v.memset(zero[:, :], 0.0).then_inc(zeroed, 1)
            m0 = c.m0[:, :].unsqueeze(1).to_broadcast([P, CT, D])

            def scale(n, m, b):
                ends.wait(dve, m, b)
                x2 = xb[b][:, :, :].rearrange("p t (e k) -> p (t e) k", e=2)
                n2 = xn[:, :, :].rearrange("p t (e k) -> p (t e) k", e=2)
                link.go(v.tensor_reduce(low[:, :], x2, AX.X, ALU.min))
                link(v.tensor_reduce(high_[:, :], x2, AX.X, ALU.max))
                link.go(v.scalar_tensor_tensor(out=rng[:, :], in0=high_[:, :], scalar=EPS, in1=low[:, :],
                                               op0=ALU.add, op1=ALU.subtract))
                wait(dve, turned, 2 * n)
                link(v.tensor_tensor(n2, x2, bc(low[:, :], D), ALU.subtract))
                link(v.reciprocal(rng[:, :], rng[:, :]))
                v.tensor_tensor(n2, n2, bc(rng[:, :], D), ALU.mult).then_inc(normed, 1)

            def centre_sources(n, m, b):
                y = rr[b][:, :, D:2 * D]
                link(v.tensor_reduce(total[:, :], y, AX.X, ALU.add))
                v.scalar_tensor_tensor(out=y, in0=bc(total[:, :], D), scalar=-1.0 / D, in1=y,
                                       op0=ALU.mult, op1=ALU.add).then_inc(centred, 1)

            def scan(n, m, b):
                dve.wait_ge(turned2, n + 1)
                dve.wait_ge(flagged[b], m * 16 + 16)
                link.go(v.tensor_tensor_scan(out=sca[:, :], data0=fl[b][:, :], data1=pA[:, 0:CW], initial=sca[:, CW - 1:CW],
                                             op0=ALU.mult, op1=ALU.add))
                v.tensor_tensor_scan(out=scb[:, :], data0=fl[b][0:D, :], data1=pB[0:D, 0:CW], initial=scb[:, CW - 1:CW],
                                     op0=ALU.mult, op1=ALU.add).then_inc(scanned, 1)
                dve.wait_ge(scanned, n + 1)

            def normalise_sources(n, m, b):
                dve.wait_ge(squared, n + 1)
                v.tensor_reduce(std[:, :], sq[:, :, :], AX.X, ALU.add).then_inc(summed, 1)
                link(v.tensor_tensor(t1[:, :, :], eb[b][:, :, 2 * D:3 * D], rr[b][:, :, 0:D], ALU.mult))
                dve.wait_ge(rooted, n + 1)
                link(v.reciprocal(rstd[:, :], std[:, :]))
                wait(dve, stored[b], m * 48)
                link(v.tensor_tensor(xs1[b][:, :, :], rr[b][:, :, D:2 * D], bc(rstd[:, :], D), ALU.mult))

            def conclude(n, m, b):
                rd, res = rr[b][:, :, 0:D], rr[b][:, :, 2 * D:3 * D]
                sel, ser = eb[b][:, :, 2 * D:3 * D], eb[b][:, :, 3 * D:4 * D]
                w3, rest = st[b][:, :, 2 * D:3 * D], st[b][:, :, 3 * D:4 * D]
                dve.wait_ge(back, n + 1)
                back_a = pA[:, 0:CW].rearrange("p (t k) -> p t k", k=P)
                back_b = pB[:, 0:CT * D].rearrange("p (t k) -> p t k", k=D)
                link.go(v.tensor_tensor(t1[:, :, :], back_a[:, :, 0:D], t1[:, :, :], ALU.add))
                link.go(v.tensor_tensor(sl[:, :, :], back_a[:, :, D:P], sel, ALU.add))
                link(v.tensor_tensor(sr[:, :, :], back_b, ser, ALU.add))
                link(v.tensor_tensor(both[:, :, :], sl[:, :, :], sr[:, :, :], ALU.mult))
                link.go(v.tensor_tensor(t1[:, :, :], t1[:, :, :], sr[:, :, :], ALU.mult))
                link.go(v.tensor_tensor(w3, sl[:, :, :], m0, ALU.mult))
                link(v.reciprocal(both[:, :, :], both[:, :, :]))
                link.go(v.tensor_tensor(t1[:, :, :], t1[:, :, :], both[:, :, :], ALU.mult))
                link(v.tensor_tensor(w3, w3, both[:, :, :], ALU.mult))
                link.go(v.tensor_tensor(dv[b][:, :, :], t1[:, :, :], rd, ALU.subtract))
                link(v.tensor_tensor(sl[:, :, :], t1[:, :, :], ser, ALU.mult))
                link(v.tensor_tensor(sl[:, :, :], sl[:, :, :], w3, ALU.mult))
                v.tensor_tensor(rest, sl[:, :, :], res, ALU.add).then_inc(finished, 1)
                dve.wait_ge(finished, n + 1)

            def weigh(n, m, b):
                dve.wait_ge(expd, 3 * n + 3)
                v.tensor_tensor(eb[b][:, :, 0:D], eb[b][:, :, D:2 * D], st[b][:, :, D:2 * D], ALU.mult).then_inc(fed, 1)
                v.tensor_tensor(rr[b][:, :, D:3 * D], rr[b][:, :, D:3 * D], xb[b][:, :, :], ALU.add).then_inc(rested, 1)
                dve.wait_ge(rested, n + 1)
            staged(dve, NCH, [(0, scale), (1, centre_sources), (1, scan), (1, normalise_sources), (1, conclude), (0, weigh)],
                   [link])


def attention_out(nc, c, same, stash, d_table, x1_table):
    with Scope(nc, "ato_") as s:
        g = Gather(nc, s, [(d_table, c.idx["b1"], 0, D)], D)
        st = [s.sb(f"weights{b}", [P, CT, 2 * D]) for b in range(2)]
        sr = [s.sb(f"rest{b}", [P, CT, 2 * D]) for b in range(2)]
        fl = [s.sb(f"same{b}", [D, CW]) for b in range(2)]
        msg = [s.sb(f"messages{b}", [P, CT, D]) for b in range(2)]
        sc = s.sb("scan", [D, CW])
        y = s.sb("y", [P, CT, D])
        o = [s.sb(f"out{b}", [P, CT, D]) for b in range(2)]
        norm = Norm(nc, s, c, CT)
        pT = [s.ps(f"pT{b}", [D, 1024]) for b in range(2)]
        pR = [s.ps(f"pR{b}", [P, 512]) for b in range(2)]
        loaded, flagged, rest_in, stored = ([s.sem(f"{n}{b}") for b in range(2)] for n in
                                            ("loaded", "flagged", "rest_in", "stored"))
        fed, turned, scanned, back, finished, linked = (s.sem(n) for n in ("fed", "turned", "scanned", "back", "finished", "linked"))
        block = s.block()
        stash3 = stash.rearrange("(p t) k -> p t k", p=P)

        @block.sync
        def _(sp):
            def early(n, m, b):
                g.sp(sp, n, m, b)
                wait(sp, fed, n - 1)
                sp.dma_start(st[b][:, :, :], stash3[:, bass.ds(n * CT, CT), 0:2 * D]).then_inc(loaded[b], 16)

            def flags(n, m, b):
                wait(sp, scanned, n - 1)
                sp.dma_start(fl[b][:, :], flag_chunk(same, n, D)).then_inc(flagged[b], 16)

            def rest(n, m, b):
                wait(sp, finished, n - 1)
                sp.dma_start(sr[b][:, :, :], stash3[:, bass.ds(n * CT, CT), 2 * D:4 * D]).then_inc(rest_in[b], 16)
            staged(sp, NCH, [(0, early), (2, flags), (3, rest)])

        @block.gpsimd
        def _(pool):
            g.start(pool)

            def body(n, m, b):
                wait(pool, fed, n - 1)
                g.pool(pool, n, m, b)
            staged(pool, NCH, [(0, body)])

        @block.tensor
        def _(pe):
            def turn(n, m, b):
                pe.wait_ge(fed, n + 1)
                wait(pe, scanned, n - 1)
                for k in range(CT):
                    mm = turn_64(nc, pT[b][:, k * P:(k + 1) * P], msg[b][:, k, :], c.ident, k == 0)
                mm.then_inc(turned, 1)

            def rows(n, m, b):
                pe.wait_ge(scanned, n + 1)
                wait(pe, finished, n - 1)
                for k in range(CT):
                    mm = nc.tensor.matmul(pR[b][:, k * D:(k + 1) * D], sc[:, k * P:(k + 1) * P], c.ident[0:D, 0:D], start=True, stop=True)
                mm.then_inc(back, 1)
            staged(pe, NCH, [(0, turn), (1, rows)])

        @block.scalar
        def _(act):
            def body(n, m, b):
                norm.root(act, n)
                act.wait_ge(finished, n + 1)
                act.dma_start(chunk_of(x1_table, 0, n, D), flat(o[b][:, :, :])).then_inc(stored[b], 16)
            staged(act, NCH, [(0, body)])
            for b in range(2):
                act.wait_ge(stored[b], 16 * PAIRS)

        @block.vector
        def _(dve):
            link = Link(dve, linked)
            v = nc.vector
            link(v.memset(sc[:, CW - 1:CW], 0.0))

            def messages(n, m, b):
                g.wait(dve, m, b)
                dve.wait_ge(loaded[b], m * 16 + 16)
                t = msg[b][:, :, :]
                link(v.tensor_tensor(t, g.buf[b][:, :, :], st[b][:, :, D:2 * D], ALU.add))
                v.tensor_tensor(t, t, st[b][:, :, 0:D], ALU.mult).then_inc(fed, 1)

            def scan(n, m, b):
                dve.wait_ge(turned, n + 1)
                dve.wait_ge(flagged[b], m * 16 + 16)
                wait(dve, back, n)
                v.tensor_tensor_scan(out=sc[:, :], data0=fl[b][:, :], data1=pT[b][:, 0:CW], initial=sc[:, CW - 1:CW],
                                     op0=ALU.mult, op1=ALU.add).then_inc(scanned, 1)
                dve.wait_ge(scanned, n + 1)

            def conclude(n, m, b):
                wait(dve, stored[b], m * 16)
                dve.wait_ge(rest_in[b], m * 16 + 16)
                dve.wait_ge(back, n + 1)
                rows = pR[b][:, 0:CT * D].rearrange("p (t k) -> p t k", k=D)
                link(v.tensor_tensor(y[:, :, :], rows, sr[b][:, :, 0:D], ALU.mult))
                link(v.tensor_tensor(y[:, :, :], y[:, :, :], sr[b][:, :, D:2 * D], ALU.add))
                norm.dve(dve, link, n, y[:, :, :], o[b][:, :, :])
                v.tensor_copy(y[:, 0, 0:1], o[b][:, 0, 0:1]).then_inc(finished, 1)
                dve.wait_ge(finished, n + 1)
            staged(dve, NCH, [(0, messages), (1, scan), (2, conclude)], [link])


def chebyshev_start(nc, c, x1_table, t0_src, x2_table, same, p_out):
    with Scope(nc, "ch0_") as s:
        g = Gather(nc, s, [(x1_table, c.idx["a3"], 0, D), (x1_table, c.idx["a2"], D, D)], 2 * D)
        fl = [s.sb(f"same{b}", [D, CW]) for b in range(2)]
        xT = s.sb("rowsT", [P, CW])
        y = s.sb("y", [P, CT, D])
        o = [s.sb(f"out{b}", [P, CT, D]) for b in range(2)]
        msg = s.sb("messages", [P, CT, D])
        sc = s.sb("scan", [D, CW])
        po = [s.sb(f"propagated{b}", [P, CT, D]) for b in range(2)]
        tmp = s.sb("product_part", [P, CT, D])
        norm = Norm(nc, s, c, CT)
        pT = s.ps("pT", [P, 1024])
        pR = s.ps("pR", [P, 1024])
        pM = s.ps("messagesT", [D, 1024])
        pB = s.ps("sums", [P, 1024])
        loaded = [s.sem(f"loaded{b}") for b in range(2)]
        stored = [s.sem(f"stored{b}") for b in range(2)]
        kept = [s.sem(f"kept{b}") for b in range(2)]
        turned, evac, product, fed, msg_turned, scanned, back, finished, linked = (
            s.sem(n) for n in ("turned", "evac", "product", "fed", "msg_turned", "scanned", "back", "finished", "linked"))
        block = s.block()
        t0v = t0_src.rearrange("(p t) k -> p t k", p=P)

        @block.sync
        def _(sp):
            def flags(n, m, b):
                wait(sp, scanned, n - 1)
                sp.dma_start(fl[b][:, :], flag_chunk(same, n, D)).then_inc(loaded[b], 16)
            staged(sp, NCH, [(0, lambda n, m, b: g.sp(sp, n, m, b)), (2, flags)])

        @block.gpsimd
        def _(pool):
            g.start(pool)

            def body(n, m, b):
                wait(pool, turned, n - 1)
                wait(pool, fed, n - 1)
                wait(pool, kept[b], m * 16)
                g.pool(pool, n, m, b)
            staged(pool, NCH, [(0, body)])

        @block.tensor
        def _(pe):
            def turn(n, m, b):
                g.wait(pe, m, b)
                wait(pe, evac, n)
                for k in range(CT):
                    mm = nc.tensor.transpose(pT[:, k * P:(k + 1) * P], g.buf[b][:, k, :], c.ident[:, :])
                mm.then_inc(turned, 1)

            def multiply(n, m, b):
                pe.wait_ge(evac, n + 1)
                wait(pe, finished, n)
                for k in range(CT):
                    nc.tensor.matmul(pR[:, k * P:(k + 1) * P], xT[:, k * P:(k + 1) * P], c.w1d[:, :], start=True, stop=False)
                    mm = nc.tensor.matmul(pR[:, k * P:(k + 1) * P], c.ones3[:, :], c.b1x[:, :], start=False, stop=True)
                mm.then_inc(product, 1)

            def turn_messages(n, m, b):
                pe.wait_ge(fed, n + 1)
                for k in range(CT):
                    mm = turn_64(nc, pM[:, k * P:(k + 1) * P], msg[:, k, :], c.ident, k == 0)
                mm.then_inc(msg_turned, 1)

            def rows(n, m, b):
                pe.wait_ge(scanned, n + 1)
                wait(pe, finished, n)
                for k in range(CT):
                    mm = nc.tensor.matmul(pB[:, k * P:(k + 1) * P], sc[:, k * P:(k + 1) * P], c.wp[:, 0, :], start=True, stop=True)
                mm.then_inc(back, 1)
            staged(pe, NCH, [(1, rows), (0, turn), (0, turn_messages), (0, multiply)])

        @block.scalar
        def _(act):
            def evacuate(n, m, b):
                act.wait_ge(turned, n + 1)
                wait(act, product, n)
                nc.scalar.activation(xT[:, :], pT[:, 0:CW], ACT.Copy).then_inc(evac, 1)
                g.wait(act, m, b)
                act.dma_start(t0v[:, bass.ds(n * CT, CT), :], g.buf[b][:, :, 0:D]).then_inc(kept[b], 16)

            def store(n, m, b):
                norm.root(act, n)
                act.wait_ge(finished, n + 1)
                act.dma_start(chunk_of(x2_table, 2 * SLOTS, n, D), flat(o[b][:, :, :])).then_inc(stored[b], 16)
                act.dma_start(chunk_of(p_out, 0, n, D), flat(po[b][:, :, :])).then_inc(stored[b], 16)
            staged(act, NCH, [(0, evacuate), (1, store)])
            for b in range(2):
                act.wait_ge(kept[b], 16 * PAIRS)
                act.wait_ge(stored[b], 32 * PAIRS)

        @block.vector
        def _(dve):
            link = Link(dve, linked)
            v = nc.vector
            link(v.memset(sc[:, CW - 1:CW], 0.0))

            def messages(n, m, b):
                g.wait(dve, m, b)
                t_here = flat(c.t_even[:, :, :])[:, bass.ds(n * (CT * D), CT * D)].rearrange("p (t k) -> p t k", k=D)
                link.go(v.tensor_scalar(t_here, g.buf[b][:, :, D:2 * D], 1.0, None, ALU.mult))
                v.tensor_tensor(msg[:, :, :], g.buf[b][:, :, D:2 * D],
                                bc(c.norm[:, bass.ds(n * CT, CT)], D), ALU.mult).then_inc(fed, 1)

            def scan(n, m, b):
                dve.wait_ge(msg_turned, n + 1)
                dve.wait_ge(loaded[b], m * 16 + 16)
                v.tensor_tensor_scan(out=sc[:, :], data0=fl[b][:, :], data1=pM[:, 0:CW], initial=sc[:, CW - 1:CW],
                                     op0=ALU.mult, op1=ALU.add).then_inc(scanned, 1)
                dve.wait_ge(scanned, n + 1)

            def first_product(n, m, b):
                dve.wait_ge(product, n + 1)
                wait(dve, stored[b], m * 32)
                rows = pR[:, 0:CW].rearrange("p (t k) -> p t k", k=P)
                at = bass.ds(n * (CT * D), CT * D)
                link.go(v.tensor_scalar(flat(c.acc[:, :, :])[:, at].rearrange("p (t k) -> p t k", k=D), rows[:, :, 0:D], 1.0, None, ALU.mult))
                link(v.scalar_tensor_tensor(out=y[:, :, :], in0=rows[:, :, D:P], scalar=0.0,
                                            in1=flat(c.t_even[:, :, :])[:, at].rearrange("p (t k) -> p t k", k=D),
                                            op0=ALU.max, op1=ALU.add))
                norm.dve(dve, link, n, y[:, :, :], o[b][:, :, :])

            def sums(n, m, b):
                dve.wait_ge(back, n + 1)
                got = pB[:, 0:CW].rearrange("p (t k) -> p t k", k=P)
                nd = bc(c.neg_dis[:, bass.ds(n * CT, CT)], D)
                link.go(v.tensor_tensor(po[b][:, :, :], got[:, :, 0:D], nd, ALU.mult))
                link(v.tensor_tensor(tmp[:, :, :], got[:, :, D:P], nd, ALU.mult))
                acc = flat(c.acc[:, :, :])[:, bass.ds(n * (CT * D), CT * D)]
                v.tensor_tensor(acc, acc, flat(tmp[:, :, :]), ALU.add).then_inc(finished, 1)
                dve.wait_ge(finished, n + 1)
            staged(dve, NCH, [(1, scan), (0, messages), (1, first_product), (1, sums)], [link])


def chebyshev_hop(nc, c, k_hop, same, p_in, p_out, t0_src, x2_table, x3_table):
    last_hop = k_hop == 4
    with Scope(nc, f"hop{k_hop}_") as s:
        g = Gather(nc, s, [(p_in, c.idx["a4"], 0, D)], D)
        fl = [s.sb(f"same{b}", [D, CW]) for b in range(2)]
        msg = [s.sb(f"messages{b}", [P, CT, D]) for b in range(2)]
        sc = s.sb("scan", [D, CW])
        if last_hop:
            t0 = [s.sb(f"t0_{b}", [P, CT, D]) for b in range(2)]
            y = [s.sb(f"y{b}", [P, CT, D]) for b in range(2)]
            norm = Norm(nc, s, c, CT)
            tables = ((x2_table, SLOTS), (x3_table, SLOTS), (x2_table, 0))
        else:
            tables = ((p_out, 0),)
        o = [[s.sb(f"out{j}_{b}", [P, CT, D]) for j in range(len(tables))] for b in range(2)]
        part = y if last_hop else [s.sb("product", [P, CT, D])] * 2
        pT = [s.ps(f"pT{b}", [D, 1024]) for b in range(2)]
        pR = [s.ps(f"pR{b}", [P, 1024]) for b in range(2)]
        loaded = [s.sem(f"loaded{b}") for b in range(2)]
        own_in = [s.sem(f"own_in{b}") for b in range(2)]
        stored = [s.sem(f"stored{b}") for b in range(2)]
        fed, turned, scanned, back, summed, squared, finished, linked = (
            s.sem(n) for n in ("fed", "turned", "scanned", "back", "summed", "squared", "finished", "linked"))
        t_here = c.t_odd if k_hop % 2 else c.t_even
        block = s.block()

        @block.sync
        def _(sp):
            def flags(n, m, b):
                wait(sp, scanned, n - 1)
                sp.dma_start(fl[b][:, :], flag_chunk(same, n, D)).then_inc(loaded[b], 16)

            def own_rows(n, m, b):
                wait(sp, summed, n - 1)
                sp.dma_start(flat(t0[b][:, :, :]), chunk_of(t0_src, 0, n, D)).then_inc(own_in[b], 16)
            staged(sp, NCH, [(0, lambda n, m, b: g.sp(sp, n, m, b)), (2, flags)] + ([(3, own_rows)] if last_hop else []))

        @block.gpsimd
        def _(pool):
            g.start(pool)

            def body(n, m, b):
                wait(pool, fed, n - 1)
                g.pool(pool, n, m, b)
            staged(pool, NCH, [(0, body)])

        @block.tensor
        def _(pe):
            def turn(n, m, b):
                pe.wait_ge(fed, n + 1)
                wait(pe, scanned, n - 1)
                for k in range(CT):
                    mm = turn_64(nc, pT[b][:, k * P:(k + 1) * P], msg[b][:, k, :], c.ident, k == 0)
                mm.then_inc(turned, 1)

            def rows(n, m, b):
                pe.wait_ge(scanned, n + 1)
                wait(pe, summed if last_hop else finished, n - 1)
                for k in range(CT):
                    mm = nc.tensor.matmul(pR[b][:, k * P:(k + 1) * P], sc[:, k * P:(k + 1) * P], c.wp[:, k_hop, :], start=True, stop=True)
                mm.then_inc(back, 1)
            staged(pe, NCH, [(0, turn), (1, rows)])

        @block.scalar
        def _(act):
            def square(n, m, b):
                act.wait_ge(summed, n + 1)
                nc.scalar.activation(norm.sq[:, :, :], y[b][:, :, :], ACT.Square).then_inc(squared, 1)

            def store(n, m, b):
                act.wait_ge(finished, n + 1)
                for j, (table, first) in enumerate(tables):
                    act.dma_start(chunk_of(table, first, n, D), flat(o[b][j][:, :, :])).then_inc(stored[b], 16)
            if last_hop:
                staged(act, NCH, [(1, lambda n, m, b: norm.root(act, n, twice=True)), (0, square), (1, store)])
            else:
                staged(act, NCH, [(0, store)])
            for b in range(2):
                act.wait_ge(stored[b], 16 * len(tables) * PAIRS)

        @block.vector
        def _(dve):
            link = Link(dve, linked)
            v = nc.vector
            link(v.memset(sc[:, CW - 1:CW], 0.0))

            def messages(n, m, b):
                at = bass.ds(n * (CT * D), CT * D)
                here = flat(t_here[:, :, :])[:, at]
                if k_hop == 1:
                    g.wait(dve, m, b)
                    link(v.tensor_scalar(here, flat(g.buf[b][:, :, :]), 1.0, None, ALU.mult))
                elif k_hop > 1:
                    g.wait(dve, m, b)
                    link(v.scalar_tensor_tensor(out=here, in0=flat(g.buf[b][:, :, :]), scalar=2.0, in1=here,
                                                op0=ALU.mult, op1=ALU.subtract))
                v.tensor_tensor(msg[b][:, :, :], here.rearrange("p (t k) -> p t k", k=D),
                                bc(c.norm[:, bass.ds(n * CT, CT)], D), ALU.mult).then_inc(fed, 1)

            def scan(n, m, b):
                dve.wait_ge(turned, n + 1)
                dve.wait_ge(loaded[b], m * 16 + 16)
                wait(dve, back, n)
                v.tensor_tensor_scan(out=sc[:, :], data0=fl[b][:, :], data1=pT[b][:, 0:CW], initial=sc[:, CW - 1:CW],
                                     op0=ALU.mult, op1=ALU.add).then_inc(scanned, 1)
                dve.wait_ge(scanned, n + 1)

            def sums(n, m, b):
                if not last_hop:
                    wait(dve, stored[b], m * 16)
                dve.wait_ge(back, n + 1)
                got = pR[b][:, 0:CW].rearrange("p (t k) -> p t k", k=P)
                nd = bc(c.neg_dis[:, bass.ds(n * CT, CT)], D)
                tmp = part[b][:, :, :]
                acc = flat(c.acc[:, :, :])[:, bass.ds(n * (CT * D), CT * D)]
                if not last_hop:
                    link.go(v.tensor_tensor(o[b][0][:, :, :], got[:, :, 0:D], nd, ALU.mult))
                link(v.tensor_tensor(tmp, got[:, :, D:P], nd, ALU.mult))
                if last_hop:
                    dve.wait_ge(own_in[b], m * 16 + 16)
                    link(v.tensor_tensor(flat(tmp), acc, flat(tmp), ALU.add))
                    link(v.scalar_tensor_tensor(out=y[b][:, :, :], in0=tmp, scalar=0.0, in1=t0[b][:, :, :],
                                                op0=ALU.max, op1=ALU.add))
                    norm.centre(link, y[b][:, :, :]).then_inc(summed, 1)
                else:
                    v.tensor_tensor(acc, acc, flat(tmp), ALU.add).then_inc(finished, 1)
                    dve.wait_ge(finished, n + 1)

            def variance(n, m, b):
                dve.wait_ge(squared, n + 1)
                norm.variance()

            def normalise(n, m, b):
                wait(dve, stored[b], m * 48)
                norm.normalise(dve, link, n, y[b][:, :, :], o[b][0][:, :, :], o[b][1][:, :, :])
                v.tensor_tensor(o[b][2][:, :, :], o[b][0][:, :, :], bc(c.inv_out[:, bass.ds(n * CT, CT)], D),
                                ALU.mult).then_inc(finished, 1)
            if last_hop:
                staged(dve, NCH, [(3, variance), (0, messages), (1, scan), (2, sums), (3, normalise)], [link])
            else:
                staged(dve, NCH, [(0, messages), (1, scan), (2, sums)], [link])


class Scatter:

    def __init__(self, nc, s, out, index):
        self.nc, self.out, self.index = nc, out, index
        self.buf = [s.sb(f"final_rows{b}", [P, CT, D]) for b in range(2)]
        self.stage = [s.sb(f"target{b}", [P, CT], I32) for b in range(2)]
        self.gate = s.sb("gate_out", [P, 2], I32)
        self.gates = s.sem("gates_out")
        self.staged = [s.sem(f"targets{b}") for b in range(2)]
        self.done = [s.sem(f"scattered{b}") for b in range(2)]
        self.per = 16 * CT

    def targets(self, act, n, m, b):
        wait(act, self.done[b], m * self.per)
        act.dma_start(self.stage[b][:, :], self.index[:, bass.ds(n * CT, CT)]).then_inc(self.staged[b], 16)

    def start(self, pool):
        self.nc.gpsimd.memset(self.gate[:, :], 0).then_inc(self.gates, 1)

    def pool(self, pool, n, m, b):
        pool.wait_ge(self.staged[b], m * 16 + 16)
        pass_gate(self.nc, pool, self.gate, self.gates, n + 1)
        for k in range(CT):
            self.nc.gpsimd.indirect_dma_start(
                out=self.out[:, :], out_offset=bass.IndirectOffsetOnAxis(ap=self.stage[b][:, k:k + 1].bitcast(U32), axis=0),
                in_=self.buf[b][:, k, :], in_offset=None, bounds_check=N - 1, oob_is_err=False).then_inc(self.done[b], 16)


def pool_gather_scatter(pool, g, sc, finished):
    g.start(pool)
    sc.start(pool)

    def gather(n, m, b):
        wait(pool, finished, n - 1)
        g.pool(pool, n, m, b)

    def scatter(n, m, b):
        pool.wait_ge(finished, n + 1)
        sc.pool(pool, n, m, b)
    staged(pool, NCH, [(2, scatter), (0, gather)])
    for b in range(2):
        pool.wait_ge(sc.done[b], sc.per * PAIRS)


def light_layer(nc, c, same, x2_table, x3_table, out):
    with Scope(nc, "lgt_") as s:
        g = Gather(nc, s, [(x2_table, c.idx["b2"], 0, D), (x2_table, c.idx["b3"], D, D)], 2 * D)
        sca = Scatter(nc, s, out, c.out_b)
        fl = [s.sb(f"same{b}", [P, CW]) for b in range(2)]
        sc = s.sb("scan", [D, CW])
        ri = s.sb("root_in", [P, CT])
        y = s.sb("y", [P, CT, D])
        o = [s.sb(f"out{b}", [P, CT, D]) for b in range(2)]
        norm = Norm(nc, s, c, CT)
        pT = s.ps("pT", [D, 1024])
        pR = s.ps("pR", [P, 512])
        loaded = [s.sem(f"loaded{b}") for b in range(2)]
        stored = [s.sem(f"stored{b}") for b in range(2)]
        turned, scanned, back, finished, linked = (s.sem(n) for n in ("turned", "scanned", "back", "finished", "linked"))
        block = s.block()

        @block.sync
        def _(sp):
            def body(n, m, b):
                g.sp(sp, n, m, b)
                wait(sp, finished, n - 1)
                sp.dma_start(fl[b][:, :], flag_chunk(same, n)).then_inc(loaded[b], 16)
            staged(sp, NCH, [(0, body)])

        @block.gpsimd
        def _(pool):
            pool_gather_scatter(pool, g, sca, finished)

        @block.tensor
        def _(pe):
            def body(n, m, b):
                g.wait(pe, m, b)
                wait(pe, scanned, n)
                for k in range(CT):
                    mm = turn_64(nc, pT[:, k * P:(k + 1) * P], g.buf[b][:, k, 0:D], c.ident, k == 0)
                mm.then_inc(turned, 1)
                pe.wait_ge(scanned, n + 1)
                for k in range(CT):
                    mm = nc.tensor.matmul(pR[:, k * D:(k + 1) * D], sc[:, k * P:(k + 1) * P], c.ident[0:D, 0:D], start=True, stop=True)
                mm.then_inc(back, 1)
            staged(pe, NCH, [(0, body)])

        @block.scalar
        def _(act):
            def body(n, m, b):
                sca.targets(act, n, m, b)
                norm.root(act, n, twice=True)
                act.wait_ge(finished, n + 1)
                act.dma_start(chunk_of(x3_table, 0, n, D), flat(o[b][:, :, :])).then_inc(stored[b], 16)
            staged(act, NCH, [(0, body)])
            for b in range(2):
                act.wait_ge(stored[b], 16 * PAIRS)

        @block.vector
        def _(dve):
            link = Link(dve, linked)
            v = nc.vector
            link(v.memset(sc[:, CW - 1:CW], 0.0))

            def body(n, m, b):
                link(v.tensor_scalar(ri[:, :], c.inv_in[:, bass.ds(n * CT, CT)], 1.0, None, ALU.mult))
                dve.wait_ge(turned, n + 1)
                dve.wait_ge(loaded[b], m * 16 + 16)
                v.tensor_tensor_scan(out=sc[:, :], data0=fl[b][0:D, :], data1=pT[:, 0:CW], initial=sc[:, CW - 1:CW],
                                     op0=ALU.mult, op1=ALU.add).then_inc(scanned, 1)
                dve.wait_ge(scanned, n + 1)
                wait(dve, stored[b], m * 16)
                wait(dve, sca.done[b], m * sca.per)
                g.wait(dve, m, b)
                dve.wait_ge(back, n + 1)
                rows = pR[:, 0:CT * D].rearrange("p (t k) -> p t k", k=D)
                link(v.tensor_tensor(y[:, :, :], rows, bc(ri[:, :], D), ALU.mult))
                link(v.tensor_tensor(y[:, :, :], y[:, :, :], g.buf[b][:, :, D:2 * D], ALU.add))
                norm.dve(dve, link, n, y[:, :, :], o[b][:, :, :], sca.buf[b][:, :, :])
                v.tensor_copy(y[:, 0, 0:1], sca.buf[b][:, 0, 0:1]).then_inc(finished, 1)
                dve.wait_ge(finished, n + 1)
            staged(dve, NCH, [(0, body)], [link])


def edge_layer(nc, c, far, x3_table, out):
    with Scope(nc, "edg_") as s:
        g = Gather(nc, s, [(x3_table, c.idx["a6"], 0, D), (x3_table, c.idx["a5"], D, D)], 2 * D)
        sca = Scatter(nc, s, out, c.out_a)
        fl = [s.sb(f"far{b}", [P, CW]) for b in range(2)]
        hin = s.sb("hin", [P, CT, 2 * D])
        hT = s.sb("hT", [P, CW])
        h1 = s.sb("h1", [P, CW])
        sc = s.sb("scan", [D, CW])
        y = s.sb("y", [P, CT, D])
        norm = Norm(nc, s, c, CT)
        pT = s.ps("pT", [P, 1024])
        pH = s.ps("pH", [P, 1024])
        pO = s.ps("pO", [D, 1024])
        pR = s.ps("pR", [P, 512])
        loaded = [s.sem(f"loaded{b}") for b in range(2)]
        fed, turned, evac, hid, act1, outp, scanned, back, finished, linked = (
            s.sem(n) for n in ("fed", "turned", "evac", "hidden", "relu", "product", "scanned", "back", "finished", "linked"))
        block = s.block()

        @block.sync
        def _(sp):
            def body(n, m, b):
                g.sp(sp, n, m, b)
                wait(sp, finished, n - 1)
                sp.dma_start(fl[b][:, :], flag_chunk(far, n)).then_inc(loaded[b], 16)
            staged(sp, NCH, [(0, body)])

        @block.gpsimd
        def _(pool):
            pool_gather_scatter(pool, g, sca, finished)

        @block.tensor
        def _(pe):
            def body(n, m, b):
                pe.wait_ge(fed, n + 1)
                for k in range(CT):
                    mm = nc.tensor.transpose(pT[:, k * P:(k + 1) * P], hin[:, k, :], c.ident[:, :])
                mm.then_inc(turned, 1)
                pe.wait_ge(evac, n + 1)
                for a, z in pieces():
                    mm = nc.tensor.matmul(pH[:, a:z], c.w31[:, :], hT[:, a:z], start=True, stop=True)
                mm.then_inc(hid, 1)
                pe.wait_ge(act1, n + 1)
                for a, z in pieces():
                    mm = nc.tensor.matmul(pO[:, a:z], c.w32[:, :], h1[:, a:z], start=True, stop=True)
                mm.then_inc(outp, 1)
                pe.wait_ge(scanned, n + 1)
                for k in range(CT):
                    mm = nc.tensor.matmul(pR[:, k * D:(k + 1) * D], sc[:, k * P:(k + 1) * P], c.ident[0:D, 0:D], start=True, stop=True)
                mm.then_inc(back, 1)
            staged(pe, NCH, [(0, body)])

        @block.scalar
        def _(act):
            def body(n, m, b):
                sca.targets(act, n, m, b)
                act.wait_ge(turned, n + 1)
                nc.scalar.activation(hT[:, :], pT[:, 0:CW], ACT.Copy).then_inc(evac, 1)
                act.wait_ge(hid, n + 1)
                nc.scalar.activation(h1[:, :], pH[:, 0:CW], ACT.Relu, bias=c.b31[:, :]).then_inc(act1, 1)
                norm.root(act, n)
            staged(act, NCH, [(0, body)])

        @block.vector
        def _(dve):
            link = Link(dve, linked)
            v = nc.vector
            link(v.memset(sc[:, CW - 1:CW], 0.0))

            def body(n, m, b):
                g.wait(dve, m, b)
                link(v.tensor_copy(hin[:, :, 0:D], g.buf[b][:, :, 0:D]))
                v.tensor_tensor(hin[:, :, D:2 * D], g.buf[b][:, :, D:2 * D], g.buf[b][:, :, 0:D], ALU.subtract).then_inc(fed, 1)
                dve.wait_ge(outp, n + 1)
                dve.wait_ge(loaded[b], m * 16 + 16)
                v.tensor_tensor_scan(out=sc[:, :], data0=fl[b][0:D, :], data1=pO[:, 0:CW], initial=sc[:, CW - 1:CW],
                                     op0=ALU.add, op1=ALU.max).then_inc(scanned, 1)
                dve.wait_ge(scanned, n + 1)
                wait(dve, sca.done[b], m * sca.per)
                dve.wait_ge(back, n + 1)
                rows = pR[:, 0:CT * D].rearrange("p (t k) -> p t k", k=D)
                link(v.tensor_tensor(y[:, :, :], rows, c.b32[:, :].unsqueeze(1).to_broadcast([P, CT, D]), ALU.add))
                link(v.tensor_tensor(y[:, :, :], y[:, :, :], g.buf[b][:, :, 0:D], ALU.add))
                norm.dve(dve, link, n, y[:, :, :], sca.buf[b][:, :, :])
                v.tensor_copy(y[:, 0, 0:1], sca.buf[b][:, 0, 0:1]).then_inc(finished, 1)
                dve.wait_ge(finished, n + 1)
            staged(dve, NCH, [(0, body)], [link])


class Isolated:

    R = 125
    CG = 16
    CHUNKS = N // (R * CG)

    def __init__(self, nc, s, c, x, out, first, count):
        R, CG = self.R, self.CG
        self.nc, self.c, self.first, self.count = nc, c, first, count
        self.xb = [s.sb(f"iso_x{b}", [R, CG, D]) for b in range(2)]
        self.o = [s.sb(f"iso_out{b}", [R, CG, D]) for b in range(2)]
        self.xn, self.x1 = s.sb("iso_scaled", [R, CG, D]), s.sb("iso_first", [R, CG, D])
        self.y = [s.sb(f"iso_centred{j}", [R, CG, D]) for j in range(2)]
        self.sq = [s.sb(f"iso_squares{j}", [R, CG, D]) for j in range(2)]
        self.low, self.inv = s.sb("iso_low", [R, CG]), s.sb("iso_inv", [R, CG])
        self.total = [s.sb(f"iso_total{j}", [R, CG]) for j in range(2)]
        self.std = [s.sb(f"iso_std{j}", [R, CG]) for j in range(2)]
        self.rstd = [s.sb(f"iso_rstd{j}", [R, CG]) for j in range(2)]
        self.xT = [s.sb(f"iso_xT{j}", [P, 2, 4 * R]) for j in range(2)]
        self.eps3 = s.sb("iso_eps3", [R, 1])
        self.pT = [s.ps(f"iso_pT{j}", [P, 2, 512]) for j in range(2)]
        self.pR = [s.ps(f"iso_pR{j}", [R, 1024]) for j in range(2)]
        self.loaded = [s.sem(f"iso_loaded{b}") for b in range(2)]
        self.stored = [s.sem(f"iso_stored{b}") for b in range(2)]
        self.ready, self.linked, self.finished = s.sem("iso_ready"), s.sem("iso_linked"), s.sem("iso_finished")
        (self.fed, self.turned, self.evac, self.product, self.centred, self.squared, self.summed, self.rooted) = (
            [s.sem(f"iso_{n}{j}") for j in range(2)] for n in
            ("fed", "turned", "evac", "product", "centred", "squared", "summed", "rooted"))
        self.xv = x.rearrange("(p t) k -> p (t k)", p=R)
        self.ov = out.rearrange("(p t) k -> p (t k)", p=R)

    def at(self, n):
        w = self.CG * D
        return bass.ds(n * w + self.first * w, w)

    def tensor(self, pe):
        nc, R, CG = self.nc, self.R, self.CG
        def turn_and_multiply(j, src, w, bias, n):
            pe.wait_ge(self.fed[j], n + 1)
            wait(pe, self.evac[j], n)
            for k in range(CG // 2):
                mm = nc.tensor.transpose(self.pT[j][:, k // 4, k % 4 * R:(k % 4 + 1) * R],
                                         src[:, 2 * k:2 * k + 2, :].rearrange("p a b -> p (a b)"), self.c.ident[0:R, 0:R])
            mm.then_inc(self.turned[j], 1)
            pe.wait_ge(self.evac[j], n + 1)
            wait(pe, self.centred[j], n)
            for k in range(CG // 2):
                mine = self.pR[j][:, k * P:(k + 1) * P]
                nc.tensor.matmul(mine, self.xT[j][:, k // 4, k % 4 * R:(k % 4 + 1) * R], w[:, :], start=True, stop=False)
                mm = nc.tensor.matmul(mine, self.c.ones3[:, 0:R], bias[:, :], start=False, stop=True)
            mm.then_inc(self.product[j], 1)

        staged(pe, self.count, [
            (0, lambda n, m, b: turn_and_multiply(0, self.xn, self.c.wiso, self.c.biso, n)),
            (1, lambda n, m, b: turn_and_multiply(1, self.x1, self.c.w1d, self.c.b1x, n))])

    def scalar(self, act):
        nc, R = self.nc, self.R

        def load(n, b):
            act.dma_start(flat(self.xb[b][:, :, :]), self.xv[:, self.at(n)]).then_inc(self.loaded[b], 16)

        def evacuate(j, n):
            act.wait_ge(self.turned[j], n + 1)
            wait(act, self.product[j], n)
            nc.scalar.activation(self.xT[j][:, :, :], self.pT[j][:, :, 0:4 * R], ACT.Copy).then_inc(self.evac[j], 1)

        def square(j, n):
            act.wait_ge(self.centred[j], n + 1)
            nc.scalar.activation(self.sq[j][:, :, :], self.y[j][:, :, :], ACT.Square).then_inc(self.squared[j], 1)

        def root(j, n):
            act.wait_ge(self.summed[j], n + 1)
            if j == 0:
                nc.scalar.activation(self.std[0][:, :], self.std[0][:, :], ACT.Sqrt, bias=self.c.eps[0:R, :],
                                     scale=1.0 / D).then_inc(self.rooted[0], 1)
            else:
                nc.scalar.activation(self.std[1][:, :], self.std[1][:, :], ACT.Sqrt, bias=self.eps3[:, :],
                                     scale=(1.0 + EPS + EPS * EPS) / D).then_inc(self.rooted[1], 1)

        def store(n, b):
            act.wait_ge(self.finished, n + 1)
            act.dma_start(self.ov[:, self.at(n)], flat(self.o[b][:, :, :])).then_inc(self.stored[b], 16)

        act.wait_ge(self.ready, 1)
        staged(act, self.count, [
            (1, lambda n, m, b: evacuate(0, n)),
            (2, lambda n, m, b: square(0, n)),
            (0, lambda n, m, b: load(n, b)),
            (3, lambda n, m, b: square(1, n)),
            (2, lambda n, m, b: root(0, n)),
            (3, lambda n, m, b: root(1, n)),
            (2, lambda n, m, b: evacuate(1, n)),
            (3, lambda n, m, b: store(n, b))])
        for b in range(2):
            act.wait_ge(self.stored[b], (self.count + 1 - b) // 2 * 16)

    def vector(self, dve):
        v = self.nc.vector
        link = Link(dve, self.linked)
        v.memset(self.eps3[:, :], EPS ** 3).then_inc(self.ready, 1)

        def scale(n, m, b):
            x = self.xb[b][:, :, :]
            dve.wait_ge(self.loaded[b], m * 16 + 16)
            link.go(v.tensor_reduce(self.low[:, :], x, AX.X, ALU.min))
            link(v.tensor_reduce(self.inv[:, :], x, AX.X, ALU.max))
            link.go(v.scalar_tensor_tensor(out=self.inv[:, :], in0=self.inv[:, :], scalar=EPS, in1=self.low[:, :],
                                           op0=ALU.add, op1=ALU.subtract))
            wait(dve, self.turned[0], n)
            link(v.tensor_tensor(self.xn[:, :, :], x, bc(self.low[:, :], D), ALU.subtract))
            link(v.reciprocal(self.inv[:, :], self.inv[:, :]))
            v.tensor_tensor(self.xn[:, :, :], self.xn[:, :, :], bc(self.inv[:, :], D), ALU.mult).then_inc(self.fed[0], 1)

        def centre(j, n):
            y, total = self.y[j], self.total[j]
            link(v.tensor_reduce(total[:, :], y[:, :, :], AX.X, ALU.add))
            v.scalar_tensor_tensor(out=y[:, :, :], in0=bc(total[:, :], D), scalar=-1.0 / D, in1=y[:, :, :],
                                   op0=ALU.mult, op1=ALU.add).then_inc(self.centred[j], 1)

        def first_sum(n, m, b):
            dve.wait_ge(self.product[0], n + 1)
            rows = self.pR[0][:, :].rearrange("p (t k) -> p t k", k=D)
            link(v.tensor_tensor(self.y[0][:, :, :], rows, self.xb[b][:, :, :], ALU.add))
            centre(0, n)

        def second_sum(n, m, b):
            dve.wait_ge(self.product[1], n + 1)
            rows = self.pR[1][:, :].rearrange("p (t k) -> p t k", k=D)
            link(v.scalar_tensor_tensor(out=self.y[1][:, :, :], in0=rows, scalar=0.0, in1=self.x1[:, :, :],
                                        op0=ALU.max, op1=ALU.add))
            centre(1, n)

        def variance(j, n):
            dve.wait_ge(self.squared[j], n + 1)
            v.tensor_reduce(self.std[j][:, :], self.sq[j][:, :, :], AX.X, ALU.add).then_inc(self.summed[j], 1)

        def normalise(j, n, b):
            dve.wait_ge(self.rooted[j], n + 1)
            link(v.reciprocal(self.rstd[j][:, :], self.std[j][:, :]))
            scale_of = bc(self.rstd[j][:, :], D)
            if j == 0:
                v.tensor_tensor(self.x1[:, :, :], self.y[0][:, :, :], scale_of, ALU.mult).then_inc(self.fed[1], 1)
                dve.wait_ge(self.fed[1], n + 1)
            else:
                v.tensor_tensor(self.o[b][:, :, :], self.y[1][:, :, :], scale_of, ALU.mult).then_inc(self.finished, 1)
                dve.wait_ge(self.finished, n + 1)

        def last_scale(n, m, b):
            wait(dve, self.stored[b], m * 16)
            normalise(1, n, b)

        staged(dve, self.count, [
            (0, scale),
            (1, first_sum),
            (2, second_sum),
            (1, lambda n, m, b: variance(0, n)),
            (2, lambda n, m, b: variance(1, n)),
            (1, lambda n, m, b: normalise(0, n, b)),
            (2, last_scale)], [link])

    def engines(self, block):
        @block.tensor
        def _(pe):
            self.tensor(pe)

        @block.scalar
        def _(act):
            self.scalar(act)

        @block.vector
        def _(dve):
            self.vector(dve)


def index_arrays(nc, c):
    with Scope(nc, "idx_") as s:
        ta, tb = s.sb("ta", [P, NT]), s.sb("tb", [P, NT])
        linked, vin, vout = s.sem("linked"), s.sem("vin"), s.sem("vout")
        block = s.block()
        FAR = float(4 * N)

        @block.scalar
        def _(act):
            for k, t in enumerate((c.inv_out, c.inv_in)):
                act.wait_ge(vin, k + 1)
                nc.scalar.activation(t[:, :], t[:, :], ACT.Sqrt).then_inc(vout, 1)

        @block.vector
        def _(dve):
            link = Link(dve, linked)
            v = nc.vector
            af, bf = c.rec_a[:, :, :].bitcast(FP32), c.rec_b[:, :, :].bitcast(FP32)
            for name, rec, col in (("bs", c.rec_b, 6), ("bd", c.rec_b, 7), ("b1", c.rec_b, 1), ("b2", c.rec_b, 2), ("b3", c.rec_b, 3), ("a2", c.rec_a, 2),
                                   ("a3", c.rec_a, 3), ("a4", c.rec_a, 4), ("a5", c.rec_a, 5), ("a6", c.rec_a, 6)):
                link(v.tensor_copy(c.idx[name][:, :], rec[:, :, col]))
            link(v.tensor_scalar(ta[:, :], c.last_a[:, :], -1.0, -FAR, ALU.add, ALU.mult))
            link(v.tensor_tensor(tb[:, :], af[:, :, 0], ta[:, :], ALU.add))
            link(v.tensor_copy(c.out_a[:, :], tb[:, :]))
            link(v.tensor_scalar(ta[:, :], c.last_b[:, :], -1.0, -FAR, ALU.add, ALU.mult))
            link(v.tensor_tensor(tb[:, :], bf[:, :, 0], ta[:, :], ALU.add))
            link(v.scalar_tensor_tensor(out=tb[:, :], in0=bf[:, :, 4], scalar=FAR, in1=tb[:, :], op0=ALU.mult, op1=ALU.add))
            link(v.tensor_copy(c.out_b[:, :], tb[:, :]))
            for k, (t, src) in enumerate(((c.inv_out, af[:, :, 7]), (c.inv_in, bf[:, :, 5]))):
                v.tensor_scalar(t[:, :], src, 1.0, None, ALU.max).then_inc(vin, 1)
                dve.wait_ge(vout, k + 1)
                link(v.reciprocal(t[:, :], t[:, :]))


def hop_norms(nc, c, dis):
    with Scope(nc, "nrm_") as s:
        linked = s.sem("linked")
        block = s.block()

        @block.vector
        def _(dve):
            Link(dve, linked)(nc.vector.tensor_tensor(c.norm[:, :], c.rec_a[:, :, :].bitcast(FP32)[:, :, 1], dis[:, :, 0], ALU.mult))


def zero_rows(nc, tables):
    with Scope(nc, "zr_") as s:
        z = s.sb("z", [1, D])
        a, b = s.sem("made"), s.sem("stored")
        block = s.block()

        @block.vector
        def _(dve):
            nc.vector.memset(z[:, :], 0.0).then_inc(a, 1)

        @block.sync
        def _(sp):
            sp.wait_ge(a, 1)
            for t in tables:
                sp.dma_start(t[ZERO:ZERO + 1, :], z[:, :]).then_inc(b, 16)
            sp.wait_ge(b, 16 * len(tables))


FIRST_ISO = 25


class Bag:
    pass


def build(nc, a, out):
    def dram(name, shape):
        return nc.dram_tensor(name, shape, FP32).ap()

    x = a["x"]
    entries = dram("node_entries", [P * LO, 4])
    by_dst = dram("by_dst", [SLOTS, META])
    by_src = dram("by_src", [SLOTS, META])
    v_a, v_b, w_a, w_b, same_a, same_b, far_a, far_b, deg_row = (
        dram(n, [SLOTS + 2 if n[0] == "v" else SLOTS]) for n in
        ("v_a", "v_b", "w_a", "w_b", "same_a", "same_b", "far_a", "far_b", "deg_row"))
    dis_t = dram("dis_t", [SLOTS + 1, 4])
    d_t = dram("d_t", [SLOTS + 1, D])
    stash = dram("stash", [SLOTS, 4 * D])
    x1_t = dram("x1_t", [2 * SLOTS, D])
    t0_s = dram("t0_s", [SLOTS, D])
    p_t = [dram(f"p_t{k}", [SLOTS + 1, D]) for k in range(2)]
    x2_t = dram("x2_t", [3 * SLOTS, D])
    x3_t = dram("x3_t", [2 * SLOTS, D])
    with Scope(nc) as s:
        c = Bag()
        c.ident = s.sb("ident", [P, P])
        c.eps, c.eps_eps = s.sb("eps", [P, 1]), s.sb("eps_eps", [P, 1])
        c.w0, c.b0, c.m0 = s.sb("w0", [P, 8, D]), s.sb("b0", [3, 8 * D], BF16), s.sb("m0", [P, D])
        c.ones3 = s.sb("ones3", [3, P], BF16)
        c.wiso, c.biso = s.sb("wiso", [P, P]), s.sb("biso", [3, 2 * D], BF16)
        c.w1d, c.b1x, c.wp = s.sb("w1d", [P, P]), s.sb("b1x", [3, 2 * D], BF16), s.sb("wp", [D, 5, 2 * D])
        c.w31, c.w32, c.b31, c.b32 = s.sb("w31", [P, P]), s.sb("w32", [P, D]), s.sb("b31", [P, 1]), s.sb("b32", [P, D])
        c.last_a, c.last_b = s.sb("last_a", [P, NT]), s.sb("last_b", [P, NT])
        c.neg_dis, c.norm = s.sb("neg_dis", [P, NT]), s.sb("norm", [P, NT])
        c.inv_out, c.inv_in = s.sb("inv_out", [P, NT]), s.sb("inv_in", [P, NT])
        c.out_a, c.out_b = s.sb("out_a", [P, NT], I32), s.sb("out_b", [P, NT], I32)
        c.idx = {n: s.sb("idx_" + n, [P, NT], I32) for n in ("bs", "bd", "b1", "b2", "b3", "a2", "a3", "a4", "a5", "a6")}
        with Scope(nc) as e:
            c.rec_a, c.rec_b = e.sb("rec_a", [P, NT, META], I32), e.sb("rec_b", [P, NT, META], I32)
            with Scope(nc) as r:
                c.ones, c.tri = r.sb("ones", [P, P]), r.sb("tri", [P, P])
                c.rank_mask = r.sb("rank_mask", [P, BLK * P])
                c.iota16, c.iota_part = r.sb("iota16", [P, LO], F16), r.sb("iota_part", [P, 1])
                c.ident16, c.ones16, c.w128_16 = r.sb("ident16", [P, P], F16), r.sb("ones16", [P, P], F16), r.sb("w128_16", [P, P], F16)
                c.src, c.dst, c.ew = r.sb("src", [P, NT], I32), r.sb("dst", [P, NT], I32), r.sb("ew", [P, NT])
                c.key_s, c.key_d = r.sb("key_s", [P, NT, 3]), r.sb("key_d", [P, NT, 3])
                c.node_s, c.node_d = r.sb("node_s", [P, NT], I32), r.sb("node_d", [P, NT], I32)
                c.safe_s, c.safe_d = r.sb("safe_s", [P, NT], I32), r.sb("safe_d", [P, NT], I32)
                c.rank_s, c.rank_d = r.sb("rank_s", [P, NT]), r.sb("rank_d", [P, NT])
                c.count_s, c.count_d = r.sb("count_s", [P, LO]), r.sb("count_d", [P, LO])
                c.seg_s, c.seg_d = r.sb("seg_s", [P, NT, 4]), r.sb("seg_d", [P, NT, 4])
                c.row_a, c.row_b = r.sb("row_a", [P, NT], I32), r.sb("row_b", [P, NT], I32)
                constants(nc, c)
                load_edges(nc, c, a["src"], a["dst"], a["edge_weight"])
                load_weights(nc, c, a)
                rank_edges(nc, c, c.key_s, c.rank_s, c.count_s, "rank_s_")
                rank_edges(nc, c, c.key_d, c.rank_d, c.count_d, "rank_d_")
                node_table(nc, c, entries)
                gather_segments(nc, c, (entries, c.node_s, c.seg_s, 4), (entries, c.node_d, c.seg_d, 4), x, out, (0, FIRST_ISO))
                edge_records(nc, c)
                sort_edges(nc, c, x, by_dst, by_src, out, (FIRST_ISO, Isolated.CHUNKS - FIRST_ISO))
            order_marks(nc, c, by_dst, c.rec_b, v_b, same_b, far_b, c.last_b, "mark_b_", w_b)
            order_marks(nc, c, by_src, c.rec_a, v_a, same_a, far_a, c.last_a, "mark_a_", w_a)
            source_scale(nc, c, same_a, w_a, deg_row, dis_t)
            index_arrays(nc, c)
            zero_rows(nc, p_t)
            with Scope(nc) as r:
                dis = r.sb("dis", [P, NT, 4])
                attention_sums(nc, c, x, same_b, stash, d_t, x1_t, (dis_t, c.idx["a4"], dis, 4))
                hop_norms(nc, c, dis)
        attention_out(nc, c, same_b, stash, d_t, x1_t)
        with Scope(nc) as r:
            c.acc, c.t_even = (r.sb(n, [P, NT, D]) for n in ("acc", "t_even"))
            chebyshev_start(nc, c, x1_t, t0_s, x2_t, same_a, p_t[0])
            c.t_odd = r.sb("t_odd", [P, NT, D])
            for k in range(1, 5):
                chebyshev_hop(nc, c, k, same_a, p_t[(k + 1) % 2], p_t[k % 2], t0_s, x2_t, x3_t)
        light_layer(nc, c, same_b, x2_t, x3_t, out)
        edge_layer(nc, c, far_a, x3_t, out)


_INS = ['x', 'src', 'dst', 'edge_weight', 'L0_gnn_W1', 'L0_gnn_b1', 'L0_gnn_W2', 'L0_gnn_b2', 'L0_gnn_Wres', 'L0_gnn_bres',
        'L0_gnn_m', 'L1_gnn_W', 'L1_gnn_b', 'L3_gnn_W1', 'L3_gnn_b1', 'L3_gnn_W2', 'L3_gnn_b2']


def kernel(**inputs):
    import numpy as _np
    import concourse.bacc as _bacc
    from concourse import mybir as _mybir
    from concourse.bass_utils import run_bass_kernel_spmd as _run

    nc = _bacc.Bacc("TRN2", target_bir_lowering=False, num_devices=1)
    arrays, args = {}, {}
    for name in _INS:
        a = _np.ascontiguousarray(inputs[name])
        arrays[f"in_{name}_dram"] = a
        args[name] = nc.dram_tensor(f"in_{name}_dram", a.shape, _mybir.dt.from_np(a.dtype), kind="ExternalInput").ap()
    out = nc.dram_tensor("out_0_dram", (N, D), _mybir.dt.float32, kind="ExternalOutput").ap()
    build(nc, args, out)
    r = _run(nc, [arrays], core_ids=[0])
    return r.results[0]["out_0_dram"]
```
